# Optimizing a Trainium2 kernel written in Bass

```python
import numpy as np
import jax
import jax.numpy as jnp

def _softmax(x, axis=-1):
    return jax.nn.softmax(x, axis=axis)

def _gelu(x):
    return jax.nn.gelu(x, approximate=True)

def _silu(x):
    return jax.nn.silu(x)

def _sigmoid(x):
    return jax.nn.sigmoid(x)

def _layernorm(x, axis=-1, eps=1e-05):
    m = jnp.mean(x, axis=axis, keepdims=True)
    v = jnp.var(x, axis=axis, keepdims=True)
    return (x - m) / jnp.sqrt(v + eps)

def _scatter_add(tgt, idx, src, axis=0):
    return tgt.at[idx].add(src)

def _segment_sum(src, seg, n):
    return jax.ops.segment_sum(src, seg, n)
kernel_name = 'mk_hybrid_d1_jaxref_r4_875da4'

def setup_inputs(seed: int=0):
    np.random.seed(seed)
    _w = jnp.asarray

    def _L0_attn_a_setup():
        import jax, jax.numpy as jnp
        import numpy as np
        B, S, D = (8, 2048, 256)
        MIN_RAD, MAX_RAD = (0.9, 0.999)

        def _a_param_init(key, d):
            unif = jax.random.uniform(key, (d,))
            a = 0.5 * jnp.log(unif * (MAX_RAD ** 2 - MIN_RAD ** 2) + MIN_RAD ** 2)
            return jnp.log(jnp.exp(-a) - 1.0)
        key = jax.random.key(seed)
        ks = jax.random.split(key, 6)
        s = 1.0 / np.sqrt(D)
        return {'x': jax.random.normal(ks[0], (B, S, D), jnp.float32), 'W_in': jax.random.normal(ks[1], (D, D), jnp.float32) * s, 'b_in': jnp.zeros((D,), jnp.float32), 'W_gx': jax.random.normal(ks[2], (D, D), jnp.float32) * s, 'b_gx': jnp.zeros((D,), jnp.float32), 'W_ga': jax.random.normal(ks[3], (D, D), jnp.float32) * s, 'b_ga': jnp.zeros((D,), jnp.float32), 'a_param': _a_param_init(ks[4], D), 'W_out': jax.random.normal(ks[5], (D, D), jnp.float32) * s, 'b_out': jnp.zeros((D,), jnp.float32)}
    _L0_attn_a_in = _L0_attn_a_setup()

    def _L0_attn_b_setup():
        import math
        import jax, jax.numpy as jnp
        import numpy as np
        HEADS = 16
        REL_WINDOW = 128
        key = jax.random.key(seed)
        k1, k2, k3, k4, k5 = jax.random.split(key, 5)
        b, s, d = (2, 512, 256)
        hd = d // HEADS
        R = 2 * REL_WINDOW + 1
        return {'x': jax.random.normal(k1, (b, s, d), dtype=jnp.float32), 'Wqkv': jax.random.normal(k2, (3 * d, d), dtype=jnp.float32) * (1.0 / math.sqrt(d)), 'bqkv': jax.random.normal(k3, (3 * d,), dtype=jnp.float32) * 0.02, 'Wr': jax.random.normal(k4, (R, hd), dtype=jnp.float32) * (1.0 / math.sqrt(hd)), 'br': jax.random.normal(k5, (R,), dtype=jnp.float32) * 0.02}
    _L0_attn_b_in = _L0_attn_b_setup()

    def _L0_ffn_setup():
        import jax, jax.numpy as jnp
        import numpy as np
        DIM = 256

        def _reference_tuple_inner(x, W_r, W_k, W_v, mu_r, mu_k):
            B, T, C = x.shape
            x_prev = jnp.concatenate([jnp.zeros((B, 1, C), x.dtype), x[:, :-1, :]], axis=1)
            xr = mu_r * x + (1.0 - mu_r) * x_prev
            xk = mu_k * x + (1.0 - mu_k) * x_prev
            r = jax.nn.sigmoid(jnp.einsum('btc,dc->btd', xr, W_r))
            k = jnp.einsum('btc,dc->btd', xk, W_k)
            k_act = jnp.square(jax.nn.relu(k))
            out = r * jnp.einsum('btc,dc->btd', k_act, W_v)
            new_state = x[:, -1, :]
            return (out, new_state)
        key = jax.random.key(seed)
        ks = jax.random.split(key, 6)
        B, T, C = (8, 512, DIM)
        x = jax.random.normal(ks[0], (B, T, C), dtype=jnp.float32)
        s = 1.0 / np.sqrt(C)
        W_r = jax.random.uniform(ks[1], (C, C), jnp.float32, -s, s)
        W_k = jax.random.uniform(ks[2], (C, C), jnp.float32, -s, s)
        W_v = jax.random.uniform(ks[3], (C, C), jnp.float32, -s, s)
        mu_r = jax.random.uniform(ks[4], (C,), jnp.float32)
        mu_k = jax.random.uniform(ks[5], (C,), jnp.float32)
        return {'x': x, 'W_r': W_r, 'W_k': W_k, 'W_v': W_v, 'mu_r': mu_r, 'mu_k': mu_k}
    _L0_ffn_in = _L0_ffn_setup()
    _d = {'L0_attn_a_x': _L0_attn_a_in['x'], 'L0_attn_a_W_in': _L0_attn_a_in['W_in'], 'L0_attn_a_b_in': _L0_attn_a_in['b_in'], 'L0_attn_a_W_gx': _L0_attn_a_in['W_gx'], 'L0_attn_a_b_gx': _L0_attn_a_in['b_gx'], 'L0_attn_a_W_ga': _L0_attn_a_in['W_ga'], 'L0_attn_a_b_ga': _L0_attn_a_in['b_ga'], 'L0_attn_a_a_param': _L0_attn_a_in['a_param'], 'L0_attn_a_W_out': _L0_attn_a_in['W_out'], 'L0_attn_a_b_out': _L0_attn_a_in['b_out'], 'L0_attn_b_Wqkv': _L0_attn_b_in['Wqkv'], 'L0_attn_b_bqkv': _L0_attn_b_in['bqkv'], 'L0_attn_b_Wr': _L0_attn_b_in['Wr'], 'L0_attn_b_br': _L0_attn_b_in['br'], 'L0_ffn_W_r': _L0_ffn_in['W_r'], 'L0_ffn_W_k': _L0_ffn_in['W_k'], 'L0_ffn_W_v': _L0_ffn_in['W_v'], 'L0_ffn_mu_r': _L0_ffn_in['mu_r'], 'L0_ffn_mu_k': _L0_ffn_in['mu_k']}
    _x0 = _d['L0_attn_a_x']
    _d['L0_attn_a_x'] = jax.random.normal(jax.random.fold_in(jax.random.key(seed), 1), (16, 1024, 256), dtype=_x0.dtype)
    del _x0
    return _d

def reference(L0_attn_a_x, L0_attn_a_W_in, L0_attn_a_b_in, L0_attn_a_W_gx, L0_attn_a_b_gx, L0_attn_a_W_ga, L0_attn_a_b_ga, L0_attn_a_a_param, L0_attn_a_W_out, L0_attn_a_b_out, L0_attn_b_Wqkv, L0_attn_b_bqkv, L0_attn_b_Wr, L0_attn_b_br, L0_ffn_W_r, L0_ffn_W_k, L0_ffn_W_v, L0_ffn_mu_r, L0_ffn_mu_k):

    def _L0_attn_a_ref(x, W_in, b_in, W_gx, b_gx, W_ga, b_ga, a_param, W_out, b_out):
        import jax, jax.numpy as jnp
        import numpy as np
        B, S, D = (8, 2048, 256)
        MIN_RAD, MAX_RAD = (0.9, 0.999)

        def _a_param_init(key, d):
            unif = jax.random.uniform(key, (d,))
            a = 0.5 * jnp.log(unif * (MAX_RAD ** 2 - MIN_RAD ** 2) + MIN_RAD ** 2)
            return jnp.log(jnp.exp(-a) - 1.0)
        x = x @ W_in + b_in
        gate_x = jax.nn.sigmoid(x @ W_gx + b_gx)
        gate_a = jax.nn.sigmoid(x @ W_ga + b_ga)
        log_a = -8.0 * gate_a * jax.nn.softplus(a_param)
        a = jnp.exp(log_a)
        scale = jnp.sqrt(1.0 - jnp.exp(2.0 * log_a))
        xg = gate_x * x

        def step(h, inp):
            xt, at, st = inp
            h = at * h + st * xt
            return (h, h)
        init = jnp.zeros((x.shape[0], x.shape[2]), x.dtype)
        xs = (jnp.swapaxes(xg, 0, 1), jnp.swapaxes(a, 0, 1), jnp.swapaxes(scale, 0, 1))
        _, h = jax.lax.scan(step, init, xs, reverse=False)
        h = jnp.swapaxes(h, 0, 1)
        return h @ W_out + b_out

    def _L0_attn_b_ref(x, Wqkv, bqkv, Wr, br):
        import math
        import jax, jax.numpy as jnp
        import numpy as np
        HEADS = 16
        REL_WINDOW = 128
        b, s, d = x.shape
        h = HEADS
        hd = d // h
        w = REL_WINDOW
        scale = math.sqrt(d / h)
        qkv = (x @ Wqkv.T + bqkv).reshape(b, s, h, 3 * hd)
        q, k, v = jnp.split(qkv, 3, axis=-1)
        q = q.transpose(0, 2, 1, 3)
        k = k.transpose(0, 2, 1, 3)
        v = v.transpose(0, 2, 1, 3)
        content = jnp.einsum('bhik,bhjk->bhij', q, k) / scale
        idx = jnp.arange(s)
        offsets = jnp.clip(idx[None, :] - idx[:, None], -w, w) + w
        rp = jnp.einsum('bhik,rk->bhir', q, Wr) + br
        pos = jnp.take_along_axis(rp, jnp.broadcast_to(offsets, (b, h, s, s)), axis=-1)
        attn = jax.nn.softmax(content + pos, axis=-1)
        out = jnp.einsum('bhij,bhjk->bhik', attn, v)
        return out.transpose(0, 2, 1, 3).reshape(b, s, d)

    def _L0_ffn_ref(x, W_r, W_k, W_v, mu_r, mu_k):
        import jax, jax.numpy as jnp
        import numpy as np
        DIM = 256

        def _reference_tuple_inner(x, W_r, W_k, W_v, mu_r, mu_k):
            B, T, C = x.shape
            x_prev = jnp.concatenate([jnp.zeros((B, 1, C), x.dtype), x[:, :-1, :]], axis=1)
            xr = mu_r * x + (1.0 - mu_r) * x_prev
            xk = mu_k * x + (1.0 - mu_k) * x_prev
            r = jax.nn.sigmoid(jnp.einsum('btc,dc->btd', xr, W_r))
            k = jnp.einsum('btc,dc->btd', xk, W_k)
            k_act = jnp.square(jax.nn.relu(k))
            out = r * jnp.einsum('btc,dc->btd', k_act, W_v)
            new_state = x[:, -1, :]
            return (out, new_state)
        return _reference_tuple_inner(x, W_r, W_k, W_v, mu_r, mu_k)[0]
    x = L0_attn_a_x
    x = x + _L0_attn_a_ref(_layernorm(x, axis=-1), L0_attn_a_W_in, L0_attn_a_b_in, L0_attn_a_W_gx, L0_attn_a_b_gx, L0_attn_a_W_ga, L0_attn_a_b_ga, L0_attn_a_a_param, L0_attn_a_W_out, L0_attn_a_b_out)
    x = x + _L0_ffn_ref(_layernorm(x, axis=-1), L0_ffn_W_r, L0_ffn_W_k, L0_ffn_W_v, L0_ffn_mu_r, L0_ffn_mu_k)
    x = x + _L0_attn_b_ref(_layernorm(x, axis=-1), L0_attn_b_Wqkv, L0_attn_b_bqkv, L0_attn_b_Wr, L0_attn_b_br)
    x = x + _L0_ffn_ref(_layernorm(x, axis=-1), L0_ffn_W_r, L0_ffn_W_k, L0_ffn_W_v, L0_ffn_mu_r, L0_ffn_mu_k)
    return x

_drawn_inputs = setup_inputs


def setup_inputs(seed=0):
    import zlib

    import numpy as np

    out = dict(_drawn_inputs(seed))
    spreads = {'L0_attn_a_b_in': (0.0, 0.1),
     'L0_attn_a_b_gx': (0.0, 0.397),
     'L0_attn_a_b_ga': (0.0, 0.701),
     'L0_attn_a_b_out': (0.0, 0.1)}
    factors = {'L0_attn_b_bqkv': 3.144, 'L0_attn_b_br': 46.079, 'L0_ffn_mu_r': 4.077}
    for name, (base, spread) in spreads.items():
        noise = np.random.default_rng([zlib.crc32(name.encode()), seed]).standard_normal(out[name].shape)
        drawn = base * np.exp(spread * noise) if base else spread * noise
        out[name] = jnp.asarray(drawn.astype(out[name].dtype))
    for name, factor in factors.items():
        out[name] = (out[name] * factor).astype(out[name].dtype)
    return out
```

```python
from contextlib import ExitStack

import numpy as np

import concourse.bass as bass
from concourse import mybir

F32 = mybir.dt.float32
F16 = mybir.dt.float16
BF16 = mybir.dt.bfloat16
ALU = mybir.AluOpType
ACT = mybir.ActivationFunctionType
AX_X = mybir.AxisListType.X

P = 128
D = 256
NF = D // P
S = 1024
CH = 512
NC = S // CH
NT = CH // P
HEADS = 16
HD = D // HEADS
WIN = 128
R = 2 * WIN + 1
EPS = 1e-5

HP = 2
NPR = HEADS // HP
VW = 32
NTI = S // P
TW = 512
WW = 3 * P

R_ONE = 4 * HD
R_FAR = R_ONE + 2
R_MAX = R_FAR + 4
K_TAB, K_MAXP, K_SC = R_FAR, R_MAX, R_MAX + 1


def dram(t, offset, ap):
    return bass.AP(tensor=t.tensor, offset=offset, ap=ap)


class Pool:

    def __init__(self, nc, ctx):
        self.nc, self.ctx = nc, ctx

    def sb(self, name, shape, dt=F32):
        return self.ctx.enter_context(self.nc.sbuf_tensor(name, shape, dt))

    def ps(self, name, shape):
        return self.ctx.enter_context(self.nc.psum_tensor(name, shape, F32))

    def sems(self, names):
        return [self.ctx.enter_context(self.nc.semaphore(n)) for n in names.split()]


class Norm:

    def __init__(self, m, tag):
        self.stats = [m.sb(f"{tag}_stats{c}", [P, NT, 6]) for c in range(2)]
        self.mv = [m.sb(f"{tag}_mv{c}", [P, NT, 2]) for c in range(2)]
        self.ve = [m.sb(f"{tag}_ve{c}", [P, NT]) for c in range(2)]
        self.rstd = [m.sb(f"{tag}_rstd{c}", [P, NT]) for c in range(2)]
        self.gap = m.sb(f"{tag}_gap", [P, 1])
        self.xn = [m.sb(f"{tag}_xn{c}", [P, NT, D]) for c in range(2)]
        (self.stats_done, self.mv_done, self.ve_done, self.rstd_done, self.norm_done,
         self.tr_ready, self.tr_copied) = m.sems(" ".join(
             f"{tag}_{n}" for n in "stats_done mv_done ve_done rstd_done norm_done tr_ready tr_copied".split()))

    def dve_stats(self, dve, u, c, src):
        for t in range(NT):
            dve.bn_stats(self.stats[c][:, t, :], src[:, t, :]).then_inc(self.stats_done, 1)
        dve.wait_ge(self.stats_done, u * NT + NT)
        dve.memset(self.gap[:], 0.0)
        for t in range(NT):
            dve.bn_aggr(self.mv[c][:, t, :], self.stats[c][:, t, :]).then_inc(self.mv_done, 1)

    def pool_rstd(self, pool, u, c, eps, minus_half):
        pool.wait_ge(self.mv_done, u * NT + NT)
        pool.tensor_tensor(self.ve[c][:], self.mv[c][:, :, 1], eps[:], ALU.add).then_inc(self.ve_done, 1)
        pool.wait_ge(self.ve_done, u + 1)
        pool.tensor_tensor(self.rstd[c][:], self.ve[c][:], minus_half[:], ALU.pow).then_inc(self.rstd_done, 1)

    def dve_apply(self, dve, u, c, src):
        dve.wait_ge(self.rstd_done, u + 1)
        for t in range(NT):
            dve.tensor_scalar(self.xn[c][:, t, :], src[:, t, :], self.mv[c][:, t, 0:1],
                              self.rstd[c][:, t:t + 1], ALU.subtract, ALU.mult).then_inc(self.norm_done, 1)

    def pe_transpose(self, pe, u, c, banks, ident, free):
        pe.wait_ge(self.norm_done, u * NT + NT)
        for f in range(NF):
            free(f)
            for t in range(NT):
                tr = pe.transpose(banks[f][:, t * P:(t + 1) * P], self.xn[c][:, t, f * P:(f + 1) * P], ident[:])
            tr.then_inc(self.tr_ready, 1)

    def act_copy(self, act, u, c, banks, dst):
        for f in range(NF):
            act.wait_ge(self.tr_ready, u * NF + f + 1)
            act.activation(dst[:, f, :], banks[f][:], ACT.Identity).then_inc(self.tr_copied, 1)


class Ffn:

    def __init__(self, m, tag, banks, v_banks, w):
        self.w, self.banks, self.v_banks = w, banks, v_banks
        self.ln = Norm(m, tag)
        self.xt = [m.sb(f"{tag}_xt{c}", [P, NF, CH + 1]) for c in range(2)]
        self.diff = m.sb(f"{tag}_diff", [P, NF, CH])
        self.xr = m.sb(f"{tag}_xr", [P, NF, CH])
        self.xk = m.sb(f"{tag}_xk", [P, NF, CH])
        self.tr = m.sb(f"{tag}_tr", [P, NT, D])
        self.kr = m.sb(f"{tag}_kr", [P, NF, CH])
        self.ka = m.sb(f"{tag}_ka", [P, NF, CH])
        self.rv = m.sb(f"{tag}_rv", [P, NT, D])
        (self.zeroed, self.before_set, self.diff_done, self.mixed, self.r_ready, self.r_done, self.k_ready,
         self.k_done, self.ka_done, self.v_ready, self.rv_done, self.x_done) = m.sems(" ".join(
             f"{tag}_{n}" for n in ("zeroed before_set diff_done mixed r_ready r_done k_ready k_done ka_done "
                                    "v_ready rv_done x_done").split()))

    def dve_init(self, dve):
        dve.memset(self.xt[0][:, :, 0:1], 0.0).then_inc(self.zeroed, 1)
        dve.wait_ge(self.zeroed, 1)

    def act_input(self, act, u, c):
        self.ln.act_copy(act, u, c, self.banks[0:2], self.xt[c][:, :, 1:])
        if c == 1:
            act.wait_ge(self.ln.tr_copied, u * NF)
            act.activation(self.xt[1][:, :, 0:1], self.xt[0][:, :, CH:CH + 1], ACT.Identity)\
               .then_inc(self.before_set, 1)

    def dve_mix(self, dve, u, b, c):
        dve.wait_ge(self.ln.tr_copied, u * NF + NF)
        if c == 1:
            dve.wait_ge(self.before_set, b + 1)
        dve.tensor_tensor(self.diff[:], self.xt[c][:, :, 1:], self.xt[c][:, :, 0:CH], ALU.subtract)\
           .then_inc(self.diff_done, 1)
        dve.wait_ge(self.diff_done, u + 1)
        for dst, mu in ((self.xr, self.w["mu_r"]), (self.xk, self.w["mu_k"])):
            for f in range(NF):
                dve.scalar_tensor_tensor(dst[:, f, :], self.diff[:, f, :], mu[:, f:f + 1],
                                         self.xt[c][:, f, 0:CH], ALU.mult, ALU.add).then_inc(self.mixed, 1)

    def pe_rk(self, pe, u, free_r, free_k):
        pe.wait_ge(self.mixed, u * 2 * NF + NF)
        for h in range(2):
            free_r(h)
            for t in (2 * h, 2 * h + 1):
                for f in range(NF):
                    mm = pe.matmul(self.banks[2 + h][:, (t % 2) * D:(t % 2 + 1) * D],
                                   self.xr[:, f, t * P:(t + 1) * P], self.w["wr"][:, f, :],
                                   start=(f == 0), stop=(f == NF - 1))
            mm.then_inc(self.r_ready, 1)
        pe.wait_ge(self.mixed, u * 2 * NF + 2 * NF)
        for o in range(NF):
            free_k(o)
            for f in range(NF):
                mm = pe.matmul(self.banks[o][:], self.w["wk"][:, f, o * P:(o + 1) * P], self.xk[:, f, :],
                               start=(f == 0), stop=(f == NF - 1))
            mm.then_inc(self.k_ready, 1)

    def act_rk(self, act, u):
        for h in range(2):
            act.wait_ge(self.r_ready, u * 2 + h + 1)
            act.activation(self.tr[:, 2 * h:2 * h + 2, :], self.banks[2 + h][:].rearrange("p (t d) -> p t d", t=2),
                           ACT.Tanh, scale=0.5).then_inc(self.r_done, 1)
        for o in range(NF):
            act.wait_ge(self.k_ready, u * NF + o + 1)
            act.activation(self.kr[:, o, :], self.banks[o][:], ACT.Relu).then_inc(self.k_done, 1)

    def pool_square(self, pool, u):
        for o in range(NF):
            pool.wait_ge(self.k_done, u * NF + o + 1)
            pool.tensor_tensor(self.ka[:, o, :], self.kr[:, o, :], self.kr[:, o, :], ALU.mult)\
                .then_inc(self.ka_done, 1)

    def pe_v(self, pe, u, free):
        pe.wait_ge(self.ka_done, u * NF + NF)
        for h in range(2):
            free(h)
            for t in (2 * h, 2 * h + 1):
                for f in range(NF):
                    mm = pe.matmul(self.v_banks[h][:, (t % 2) * D:(t % 2 + 1) * D],
                                   self.ka[:, f, t * P:(t + 1) * P], self.w["wv"][:, f, :],
                                   start=(f == 0), stop=(f == NF - 1))
            mm.then_inc(self.v_ready, 1)

    def dve_out(self, dve, u, x):
        for h in range(2):
            dve.wait_ge(self.v_ready, u * 2 + h + 1)
            dve.scalar_tensor_tensor(self.rv[:, 2 * h:2 * h + 2, :], self.tr[:, 2 * h:2 * h + 2, :], 1.0,
                                     self.v_banks[h][:].rearrange("p (t d) -> p t d", t=2),
                                     ALU.add, ALU.mult).then_inc(self.rv_done, 1)
        dve.wait_ge(self.rv_done, u * 2 + 2)
        dve.scalar_tensor_tensor(x[:], self.rv[:], 0.5, x[:], ALU.mult, ALU.add).then_inc(self.x_done, 1)
        dve.wait_ge(self.x_done, u + 1)


def rows(w):
    return w.rearrange("(f p) n -> p f n", p=P)


def project(nc, a, scr, nb):
    with ExitStack() as ctx:
        m = Pool(nc, ctx)
        bank = [m.ps(f"pj_bank{i}", [P, CH]) for i in range(8)]

        w_names = ["W_in", "W_gx", "W_ga", "W_out", "ffn_wr", "ffn_wk", "ffn_wv", "Wq", "Wk", "Wv"]
        w = {n: m.sb(f"pj_{n}", [P, NF, D]) for n in w_names}
        v_names = ["b_in", "b_gx", "b_ga", "a_param", "mu_r", "mu_k", "bq", "bk"]
        v = {n: m.sb(f"pj_{n}", [P, NF]) for n in v_names}
        b_out = m.sb("pj_b_out", [P, D])
        bv = m.sb("pj_bv", [P, D])
        far32 = m.sb("pj_far32", [P, NF, 32])
        far_h = m.sb("pj_far_h", [P, NF, 32], F16)
        far_l = m.sb("pj_far_l", [P, NF, 32], F16)
        bfar = m.sb("pj_bfar", [32, 1])
        ident = m.sb("pj_ident", [P, P])
        eps = m.sb("pj_eps", [P, NT])
        minus_half = m.sb("pj_minus_half", [P, NT])
        sp_a, sp_b, sp_c, decay = [m.sb(f"pj_sp{i}", [P, NF]) for i in range(4)]

        xl = [m.sb(f"pj_xl{c}", [P, NT, D]) for c in range(2)]
        xb = [m.sb(f"pj_xb{c}", [P, NT, D]) for c in range(2)]
        lnt = m.sb("pj_lnt", [P, NF, CH])
        xin = m.sb("pj_xin", [P, NF, CH])
        tgx = m.sb("pj_tgx", [P, NF, CH])
        tga = m.sb("pj_tga", [P, NF, CH])
        aa = m.sb("pj_aa", [P, NF, CH])
        zz = m.sb("pj_zz", [P, NF, CH])
        hh = [m.sb(f"pj_h{c}", [P, NF, CH]) for c in range(2)]
        lt = m.sb("pj_lt", [P, NF, CH])
        qh, ql, kh, kl = [m.sb(f"pj_{n}", [P, NF, CH], F16) for n in ("qh", "ql", "kh", "kl")]
        fh, fl = [m.sb(f"pj_{n}", [32, CH], F16) for n in ("fh", "fl")]
        vp = m.sb("pj_vp", [P, NT, HEADS, VW])

        ln1, ln3 = Norm(m, "ln1"), Norm(m, "ln3")
        ffn = Ffn(m, "f1", bank[4:8], bank[6:8], {"wr": w["ffn_wr"], "wk": w["ffn_wk"], "wv": w["ffn_wv"],
                                       "mu_r": v["mu_r"], "mu_k": v["mu_k"]})
        x_loaded = m.sems("x_loaded0 x_loaded1")
        x2_stored = m.sems("x2_stored0 x2_stored1")
        (w_loaded, consts_set, sp_step, decay_set, scaled, far_split,
         bias_added, xin_ready, xin_done, gx_ready, gx_done, ga_ready, ga_done, a_done, a2_done, z_done, sq_done,
         xg_done, u_done, h_done, y_ready, x1_done, lt_free,
         q_ready, qh_done, ql_done, k_ready, kh_done, kl_done, f_ready, fh_done, fl_done, vv_ready, vv_done,
         q_stored, k_stored, f_stored, v_stored) = m.sems(
             "w_loaded consts_set sp_step decay_set scaled far_split "
             "bias_added xin_ready xin_done gx_ready gx_done ga_ready ga_done a_done a2_done z_done sq_done "
             "xg_done u_done h_done y_ready x1_done lt_free "
             "q_ready qh_done ql_done k_ready kh_done kl_done f_ready fh_done fl_done vv_ready vv_done "
             "q_stored k_stored f_stored v_stored")

        loads = [(w[n], rows(a[n])) for n in w_names] + [(v[n], a[n]) for n in v_names]
        loads += [(b_out, a["b_out"].unsqueeze(0).to_broadcast([P, D])), (bv, a["bv"].unsqueeze(0).to_broadcast([P, D])),
                  (far32, a["far"].rearrange("(f p) n -> p f n", p=P)), (bfar, a["bfar"]), (ident, a["ident"])]
        w_all = 16 * len(loads)
        nu = nb * NC

        def rounds(eng, body):
            for u in range(4):
                body(u, u // 2, u % 2, (True, u > 0, u > 1), nu - 1 - u)
            if nb > 3:
                with eng.Fori(2, nb - 1) as b:
                    for c in range(NC):
                        body(b * NC + c, b, c, (True, True, True), 2)
            for u in range(nu - 2, nu + 2):
                body(u, u // 2, u % 2, (u < nu, u <= nu, True), nu - 1 - u)

        block = ctx.enter_context(nc.Block())

        @block.sync
        def _(sp):
            for dst, src in loads:
                sp.dma_start(dst[:], src).then_inc(w_loaded, 16)

            def load_x(b, c):
                sp.dma_start(xl[c][:], a["x"][b, c * CH:(c + 1) * CH, :].rearrange("(t p) d -> p t d", p=P))\
                  .then_inc(x_loaded[c], 16)

            load_x(0, 0)
            load_x(0, 1)

            def body(u, b, c, on, nxt):
                if on[1]:
                    c1, b1 = 1 - c, b - (1 - c)
                    sp.wait_ge(ffn.x_done, u)
                    sp.dma_start(scr["x2"][b1, c1 * CH:(c1 + 1) * CH, :].rearrange("(t p) d -> p t d", p=P), xb[c1][:])\
                      .then_inc(x2_stored[c1], 16)
                if on[2]:
                    b2, tok = b - 1, c * CH
                    for hi, lo, lo_done, name, stored in ((qh, ql, ql_done, "q", q_stored),
                                                          (kh, kl, kl_done, "k", k_stored)):
                        sp.wait_ge(lo_done, (u - 2) * NF + NF)
                        for part, src in ((1, lo), (0, hi)):
                            sp.dma_start(scr[name][part, b2, :, tok:tok + CH].rearrange("(f p) t -> p f t", p=P),
                                         src[:]).then_inc(stored, 16)
                    for part, src, done in ((0, fh, fh_done), (1, fl, fl_done)):
                        sp.wait_ge(done, u - 1)
                        for s in range(2):
                            sp.dma_start(scr["far"][part, s, b2, :, tok:tok + CH], src[s * HEADS:(s + 1) * HEADS, :])\
                              .then_inc(f_stored, 16)
                    sp.wait_ge(vv_done, (u - 2) * 2 + 2)
                    for t in range(NT):
                        sp.dma_start(scr["v"][b2, :, tok + t * P:tok + (t + 1) * P, :].rearrange("r p v -> p r v"),
                                     vp[:, t].rearrange("p (r h) v -> p r (h v)", r=NPR)).then_inc(v_stored, 16)
                if nxt >= 2:
                    sp.wait_ge(bias_added, u + 1)
                    sp.wait_ge(ln1.norm_done, u * NT + NT)
                    load_x(b + 1, c)

            rounds(sp, body)
            for sem in x2_stored:
                sp.wait_ge(sem, 16 * nb)
            for sem, n in ((q_stored, 2), (k_stored, 2), (f_stored, 4), (v_stored, NT)):
                sp.wait_ge(sem, 16 * n * nu)

        @block.gpsimd
        def _(pool):
            pool.memset(minus_half[:], -0.5).then_inc(consts_set, 1)
            pool.memset(eps[:], EPS).then_inc(consts_set, 1)
            pool.memset(vp[:], 0.0).then_inc(consts_set, 1)
            pool.wait_ge(consts_set, 3)
            pool.memset(vp[:, :, :, HD:HD + 1], 1.0).then_inc(consts_set, 1)
            pool.wait_ge(w_loaded, w_all)
            pool.tensor_scalar(w["Wk"][:], w["Wk"][:], 0.25, None, ALU.mult).then_inc(scaled, 1)
            pool.tensor_scalar(v["bk"][:], v["bk"][:], 0.25, None, ALU.mult).then_inc(scaled, 1)
            pool.tensor_scalar(v["b_gx"][:], v["b_gx"][:], 0.5, None, ALU.mult).then_inc(scaled, 1)
            pool.tensor_scalar(v["b_ga"][:], v["b_ga"][:], 0.5, None, ALU.mult).then_inc(scaled, 1)

            def body(u, b, c, on, nxt):
                if isinstance(u, int) and u == 0:
                    ln1.pool_rstd(pool, 0, 0, eps, minus_half)
                if on[0]:
                    pool.wait_ge(x_loaded[c], b * 16 + 16)
                    if on[2]:
                        pool.wait_ge(x2_stored[c], b * 16)
                        pool.wait_ge(ln3.norm_done, (u - 1) * NT)
                    pool.tensor_tensor(xb[c][:], xl[c][:], b_out[:].unsqueeze(1).to_broadcast([P, NT, D]), ALU.add)\
                        .then_inc(bias_added, 1)
                if on[1]:
                    ffn.pool_square(pool, u - 1)
                    ln3.pool_rstd(pool, u - 1, 1 - c, eps, minus_half)
                if on[0]:
                    ffn.ln.pool_rstd(pool, u, c, eps, minus_half)
                if nxt >= 1:
                    ln1.pool_rstd(pool, u + 1, 1 - c, eps, minus_half)

            rounds(pool, body)

        @block.scalar
        def _(act):
            act.wait_ge(w_loaded, w_all)
            act.wait_ge(sp_step, 1)
            act.activation(sp_b[:], sp_a[:], ACT.Exp, scale=-1.0).then_inc(sp_step, 1)
            act.wait_ge(sp_step, 2)
            act.activation(sp_c[:], sp_b[:], ACT.Ln, bias=1.0).then_inc(sp_step, 1)
            act.wait_ge(scaled, 4)
            act.wait_ge(decay_set, 1)

            def body(u, b, c, on, nxt):
                if on[0]:
                    ln1.act_copy(act, u, c, bank[0:2], lnt)
                    for o in range(NF):
                        act.wait_ge(xin_ready, u * NF + o + 1)
                        if o == 0 and on[1]:
                            act.wait_ge(xg_done, u)
                        act.activation(xin[:, o, :], bank[2 + o][:], ACT.Identity, bias=v["b_in"][:, o:o + 1])\
                           .then_inc(xin_done, 1)
                if on[1]:
                    ffn.act_input(act, u - 1, 1 - c)
                    ffn.act_rk(act, u - 1)
                if on[0]:
                    if on[1]:
                        act.wait_ge(h_done, u * NF)
                    for o in range(NF):
                        act.wait_ge(gx_ready, u * NF + o + 1)
                        act.activation(tgx[:, o, :], bank[o][:], ACT.Tanh, bias=v["b_gx"][:, o:o + 1], scale=0.5)\
                           .then_inc(gx_done, 1)
                    for o in range(NF):
                        act.wait_ge(ga_ready, u * NF + o + 1)
                        act.activation(tga[:, o, :], bank[2 + o][:], ACT.Tanh, bias=v["b_ga"][:, o:o + 1], scale=0.5)\
                           .then_inc(ga_done, 1)
                    act.wait_ge(ga_done, u * NF + NF)
                    for o in range(NF):
                        act.activation(aa[:, o, :], tga[:, o, :], ACT.Exp, bias=decay[:, o:o + 1],
                                       scale=decay[:, o:o + 1]).then_inc(a_done, 1)
                    act.wait_ge(z_done, u + 1)
                    act.activation(zz[:], zz[:], ACT.Sqrt).then_inc(sq_done, 1)
                if on[2]:
                    ln3.act_copy(act, u - 2, c, bank[4:6], lt)
                    for hi, ready, done, bb, stored, bk in ((qh, q_ready, qh_done, v["bq"], q_stored, bank[6:8]),
                                                            (kh, k_ready, kh_done, v["bk"], k_stored, bank[4:6])):
                        for o in range(NF):
                            act.wait_ge(ready, (u - 2) * NF + o + 1)
                            if o == 0:
                                wait_pos(act, stored, (u - 2) * 32)
                            act.activation(hi[:, o, :], bk[o][:], ACT.Identity, bias=bb[:, o:o + 1]).then_inc(done, 1)
                    act.wait_ge(f_ready, u - 1)
                    wait_pos(act, f_stored, (u - 2) * 64)
                    act.activation(fh[:], bank[6][0:32, :], ACT.Identity, bias=bfar[:]).then_inc(fh_done, 1)

            rounds(act, body)

        @block.vector
        def _(dve):
            dve.wait_ge(w_loaded, w_all)
            dve.scalar_tensor_tensor(sp_a[:], v["a_param"][:], -1.0, v["a_param"][:], ALU.mult, ALU.max)\
               .then_inc(sp_step, 1)
            dve.wait_ge(sp_step, 3)
            dve.scalar_tensor_tensor(decay[:], v["a_param"][:], 0.0, sp_c[:], ALU.max, ALU.add).then_inc(sp_step, 1)
            dve.wait_ge(sp_step, 4)
            dve.tensor_scalar(decay[:], decay[:], -4.0, None, ALU.mult).then_inc(decay_set, 1)
            dve.tensor_copy(far_h[:], far32[:]).then_inc(far_split, 1)
            dve.wait_ge(far_split, 1)
            dve.tensor_tensor(far_l[:], far32[:], far_h[:], ALU.subtract).then_inc(far_split, 1)
            ffn.dve_init(dve)

            def ln1_of(u, b, c):
                dve.wait_ge(x_loaded[c], b * 16 + 16)
                ln1.dve_stats(dve, u, c, xl[c])
                ln1.dve_apply(dve, u, c, xl[c])

            def body(u, b, c, on, nxt):
                if on[1]:
                    ffn.dve_mix(dve, u - 1, b - (1 - c), 1 - c)
                if on[0]:
                    dve.wait_ge(gx_done, u * NF + NF)
                    dve.wait_ge(xin_done, u * NF + NF)
                    dve.scalar_tensor_tensor(tgx[:], tgx[:], 1.0, xin[:], ALU.add, ALU.mult).then_inc(xg_done, 1)
                    dve.wait_ge(a_done, u * NF + NF)
                    dve.scalar_tensor_tensor(zz[:], aa[:], -1.0, aa[:], ALU.mult, ALU.mult).then_inc(a2_done, 1)
                    dve.wait_ge(a2_done, u + 1)
                    dve.tensor_scalar(zz[:], zz[:], 1.0, 0.0, ALU.add, ALU.max).then_inc(z_done, 1)
                if on[1]:
                    ffn.dve_out(dve, u - 1, xb[1 - c])
                    ln3.dve_stats(dve, u - 1, 1 - c, xb[1 - c])
                if on[0]:
                    dve.wait_ge(sq_done, u + 1)
                    dve.wait_ge(xg_done, u + 1)
                    dve.scalar_tensor_tensor(tgx[:], zz[:], 0.5, tgx[:], ALU.mult, ALU.mult).then_inc(u_done, 1)
                    dve.wait_ge(u_done, u + 1)
                    if on[1]:
                        dve.wait_ge(h_done, u * NF)
                    for f in range(NF):
                        start = 0.0 if c == 0 else hh[0][:, f, CH - 1:CH]
                        dve.tensor_tensor_scan(hh[c][:, f, :], aa[:, f, :], tgx[:, f, :], start, ALU.mult, ALU.add)\
                           .then_inc(h_done, 1)
                if on[1]:
                    ln3.dve_apply(dve, u - 1, 1 - c, xb[1 - c])
                if on[2]:
                    for hi, lo, done, lo_done, bb, stored, bk in (
                            (qh, ql, qh_done, ql_done, v["bq"], q_stored, bank[6:8]),
                            (kh, kl, kh_done, kl_done, v["bk"], k_stored, bank[4:6])):
                        for o in range(NF):
                            dve.wait_ge(done, (u - 2) * NF + o + 1)
                            if o == 0:
                                wait_pos(dve, stored, (u - 2) * 32)
                            dve.scalar_tensor_tensor(lo[:, o, :], bk[o][:], bb[:, o:o + 1], hi[:, o, :], ALU.add,
                                                     ALU.subtract).then_inc(lo_done, 1)
                    dve.wait_ge(fh_done, u - 1)
                    wait_pos(dve, f_stored, (u - 2) * 64)
                    dve.scalar_tensor_tensor(fl[:], bank[6][0:32, :], bfar[:], fh[:], ALU.add, ALU.subtract)\
                       .then_inc(fl_done, 1)
                    wait_pos(dve, v_stored, (u - 2) * NT * 16)
                    for h in range(2):
                        dve.wait_ge(vv_ready, (u - 2) * 2 + h + 1)
                        for t in range(2):
                            ins = dve.tensor_tensor(vp[:, 2 * h + t, :, 0:HD],
                                              bank[(7, 4)[h]][:, t * D:(t + 1) * D].rearrange("p (h d) -> p h d", d=HD),
                                              bv[:].rearrange("p (h d) -> p h d", d=HD), ALU.add)
                        ins.then_inc(vv_done, 1)
                if on[0]:
                    for h in range(2):
                        dve.wait_ge(y_ready, u * 2 + h + 1)
                        dve.wait_ge(bias_added, u + 1)
                        dve.tensor_tensor(xb[c][:, 2 * h:2 * h + 2, :],
                                          bank[h][:].rearrange("p (t d) -> p t d", t=2),
                                          xb[c][:, 2 * h:2 * h + 2, :], ALU.add).then_inc(x1_done, 1)
                    dve.wait_ge(x1_done, u * 2 + 2)
                    ffn.ln.dve_stats(dve, u, c, xb[c])
                if nxt >= 1:
                    ln1_of(u + 1, b + c, 1 - c)
                if on[0]:
                    ffn.ln.dve_apply(dve, u, c, xb[c])

            dve.wait_ge(consts_set, 4)
            ln1_of(0, 0, 0)
            rounds(dve, body)

        @block.tensor
        def _(pe):
            pe.wait_ge(w_loaded, w_all)
            pe.wait_ge(scaled, 4)
            pe.wait_ge(far_split, 2)

            def gate(src, wt, banks, ready, u, free):
                for o in range(NF):
                    free(o)
                    for f in range(NF):
                        mm = pe.matmul(banks[o][:], wt[:, f, o * P:(o + 1) * P], src[:, f, :],
                                       start=(f == 0), stop=(f == NF - 1))
                    mm.then_inc(ready, 1)

            def body(u, b, c, on, nxt):
                if on[0]:
                    ln1.pe_transpose(pe, u, c, bank[0:2], ident,
                                     lambda f: pe.wait_ge(x1_done, (u - 1) * 2 + f + 1) if on[1] else None)
                    pe.wait_ge(ln1.tr_copied, u * NF + NF)
                    gate(lnt, w["W_in"], bank[2:4], xin_ready, u,
                         lambda o: pe.wait_ge(ga_done, (u - 1) * NF + o + 1) if on[1] else None)
                if on[1]:
                    u1 = u - 1
                    def free_tr(f):
                        if not isinstance(u, int) or u > 2:
                            pe.wait_ge(*((vv_done, (u - 3) * 2 + 2), (kl_done, (u - 3) * NF + NF))[f])
                    ffn.ln.pe_transpose(pe, u1, 1 - c, bank[4:6], ident, free_tr)

                    def free_r(h):
                        if not isinstance(u, int) or u > 2:
                            pe.wait_ge(*((fl_done, u - 2), (vv_done, (u - 3) * 2 + 1))[h])
                        elif u == 2:
                            pe.wait_ge(ffn.rv_done, h + 1)
                    ffn.pe_rk(pe, u1, free_r, lambda o: pe.wait_ge(ffn.ln.tr_copied, u1 * NF + o + 1))
                if on[0]:
                    pe.wait_ge(xin_done, u * NF + NF)
                    gate(xin, w["W_gx"], bank[0:2], gx_ready, u, lambda o: None)
                    gate(xin, w["W_ga"], bank[2:4], ga_ready, u, lambda o: None)
                if on[1]:
                    ffn.pe_v(pe, u - 1, lambda h: pe.wait_ge(ffn.r_done, (u - 1) * 2 + h + 1))
                if on[2]:
                    u2 = u - 2
                    last = on[1]
                    ln3.pe_transpose(pe, u2, c, bank[4:6], ident,
                                     lambda f: pe.wait_ge(ffn.k_done, (u - 1) * NF + f + 1) if last else
                                     pe.wait_ge(*((vv_done, u2 * 2), (kl_done, u2 * NF))[f]))
                    pe.wait_ge(ln3.tr_copied, u2 * NF + NF)
                    gate(lt, w["Wq"], bank[6:8], q_ready, u2,
                         lambda o: pe.wait_ge(ffn.rv_done, (u - 1) * 2 + o + 1) if last else
                         pe.wait_ge(*((fl_done, u2), (vv_done, u2 * 2 - 1))[o]))
                    gate(lt, w["Wk"], bank[4:6], k_ready, u2, lambda o: None)
                    pe.wait_ge(ql_done, u2 * NF + NF)
                    for f in range(NF):
                        for qq in (qh, ql):
                            for ff in (far_h, far_l):
                                mm = pe.matmul(bank[6][0:32, :], ff[:, f, :], qq[:, f, :],
                                               start=(f == 0 and qq is qh and ff is far_h),
                                               stop=(f == NF - 1 and qq is ql and ff is far_l))
                    mm.then_inc(f_ready, 1)
                    for h in range(2):
                        bk = bank[(7, 4)[h]]
                        if h == 1:
                            pe.wait_ge(kl_done, u2 * NF + 1)
                        for t in (2 * h, 2 * h + 1):
                            for f in range(NF):
                                mm = pe.matmul(bk[:, (t % 2) * D:(t % 2 + 1) * D], lt[:, f, t * P:(t + 1) * P],
                                               w["Wv"][:, f, :], start=(f == 0), stop=(f == NF - 1))
                        mm.then_inc(vv_ready, 1)
                if on[0]:
                    pe.wait_ge(h_done, u * NF + NF)
                    pe.wait_ge(gx_done, u * NF + NF)
                    for h in range(2):
                        for t in (2 * h, 2 * h + 1):
                            for f in range(NF):
                                mm = pe.matmul(bank[h][:, (t % 2) * D:(t % 2 + 1) * D],
                                               hh[c][:, f, t * P:(t + 1) * P], w["W_out"][:, f, :],
                                               start=(f == 0), stop=(f == NF - 1))
                        mm.then_inc(y_ready, 1)

            rounds(pe, body)


def wait_pos(eng, sem, value):
    if not isinstance(value, int) or value > 0:
        eng.wait_ge(sem, value)


BAND, LEFT, RIGHT = range(3)


def variants(i, j0, j1):
    runs = ((LEFT, j0, min(j1, i - 1)), (BAND, max(j0, i - 1), min(j1, i + 2)), (RIGHT, max(j0, i + 2), j1))
    return [(v, a, b) for v, a, b in runs if a < b]


def attend(nc, a, scr, nb):
    npairs = nb * NPR
    LOOPS = (npairs - 2) // 3
    with ExitStack() as ctx:
        m = Pool(nc, ctx)
        st_bank = [m.ps(f"at_st{i}", [P, 2, CH]) for i in range(2)]
        mx_bank = [m.ps(f"at_mx{i}", [P, CH]) for i in range(2)]
        spare = m.ps("at_spare", [P, CH])
        o_bank = m.ps("at_o", [P, CH])

        qs = [m.sb(f"at_q{i}", [P, HP, S], F16) for i in range(3)]
        ks = [m.sb(f"at_k{i}", [P, 3, HP, S], F16) for i in range(3)]
        vs = [m.sb(f"at_v{i}", [P, NTI, HP * VW]) for i in range(3)]
        pos = [m.sb(f"at_pos{i}", [P, HP, NTI, WW]) for i in range(3)]
        tab = [m.sb(f"at_tab{i}", [P, HP, NTI // 2, TW]) for i in range(2)]
        pt = [m.sb(f"at_p{i}", [P, 2, CH]) for i in range(4)]
        os_ = m.sb("at_os", [P, CH])
        rden = m.sb("at_rden", [P, NT, HP])
        att = [m.sb(f"at_att{i}", [P, NT, HP * HD]) for i in range(2)]
        mx = [m.sb(f"at_mx_sb{i}", [P, 2, HP * NT]) for i in range(2)]
        mtop = m.sb("at_mtop", [P, HP * NT])
        mneg = [m.sb(f"at_mneg{i}", [P, HP * NT], F16) for i in range(2)]
        mrow = [m.sb(f"at_mrow{i}", [HP * NT, P], F16) for i in range(2)]
        w32 = m.sb("at_w32", [P, TW])
        w_hi = m.sb("at_w_hi", [P, TW], F16)
        w_lo = m.sb("at_w_lo", [P, TW], F16)
        wt = m.sb("at_wt", [P, TW], F16)
        sel = m.sb("at_sel", [P, 3])
        ident = m.sb("at_ident", [P, P])
        ident_b = m.sb("at_ident_b", [P, P], BF16)
        ident_h = m.sb("at_ident_h", [P, P], F16)
        pick = m.sb("at_pick", [P, HP * (HD + 1)])

        (c_loaded, c_set, wt_split, wt_loaded, tab_ready, tab_copied, mx_ready, mx_done, mtop_done, mneg_done,
         mrow_ready, mrow_copied, st_ready, exp_done, av_done, o_copied, out_ready, rden_done, att_done) = m.sems(
             "c_loaded c_set wt_split wt_loaded tab_ready tab_copied mx_ready mx_done mtop_done mneg_done "
             "mrow_ready mrow_copied st_ready exp_done av_done o_copied out_ready rden_done att_done")
        q_loaded, k_loaded, v_loaded = [m.sems(" ".join(f"{n}_loaded{i}" for i in range(3))) for n in "qkv"]
        tab_written, pos_loaded, mrow_loaded, att_stored = [
            m.sems(f"{n}0 {n}1") for n in ("tab_written", "pos_loaded", "mrow_loaded", "att_stored")]
        N_CONST = 9

        tab_steps = [2 + (i * 14) // 16 for i in range(16)]

        def turns(eng, body):
            def at(n):
                body(n, n % 3, lambda k: (n + k) // 3,
                     dict(prev=1 <= n <= npairs, now=0 <= n < npairs, nxt=0 <= n + 1 < npairs, far=n + 2 < npairs))

            for n in range(-2, 3):
                at(n)
            if LOOPS > 1:
                with eng.Fori(1, LOOPS) as it:
                    for j in range(3):
                        body(it * 3 + j, j, lambda k, j=j: it + (j + k) // 3,
                             dict(prev=True, now=True, nxt=True, far=True))
            for n in range(max(3 * LOOPS, 3), npairs + 1):
                at(n)

        block = ctx.enter_context(nc.Block())

        @block.sync
        def _(sp):
            for dst, src in ((ident[:], a["ident"]), (pick[:], a["pick"]), (sel[R_ONE:R_MAX + 1, :], a["sel"]),
                             (w32[R_ONE:R_ONE + 2, :], a["br_pad"].unsqueeze(0).to_broadcast([2, TW]))):
                sp.dma_start(dst, src).then_inc(c_loaded, 16)
            for r in range(4):
                sp.dma_start(w32[r * HD:(r + 1) * HD, :], a["wr_pad"]).then_inc(c_loaded, 16)
            sp.wait_ge(wt_split, 2)
            for lo, r0, r1 in ((0, 0, 32), (1, 32, 64), (0, 64, 65), (1, 65, 66)):
                sp.dma_start(wt[r0:r1, :], (w_hi, w_lo)[lo][r0:r1, :]).then_inc(wt_loaded, 16)

            def write_tables(n, h):
                wait_pos(sp, pos_loaded[h], n * 32)
                sp.wait_ge(tab_copied, n * 16 + 8 * h + 8)
                sp.dma_start(dram(scr["tab"], h * HP * NT * P * TW, [[TW, P], [P * TW, HP * NT], [1, TW]]),
                             tab[h][:].rearrange("p h t w -> p (h t) w")).then_inc(tab_written[h], 16)

            def read_windows(n, slot, h):
                sp.wait_ge(tab_written[h], n * 16 + 16)
                for hh in range(HP):
                    sp.dma_start(pos[slot][:, hh, h * NT:(h + 1) * NT, :],
                                 dram(scr["tab"], (h * HP + hh) * NT * P * TW + P - 1,
                                      [[TW - 1, P], [P * TW, NT], [1, WW]])).then_inc(pos_loaded[h], 16)

            def load_mrow(n, slot, h):
                sp.wait_ge(mrow_copied, n * 2 + h + 1)
                for hh in range(HP):
                    sp.dma_start(qs[slot][R_MAX:R_MAX + 1, hh, h * CH:(h + 1) * CH],
                                 mrow[h][hh * NT:(hh + 1) * NT, :]).then_inc(mrow_loaded[h], 16)

            def store(n, h):
                sp.wait_ge(att_done, n * 2 + h + 1)
                sp.dma_start(dram(scr["att"], n * (S * HP * HD) + h * (CH * HP * HD),
                                  [[HP * HD, P], [P * HP * HD, NT], [1, HP * HD]]), att[h][:])\
                  .then_inc(att_stored[h], 16)

            def body(n, j, gen, on):
                if on["nxt"]:
                    write_tables(n + 1, 1)
                if on["now"]:
                    load_mrow(n, j % 3, 1)
                if on["nxt"]:
                    read_windows(n + 1, (j + 1) % 3, 1)
                if on["prev"]:
                    store(n - 1, 1)
                if on["far"]:
                    write_tables(n + 2, 0)
                if on["nxt"]:
                    load_mrow(n + 1, (j + 1) % 3, 0)
                if on["far"]:
                    read_windows(n + 2, (j + 2) % 3, 0)
                if on["now"]:
                    store(n, 0)

            turns(sp, body)
            for h in range(2):
                sp.wait_ge(att_stored[h], 16 * npairs)

        @block.gpsimd
        def _(pool):
            def load(n, slot):
                part, head = nb * D * S, HD * S
                for rep in range(2):
                    for x in range(2):
                        r0 = rep * 2 * HD + x * HD
                        pool.dma_start(qs[slot][r0:r0 + HD, :, :],
                                       dram(scr["q"], n * (HP * head) + x * part, [[S, HD], [head, HP], [1, S]]))\
                            .then_inc(q_loaded[slot], 16)
                for x in range(2):
                    pool.dma_start(qs[slot][R_FAR + 2 * x:R_FAR + 2 * x + 2, :, :],
                                   dram(scr["far"], n * (HP * S) + x * (2 * nb * HEADS * S),
                                        [[nb * HEADS * S, 2], [S, HP], [1, S]])).then_inc(q_loaded[slot], 16)
                for rep in range(2):
                    for x in range(2):
                        r0 = rep * 2 * HD + x * HD
                        for v in range(3):
                            pool.dma_start(ks[slot][r0:r0 + HD, v, :, :],
                                           dram(scr["k"], n * (HP * head) + rep * part, [[S, HD], [head, HP], [1, S]]))\
                                .then_inc(k_loaded[slot], 16)

            def load_v(n, slot):
                pool.dma_start(vs[slot][:], dram(scr["v"], n * (S * HP * VW),
                                                 [[HP * VW, P], [P * HP * VW, NTI], [1, HP * VW]]))\
                    .then_inc(v_loaded[slot], 16)

            def body(n, j, gen, on):
                if on["far"]:
                    if on["prev"]:
                        pool.wait_ge(st_ready, n * 16)
                    load(n + 2, (j + 2) % 3)
                    if on["prev"]:
                        pool.wait_ge(av_done, n * 8)
                    load_v(n + 2, (j + 2) % 3)

            turns(pool, body)

        @block.scalar
        def _(act):
            def body(n, j, gen, on):
                for k in range(16):
                    if on["now"]:
                        act.wait_ge(st_ready, n * 16 + k + 1)
                        wait_pos(act, av_done, n * 8 + k // 2 - 1)
                        act.activation(pt[k % 4][:], st_bank[k % 2][:], ACT.Exp).then_inc(exp_done, 1)
                    if on["far"]:
                        for i in [i for i in range(16) if tab_steps[i] == k]:
                            h = i // 8
                            act.wait_ge(tab_ready, (n + 2) * 16 + i + 1)
                            if i % 8 == 0:
                                wait_pos(act, tab_written[h], (n + 2) * 16)
                            act.activation(tab[h][:, (i % 8) // NT, i % NT, :], spare[:], ACT.Identity)\
                               .then_inc(tab_copied, 1)

            turns(act, body)

        @block.vector
        def _(dve):
            for s in range(3):
                dve.memset(qs[s][R_ONE:R_FAR, :, :], 1.0).then_inc(c_set, 1)
            dve.wait_ge(c_loaded, 8 * 16)
            for s in range(3):
                for v in range(3):
                    dve.tensor_copy(ks[s][R_ONE:R_MAX + 1, v, :, :].rearrange("p h s -> p (h s)"),
                                    sel[R_ONE:R_MAX + 1, v:v + 1].to_broadcast([R_MAX + 1 - R_ONE, HP * S]))\
                       .then_inc(c_set, 1)
            dve.tensor_copy(ident_b[:], ident[:]).then_inc(c_set, 1)
            dve.tensor_copy(ident_h[:], ident[:]).then_inc(c_set, 1)
            dve.tensor_copy(w_hi[0:K_TAB, :], w32[0:K_TAB, :]).then_inc(wt_split, 1)
            dve.wait_ge(wt_split, 1)
            dve.tensor_tensor(w_lo[0:K_TAB, :], w32[0:K_TAB, :], w_hi[0:K_TAB, :], ALU.subtract).then_inc(wt_split, 1)

            def negate(n, h):
                dve.wait_ge(mx_done, n * 32 + 16 * h + 16)
                dve.tensor_tensor(mtop[:], mx[h][:, 0, :], mx[h][:, 1, :], ALU.max).then_inc(mtop_done, 1)
                dve.wait_ge(mtop_done, n * 2 + h + 1)
                dve.tensor_scalar(mneg[h][:], mtop[:], -1.0, None, ALU.mult).then_inc(mneg_done, 1)

            def copy_mrow(n, h):
                dve.wait_ge(mrow_ready, n * 2 + h + 1)
                wait_pos(dve, mrow_loaded[h], n * 32)
                dve.tensor_copy(mrow[h][:], spare[0:HP * NT, 0:P]).then_inc(mrow_copied, 1)

            def copy_o(n, h):
                dve.wait_ge(av_done, n * 8 + 4 * h + 4)
                wait_pos(dve, out_ready, n * 2 + h)
                dve.tensor_copy(os_[:], o_bank[:]).then_inc(o_copied, 1)

            def normalise(n, h):
                dve.wait_ge(out_ready, n * 2 + h + 1)
                out = spare[:, 0:NT * HP * (HD + 1)].rearrange("p (t h v) -> p t h v", t=NT, h=HP)
                dve.reciprocal(rden[:].unsqueeze(3), out[:, :, :, HD:HD + 1]).then_inc(rden_done, 1)
                dve.wait_ge(rden_done, n * 2 + h + 1)
                wait_pos(dve, att_stored[h], n * 16)
                dve.tensor_tensor(att[h][:].rearrange("p t (h v) -> p t h v", h=HP), out[:, :, :, 0:HD],
                                  rden[:].unsqueeze(3).to_broadcast([P, NT, HP, HD]), ALU.mult).then_inc(att_done, 1)

            def body(n, j, gen, on):
                for k in range(16):
                    if k == 0 and on["now"]:
                        negate(n, 1)
                    if k == 2 and on["now"]:
                        copy_mrow(n, 1)
                    if k == 2 and on["prev"]:
                        copy_o(n - 1, 1)
                    if k == 5 and on["prev"]:
                        normalise(n - 1, 1)
                    if k == 8 and on["nxt"]:
                        negate(n + 1, 0)
                    if k == 10 and on["nxt"]:
                        copy_mrow(n + 1, 0)
                    if k == 10 and on["now"]:
                        copy_o(n, 0)
                    if k == 13 and on["now"]:
                        normalise(n, 0)
                    if on["nxt"]:
                        for kh in range(2):
                            dve.wait_ge(mx_ready, (n + 1) * 32 + 2 * k + kh + 1)
                            dve.tensor_reduce(mx[k // 8][:, kh, k % 8:k % 8 + 1], mx_bank[kh][:], AX_X, ALU.max)\
                               .then_inc(mx_done, 1)

            turns(dve, body)

        @block.tensor
        def _(pe):
            pe.wait_ge(c_loaded, 8 * 16)
            pe.wait_ge(c_set, 3 + 9 + 2)
            pe.wait_ge(wt_loaded, 4 * 16)

            def scores(n, slot, k):
                h, jp, hh = k // 8, (k % 8) // 2, k % 2
                if k % 8 == 0:
                    pe.wait_ge(mrow_loaded[h], n * 32 + 32)
                wait_pos(pe, exp_done, n * 16 + k - 1)
                for jj in range(2):
                    jt = 2 * jp + jj
                    out = st_bank[k % 2][:, jj, :]
                    tiles = range(h * NT, (h + 1) * NT)
                    runs = [(v, [i for i in tiles if test(i - jt)]) for v, test in
                            ((RIGHT, lambda x: x <= -2), (BAND, lambda x: abs(x) <= 1), (LEFT, lambda x: x >= 2))]
                    runs = [(v, r) for v, r in runs if r]
                    near = [i for v, r in runs if v == BAND for i in r]
                    for at, (v, r) in enumerate(runs):
                        mm = pe.matmul(out[:, (r[0] - h * NT) * P:(r[-1] + 1 - h * NT) * P],
                                       ks[slot][0:K_SC, v, hh, jt * P:(jt + 1) * P],
                                       qs[slot][0:K_SC, hh, r[0] * P:(r[-1] + 1) * P],
                                       start=(at == 0), stop=(v != BAND), skip_group_check=True)
                    for i in near:
                        w0 = (jt - i + 1) * P
                        mm = pe.matmul(out[:, (i - h * NT) * P:(i + 1 - h * NT) * P],
                                       pos[slot][:, hh, i, w0:w0 + P], ident[:], start=False, stop=True,
                                       skip_group_check=True)
                mm.then_inc(st_ready, 1)

            def maxima(n, slot, k, gen):
                h, hh, i = k // 8, (k % 8) // NT, (k // 8) * NT + k % NT
                if k == 0:
                    pe.wait_ge(k_loaded[slot], (gen + 1) * 12 * 16)
                if k % 8 == 0:
                    pe.wait_ge(pos_loaded[h], (n + 1) * 2 * 16)
                for kh in range(2):
                    wait_pos(pe, mx_done, n * 32 + 2 * k + kh - 1)
                    out = mx_bank[kh]
                    j0 = kh * NT
                    runs = variants(i, j0, j0 + NT)
                    for at, (v, ja, jb) in enumerate(runs):
                        mm = pe.matmul(out[:, (ja - j0) * P:(jb - j0) * P], qs[slot][0:K_MAXP, hh, i * P:(i + 1) * P],
                                       ks[slot][0:K_MAXP, v, hh, ja * P:jb * P], start=(at == 0), stop=(v != BAND),
                                       skip_group_check=True)
                    for v, ja, jb in runs:
                        if v == BAND:
                            upper = pos[slot][:, hh, i, :].bitcast(BF16).rearrange("p (w two) -> p w two", two=2)
                            mm = pe.matmul(out[:, (ja - j0) * P:(jb - j0) * P], ident_b[:],
                                           upper[:, (ja - i + 1) * P:(jb - i + 1) * P, 1], start=False, stop=True,
                                           skip_group_check=True)
                    mm.then_inc(mx_ready, 1)

            def table(n, slot, i, gen):
                h, hh, t = i // 8, (i % 8) // NT, (i // 8) * NT + i % NT
                if i == 0:
                    pe.wait_ge(q_loaded[slot], (gen + 1) * 6 * 16)
                pe.matmul(spare[:], qs[slot][0:K_TAB, hh, t * P:(t + 1) * P], wt[0:K_TAB, :], start=True, stop=True)\
                  .then_inc(tab_ready, 1)

            def turn_maxima(n, h):
                pe.wait_ge(mneg_done, n * 2 + h + 1)
                pe.matmul(spare[0:HP * NT, 0:P], mneg[h][:], ident_h[:], start=True, stop=True).then_inc(mrow_ready, 1)

            def values(n, slot, g, gen):
                h, jp = g // 4, g % 4
                if g == 0:
                    pe.wait_ge(v_loaded[slot], (gen + 1) * 16)
                if jp == 0:
                    wait_pos(pe, o_copied, n * 2 + h)
                pe.wait_ge(exp_done, n * 16 + 2 * g + 2)
                for hh in range(HP):
                    for jj in range(2):
                        r0 = (2 * hh + jj) * VW
                        mm = pe.matmul(o_bank[r0:r0 + VW, :], vs[slot][:, 2 * jp + jj, hh * VW:(hh + 1) * VW],
                                       pt[(2 * g + hh) % 4][:, jj, :], start=(jp == 0), stop=(jp == 3),
                                       skip_group_check=True)
                mm.then_inc(av_done, 1)

            def outputs(n, h):
                pe.wait_ge(o_copied, n * 2 + h + 1)
                w = HP * (HD + 1)
                for t in range(NT):
                    mm = pe.matmul(spare[:, t * w:(t + 1) * w], os_[:, t * P:(t + 1) * P], pick[:],
                                   start=True, stop=True)
                mm.then_inc(out_ready, 1)

            def body(n, j, gen, on):
                free = (tab_copied, n * 16 + 32) if on["nxt"] else (att_done, n * 2 - 1)
                for k in range(16):
                    if on["now"]:
                        scores(n, j % 3, k)
                    if on["nxt"]:
                        maxima(n + 1, (j + 1) % 3, k, gen(1))
                    if on["far"]:
                        for i in [i for i in range(16) if tab_steps[i] == k]:
                            wait_pos(pe, *free)
                            table(n + 2, (j + 2) % 3, i, gen(2))
                            free = (tab_copied, (n + 2) * 16 + i + 1)
                    if k == 1 and on["prev"]:
                        values(n - 1, (j - 1) % 3, 7, gen(-1))
                    if k % 2 == 1 and k > 1 and on["now"]:
                        values(n, j % 3, (k - 3) // 2, gen(0))
                    if k == 1 and on["now"]:
                        wait_pos(pe, *free)
                        turn_maxima(n, 1)
                        free = (mrow_copied, n * 2 + 2)
                    if k == 4 and on["prev"]:
                        wait_pos(pe, *free)
                        outputs(n - 1, 1)
                        free = (att_done, n * 2)
                    if k == 9 and on["nxt"]:
                        wait_pos(pe, *free)
                        turn_maxima(n + 1, 0)
                        free = (mrow_copied, n * 2 + 3)
                    if k == 12 and on["now"]:
                        wait_pos(pe, *free)
                        outputs(n, 0)
                        free = (att_done, n * 2 + 1)

            turns(pe, body)


def finish(nc, a, scr, nb):
    with ExitStack() as ctx:
        m = Pool(nc, ctx)
        bank = [m.ps(f"fi_bank{i}", [P, CH]) for i in range(6)]
        w_names = ["ffn_wr", "ffn_wk", "ffn_wv"]
        w = {n: m.sb(f"fi_{n}", [P, NF, D]) for n in w_names}
        v = {n: m.sb(f"fi_{n}", [P, NF]) for n in ("mu_r", "mu_k")}
        ident = m.sb("fi_ident", [P, P])
        eps = m.sb("fi_eps", [P, NT])
        minus_half = m.sb("fi_minus_half", [P, NT])
        xl = [m.sb(f"fi_xl{c}", [P, NT, D]) for c in range(2)]
        at = [m.sb(f"fi_at{c}", [P, NT, D]) for c in range(2)]
        xb = [m.sb(f"fi_xb{c}", [P, NT, D]) for c in range(2)]
        ffn = Ffn(m, "f2", bank[0:4], bank[4:6], {"wr": w["ffn_wr"], "wk": w["ffn_wk"], "wv": w["ffn_wv"], **v})
        w_loaded, consts_set, x3_done = m.sems("f2_w_loaded f2_consts_set x3_done")
        x_loaded = m.sems("x2_loaded0 x2_loaded1")
        out_stored = m.sems("out_stored0 out_stored1")
        loads = [(w[n], rows(a[n])) for n in w_names] + [(v[n], a[n]) for n in v] + [(ident, a["ident"])]
        w_all = 16 * len(loads)
        nu = nb * NC

        def rounds(eng, body):
            for u in range(2):
                body(u, 0, u, (True, u > 0), nu - 1 - u)
            with eng.Fori(1, nb - 1) as b:
                for c in range(NC):
                    body(b * NC + c, b, c, (True, True), 2)
            for u in range(nu - 2, nu + 1):
                body(u, u // 2, u % 2, (u < nu, True), nu - 1 - u)

        block = ctx.enter_context(nc.Block())

        @block.sync
        def _(sp):
            for dst, src in loads:
                sp.dma_start(dst[:], src).then_inc(w_loaded, 16)

            def load_x(b, c):
                tok = slice(c * CH, (c + 1) * CH)
                sp.dma_start(xl[c][:], scr["x2"][b, tok, :].rearrange("(t p) d -> p t d", p=P))\
                  .then_inc(x_loaded[c], 16)
                for t in range(NT):
                    r = c * CH + t * P
                    sp.dma_start(at[c][:, t, :].rearrange("p (r v) -> p r v", r=NPR),
                                 scr["att"][b, :, r:r + P, :].rearrange("r p v -> p r v")).then_inc(x_loaded[c], 16)

            load_x(0, 0)
            load_x(0, 1)

            def body(u, b, c, on, nxt):
                if nxt >= 2:
                    sp.wait_ge(x3_done, u + 1)
                    load_x(b + 1, c)
                if on[1]:
                    c1, b1 = 1 - c, b - (1 - c)
                    sp.wait_ge(ffn.x_done, u)
                    sp.dma_start(a["out"][b1, c1 * CH:(c1 + 1) * CH, :].rearrange("(t p) d -> p t d", p=P), xb[c1][:])\
                      .then_inc(out_stored[c1], 16)

            rounds(sp, body)
            for c in range(2):
                sp.wait_ge(out_stored[c], 16 * nb)

        @block.gpsimd
        def _(pool):
            pool.memset(minus_half[:], -0.5).then_inc(consts_set, 1)
            pool.memset(eps[:], EPS).then_inc(consts_set, 1)
            pool.wait_ge(consts_set, 2)
            ffn.ln.pool_rstd(pool, 0, 0, eps, minus_half)

            def body(u, b, c, on, nxt):
                if nxt >= 1:
                    ffn.ln.pool_rstd(pool, u + 1, 1 - c, eps, minus_half)
                if on[0]:
                    ffn.pool_square(pool, u)

            rounds(pool, body)

        @block.scalar
        def _(act):
            def body(u, b, c, on, nxt):
                if on[0]:
                    ffn.act_input(act, u, c)
                    if on[1]:
                        act.wait_ge(ffn.rv_done, u * 2)
                    ffn.act_rk(act, u)

            rounds(act, body)

        @block.vector
        def _(dve):
            dve.wait_ge(w_loaded, w_all)
            ffn.dve_init(dve)

            def x3_of(u, b, c):
                dve.wait_ge(x_loaded[c], b * 80 + 80)
                wait_pos(dve, out_stored[c], b * 16)
                dve.tensor_tensor(xb[c][:], xl[c][:], at[c][:], ALU.add).then_inc(x3_done, 1)
                dve.wait_ge(x3_done, u + 1)
                ffn.ln.dve_stats(dve, u, c, xb[c])

            x3_of(0, 0, 0)
            ffn.ln.dve_apply(dve, 0, 0, xb[0])

            def body(u, b, c, on, nxt):
                if nxt >= 1 and (not on[1]):
                    x3_of(u + 1, b + c, 1 - c)
                if on[0]:
                    ffn.dve_mix(dve, u, b, c)
                if on[1]:
                    ffn.dve_out(dve, u - 1, xb[1 - c])
                    if nxt >= 1:
                        x3_of(u + 1, b + c, 1 - c)
                if nxt >= 1:
                    ffn.ln.dve_apply(dve, u + 1, 1 - c, xb[1 - c])

            rounds(dve, body)

        @block.tensor
        def _(pe):
            pe.wait_ge(w_loaded, w_all)

            def body(u, b, c, on, nxt):
                if on[0]:
                    ffn.ln.pe_transpose(pe, u, c, bank[0:2], ident,
                                        lambda f: pe.wait_ge(ffn.k_done, (u - 1) * NF + f + 1) if on[1] else None)
                if on[1]:
                    ffn.pe_v(pe, u - 1, lambda h: wait_pos(pe, ffn.rv_done, (u - 2) * 2 + h + 1))
                if on[0]:
                    ffn.pe_rk(pe, u, lambda h: pe.wait_ge(ffn.r_done, (u - 1) * 2 + h + 1) if on[1] else None,
                              lambda o: pe.wait_ge(ffn.ln.tr_copied, u * NF + o + 1))

            rounds(pe, body)


def hybrid_kernel(nc, a, out):
    nb = a["x"].shape[0]
    a = dict(a, out=out)

    def scratch(name, shape, dt=F32):
        return nc.dram_tensor(name, shape, dt).ap()

    scr = {
        "x2": scratch("scr_x2", [nb, S, D]),
        "q": scratch("scr_q", [2, nb, D, S], F16),
        "k": scratch("scr_k", [2, nb, D, S], F16),
        "far": scratch("scr_far", [2, 2, nb, HEADS, S], F16),
        "v": scratch("scr_v", [nb, NPR, S, HP * VW]),
        "tab": scratch("scr_tab", [2, HP * NT * P, TW]),
        "att": scratch("scr_att", [nb, NPR, S, HP * HD]),
    }
    project(nc, a, scr, nb)
    attend(nc, a, scr, nb)
    finish(nc, a, scr, nb)


def _layout(x, W_in, b_in, W_gx, b_gx, W_ga, b_ga, a_param, W_out, b_out, Wqkv, bqkv, Wr, br, W_r, W_k, W_v, mu_r, mu_k):
    w = Wqkv.reshape(HEADS, 3, HD, D)
    bb = bqkv.reshape(HEADS, 3, HD)
    at = np.clip(np.arange(TW) - (P - 1), 0, R - 1)
    far = np.zeros((D, 32), np.float32)
    for h in range(HEADS):
        far[h * HD:(h + 1) * HD, h] = Wr[0]
        far[h * HD:(h + 1) * HD, HEADS + h] = Wr[R - 1]
    sel = np.zeros((R_MAX + 1 - R_ONE, 3), np.float32)
    sel[R_MAX - R_ONE, :] = 1.0
    for x2 in (0, 2):
        sel[R_FAR - R_ONE + x2, LEFT] = 1.0
        sel[R_FAR - R_ONE + x2 + 1, RIGHT] = 1.0
    pick = np.zeros((P, HP * (HD + 1)), np.float32)
    for hh in range(HP):
        for jj in range(2):
            for r in range(HD + 1):
                pick[(2 * hh + jj) * VW + r, hh * (HD + 1) + r] = 1.0

    def cols(v):
        return v.reshape(NF, P).T

    return {
        "x": x, "W_in": W_in, "b_in": cols(b_in), "W_gx": W_gx, "b_gx": cols(b_gx), "W_ga": W_ga, "b_ga": cols(b_ga),
        "a_param": cols(a_param), "W_out": W_out, "b_out": b_out,
        "Wq": w[:, 0].reshape(D, D).T, "Wk": w[:, 1].reshape(D, D).T, "Wv": w[:, 2].reshape(D, D).T,
        "bq": cols(bb[:, 0].reshape(D)), "bk": cols(bb[:, 1].reshape(D)), "bv": bb[:, 2].reshape(D),
        "wr_pad": Wr.T[:, at], "br_pad": br[at], "far": far,
        "bfar": np.repeat(br[[0, R - 1]], HEADS).reshape(2 * HEADS, 1),
        "sel": sel, "pick": pick, "ident": np.eye(P, dtype=np.float32),
        "ffn_wr": W_r.T, "ffn_wk": W_k.T, "ffn_wv": W_v.T, "mu_r": cols(mu_r), "mu_k": cols(mu_k),
    }


_ORDER = ["L0_attn_a_x", "L0_attn_a_W_in", "L0_attn_a_b_in", "L0_attn_a_W_gx", "L0_attn_a_b_gx", "L0_attn_a_W_ga",
          "L0_attn_a_b_ga", "L0_attn_a_a_param", "L0_attn_a_W_out", "L0_attn_a_b_out", "L0_attn_b_Wqkv",
          "L0_attn_b_bqkv", "L0_attn_b_Wr", "L0_attn_b_br", "L0_ffn_W_r", "L0_ffn_W_k", "L0_ffn_W_v",
          "L0_ffn_mu_r", "L0_ffn_mu_k"]


def kernel(**inputs):
    import concourse.bacc as _bacc
    from concourse.bass_utils import run_bass_kernel_spmd as _run

    nc = _bacc.Bacc("TRN2", target_bir_lowering=False, num_devices=1)
    arrays = {f"in_{k}": np.ascontiguousarray(v)
              for k, v in _layout(*[np.asarray(inputs[n]) for n in _ORDER]).items()}
    args = {k[3:]: nc.dram_tensor(k, v.shape, mybir.dt.from_np(v.dtype), kind="ExternalInput").ap()
            for k, v in arrays.items()}
    shape = arrays["in_x"].shape
    out = nc.dram_tensor("out", shape, F32, kind="ExternalOutput").ap()
    hybrid_kernel(nc, args, out)
    r = _run(nc, [arrays], core_ids=[0])
    return r.results[0]["out"]
```

```python
from contextlib import ExitStack

import numpy as np

import concourse.bass as bass
from concourse import mybir

F32 = mybir.dt.float32
F16 = mybir.dt.float16
BF16 = mybir.dt.bfloat16
ALU = mybir.AluOpType
ACT = mybir.ActivationFunctionType
AX_X = mybir.AxisListType.X

P = 128
D = 256
NF = D // P
S = 1024
CH = 512
NC = S // CH
NT = CH // P
HEADS = 16
HD = D // HEADS
WIN = 128
R = 2 * WIN + 1
EPS = 1e-5

HP = 2
NPR = HEADS // HP
VW = 32
NTI = S // P
TW = 512
NQ = 2 * HP
TLAG = 4
WW = 3 * P

R_ONE = 4 * HD
R_FAR = R_ONE + 2
R_MAX = R_FAR + 4
K_TAB, K_MAXP, K_SC = R_FAR, R_MAX, R_MAX + 1


def dram(t, offset, ap):
    return bass.AP(tensor=t.tensor, offset=offset, ap=ap)


class Pool:

    def __init__(self, nc, ctx):
        self.nc, self.ctx = nc, ctx

    def sb(self, name, shape, dt=F32):
        return self.ctx.enter_context(self.nc.sbuf_tensor(name, shape, dt))

    def ps(self, name, shape):
        return self.ctx.enter_context(self.nc.psum_tensor(name, shape, F32))

    def sems(self, names):
        return [self.ctx.enter_context(self.nc.semaphore(n)) for n in names.split()]


class Norm:

    def __init__(self, m, tag):
        self.stats = [m.sb(f"{tag}_stats{c}", [P, NT, 6]) for c in range(2)]
        self.mv = [m.sb(f"{tag}_mv{c}", [P, NT, 2]) for c in range(2)]
        self.ve = [m.sb(f"{tag}_ve{c}", [P, NT]) for c in range(2)]
        self.rstd = [m.sb(f"{tag}_rstd{c}", [P, NT]) for c in range(2)]
        self.gap = m.sb(f"{tag}_gap", [P, 1])
        self.xn = [m.sb(f"{tag}_xn{c}", [P, NT, D]) for c in range(2)]
        (self.stats_done, self.mv_done, self.ve_done, self.rstd_done, self.norm_done,
         self.tr_ready, self.tr_copied) = m.sems(" ".join(
             f"{tag}_{n}" for n in "stats_done mv_done ve_done rstd_done norm_done tr_ready tr_copied".split()))

    def dve_stats(self, dve, u, c, src):
        for t in range(NT):
            dve.bn_stats(self.stats[c][:, t, :], src[:, t, :]).then_inc(self.stats_done, 1)
        dve.wait_ge(self.stats_done, u * NT + NT)
        dve.memset(self.gap[:], 0.0)
        for t in range(NT):
            dve.bn_aggr(self.mv[c][:, t, :], self.stats[c][:, t, :]).then_inc(self.mv_done, 1)

    def pool_rstd(self, pool, u, c, eps, minus_half):
        pool.wait_ge(self.mv_done, u * NT + NT)
        pool.tensor_tensor(self.ve[c][:], self.mv[c][:, :, 1], eps[:], ALU.add).then_inc(self.ve_done, 1)
        pool.wait_ge(self.ve_done, u + 1)
        pool.tensor_tensor(self.rstd[c][:], self.ve[c][:], minus_half[:], ALU.pow).then_inc(self.rstd_done, 1)

    def dve_apply(self, dve, u, c, src):
        dve.wait_ge(self.rstd_done, u + 1)
        for t in range(NT):
            dve.tensor_scalar(self.xn[c][:, t, :], src[:, t, :], self.mv[c][:, t, 0:1],
                              self.rstd[c][:, t:t + 1], ALU.subtract, ALU.mult).then_inc(self.norm_done, 1)

    def pe_transpose(self, pe, u, c, banks, ident, free):
        pe.wait_ge(self.norm_done, u * NT + NT)
        for f in range(NF):
            free(f)
            for t in range(NT):
                tr = pe.transpose(banks[f][:, t * P:(t + 1) * P], self.xn[c][:, t, f * P:(f + 1) * P], ident[:])
            tr.then_inc(self.tr_ready, 1)

    def act_copy(self, act, u, c, banks, dst):
        for f in range(NF):
            act.wait_ge(self.tr_ready, u * NF + f + 1)
            act.activation(dst[:, f, :], banks[f][:], ACT.Identity).then_inc(self.tr_copied, 1)


class Ffn:

    def __init__(self, m, tag, banks, v_banks, w):
        self.w, self.banks, self.v_banks = w, banks, v_banks
        self.ln = Norm(m, tag)
        self.xt = [m.sb(f"{tag}_xt{c}", [P, NF, CH + 1]) for c in range(2)]
        self.diff = m.sb(f"{tag}_diff", [P, NF, CH])
        self.xr = m.sb(f"{tag}_xr", [P, NF, CH])
        self.xk = m.sb(f"{tag}_xk", [P, NF, CH])
        self.tr = m.sb(f"{tag}_tr", [P, NT, D])
        self.kr = m.sb(f"{tag}_kr", [P, NF, CH])
        self.ka = m.sb(f"{tag}_ka", [P, NF, CH])
        self.rv = m.sb(f"{tag}_rv", [P, NT, D])
        (self.zeroed, self.before_set, self.diff_done, self.mixed, self.r_ready, self.r_done, self.k_ready,
         self.k_done, self.ka_done, self.v_ready, self.rv_done, self.x_done) = m.sems(" ".join(
             f"{tag}_{n}" for n in ("zeroed before_set diff_done mixed r_ready r_done k_ready k_done ka_done "
                                    "v_ready rv_done x_done").split()))

    def dve_init(self, dve):
        dve.memset(self.xt[0][:, :, 0:1], 0.0).then_inc(self.zeroed, 1)
        dve.wait_ge(self.zeroed, 1)

    def act_input(self, act, u, c):
        self.ln.act_copy(act, u, c, self.banks[0:2], self.xt[c][:, :, 1:])
        if c == 1:
            act.wait_ge(self.ln.tr_copied, u * NF)
            act.activation(self.xt[1][:, :, 0:1], self.xt[0][:, :, CH:CH + 1], ACT.Identity)\
               .then_inc(self.before_set, 1)

    def dve_mix(self, dve, u, b, c):
        dve.wait_ge(self.ln.tr_copied, u * NF + NF)
        if c == 1:
            dve.wait_ge(self.before_set, b + 1)
        dve.tensor_tensor(self.diff[:], self.xt[c][:, :, 1:], self.xt[c][:, :, 0:CH], ALU.subtract)\
           .then_inc(self.diff_done, 1)
        dve.wait_ge(self.diff_done, u + 1)
        for dst, mu in ((self.xk, self.w["mu_k"]), (self.xr, self.w["mu_r"])):
            for f in range(NF):
                dve.scalar_tensor_tensor(dst[:, f, :], self.diff[:, f, :], mu[:, f:f + 1],
                                         self.xt[c][:, f, 0:CH], ALU.mult, ALU.add).then_inc(self.mixed, 1)

    def pe_kr(self, pe, u, free_k, free_r):
        pe.wait_ge(self.mixed, u * 2 * NF + NF)
        for o in range(NF):
            free_k(o)
            for f in range(NF):
                mm = pe.matmul(self.banks[o][:], self.w["wk"][:, f, o * P:(o + 1) * P], self.xk[:, f, :],
                               start=(f == 0), stop=(f == NF - 1))
            mm.then_inc(self.k_ready, 1)
        pe.wait_ge(self.mixed, u * 2 * NF + 2 * NF)
        for h in range(2):
            free_r(h)
            for t in (2 * h, 2 * h + 1):
                for f in range(NF):
                    mm = pe.matmul(self.banks[2 + h][:, (t % 2) * D:(t % 2 + 1) * D],
                                   self.xr[:, f, t * P:(t + 1) * P], self.w["wr"][:, f, :],
                                   start=(f == 0), stop=(f == NF - 1))
            mm.then_inc(self.r_ready, 1)

    def act_kr(self, act, u, used=None):
        for o in range(NF):
            act.wait_ge(self.k_ready, u * NF + o + 1)
            act.activation(self.kr[:, o, :], self.banks[o][:], ACT.Relu).then_inc(self.k_done, 1)
        if used is not None:
            act.wait_ge(self.rv_done, used)
        for h in range(2):
            act.wait_ge(self.r_ready, u * 2 + h + 1)
            act.activation(self.tr[:, 2 * h:2 * h + 2, :], self.banks[2 + h][:].rearrange("p (t d) -> p t d", t=2),
                           ACT.Tanh, scale=0.5).then_inc(self.r_done, 1)

    def pool_square(self, pool, u):
        for o in range(NF):
            pool.wait_ge(self.k_done, u * NF + o + 1)
            pool.tensor_tensor(self.ka[:, o, :], self.kr[:, o, :], self.kr[:, o, :], ALU.mult)\
                .then_inc(self.ka_done, 1)

    def pe_v(self, pe, u, free):
        pe.wait_ge(self.ka_done, u * NF + NF)
        for h in range(2):
            free(h)
            for t in (2 * h, 2 * h + 1):
                for f in range(NF):
                    mm = pe.matmul(self.v_banks[h][:, (t % 2) * D:(t % 2 + 1) * D],
                                   self.ka[:, f, t * P:(t + 1) * P], self.w["wv"][:, f, :],
                                   start=(f == 0), stop=(f == NF - 1))
            mm.then_inc(self.v_ready, 1)

    def dve_out(self, dve, u, x):
        for h in range(2):
            dve.wait_ge(self.r_done, u * 2 + h + 1)
            dve.wait_ge(self.v_ready, u * 2 + h + 1)
            dve.scalar_tensor_tensor(self.rv[:, 2 * h:2 * h + 2, :], self.tr[:, 2 * h:2 * h + 2, :], 1.0,
                                     self.v_banks[h][:].rearrange("p (t d) -> p t d", t=2),
                                     ALU.add, ALU.mult).then_inc(self.rv_done, 1)
        dve.wait_ge(self.rv_done, u * 2 + 2)
        dve.scalar_tensor_tensor(x[:], self.rv[:], 0.5, x[:], ALU.mult, ALU.add).then_inc(self.x_done, 1)
        dve.wait_ge(self.x_done, u + 1)


def rows(w):
    return w.rearrange("(f p) n -> p f n", p=P)


def project(nc, a, scr, nb):
    with ExitStack() as ctx:
        m = Pool(nc, ctx)
        bank = [m.ps(f"pj_bank{i}", [P, CH]) for i in range(8)]

        w_names = ["W_in", "W_gx", "W_ga", "W_out", "ffn_wr", "ffn_wk", "ffn_wv", "Wq", "Wk", "Wv"]
        w = {n: m.sb(f"pj_{n}", [P, NF, D]) for n in w_names}
        v_names = ["b_in", "b_gx", "b_ga", "a_param", "mu_r", "mu_k", "bq", "bk"]
        v = {n: m.sb(f"pj_{n}", [P, NF]) for n in v_names}
        b_out = m.sb("pj_b_out", [P, D])
        bv = m.sb("pj_bv", [P, D])
        far32 = m.sb("pj_far32", [P, NF, 32])
        far_h = m.sb("pj_far_h", [P, NF, 32], F16)
        far_l = m.sb("pj_far_l", [P, NF, 32], F16)
        bfar = m.sb("pj_bfar", [32, 1])
        ident = m.sb("pj_ident", [P, P])
        eps = m.sb("pj_eps", [P, NT])
        minus_half = m.sb("pj_minus_half", [P, NT])
        sp_a, sp_b, sp_c, decay = [m.sb(f"pj_sp{i}", [P, NF]) for i in range(4)]

        xl = [m.sb(f"pj_xl{c}", [P, NT, D]) for c in range(2)]
        xb = [m.sb(f"pj_xb{c}", [P, NT, D]) for c in range(2)]
        lnt = m.sb("pj_lnt", [P, NF, CH])
        xin = m.sb("pj_xin", [P, NF, CH])
        tgx = m.sb("pj_tgx", [P, NF, CH])
        tga = m.sb("pj_tga", [P, NF, CH])
        aa = m.sb("pj_aa", [P, NF, CH])
        zz = m.sb("pj_zz", [P, NF, CH])
        hh = [m.sb(f"pj_h{c}", [P, NF, CH]) for c in range(2)]
        lt = m.sb("pj_lt", [P, NF, CH])
        qh, ql, kh, kl = [m.sb(f"pj_{n}", [P, NF, CH], F16) for n in ("qh", "ql", "kh", "kl")]
        fh, fl = [m.sb(f"pj_{n}", [32, CH], F16) for n in ("fh", "fl")]
        vp = m.sb("pj_vp", [P, NT, HEADS, VW])

        ln1, ln3 = Norm(m, "ln1"), Norm(m, "ln3")
        ffn = Ffn(m, "f1", bank[4:8], bank[6:8], {"wr": w["ffn_wr"], "wk": w["ffn_wk"], "wv": w["ffn_wv"],
                                       "mu_r": v["mu_r"], "mu_k": v["mu_k"]})
        x_loaded = m.sems("x_loaded0 x_loaded1")
        x2_stored = m.sems("x2_stored0 x2_stored1")
        (w_loaded, consts_set, sp_step, decay_set, scaled, far_split,
         bias_added, xin_ready, xin_done, gx_ready, gx_done, ga_ready, ga_done, a_done, a2_done, z_done, sq_done,
         xg_done, u_done, h_done, y_ready, x1_done, lt_free,
         q_ready, qh_done, ql_done, k_ready, kh_done, kl_done, f_ready, fh_done, fl_done, vv_ready, vv_done,
         q_stored, k_stored, f_stored, v_stored) = m.sems(
             "w_loaded consts_set sp_step decay_set scaled far_split "
             "bias_added xin_ready xin_done gx_ready gx_done ga_ready ga_done a_done a2_done z_done sq_done "
             "xg_done u_done h_done y_ready x1_done lt_free "
             "q_ready qh_done ql_done k_ready kh_done kl_done f_ready fh_done fl_done vv_ready vv_done "
             "q_stored k_stored f_stored v_stored")

        loads = [(w[n], rows(a[n])) for n in w_names] + [(v[n], a[n]) for n in v_names]
        loads += [(b_out, a["b_out"].unsqueeze(0).to_broadcast([P, D])), (bv, a["bv"].unsqueeze(0).to_broadcast([P, D])),
                  (far32, a["far"].rearrange("(f p) n -> p f n", p=P)), (bfar, a["bfar"]), (ident, a["ident"])]
        w_all = 16 * len(loads)
        nu = nb * NC

        def rounds(eng, body):
            for u in range(4):
                body(u, u // 2, u % 2, (True, u > 0, u > 1), nu - 1 - u)
            if nb > 3:
                with eng.Fori(2, nb - 1) as b:
                    for c in range(NC):
                        body(b * NC + c, b, c, (True, True, True), 2)
            for u in range(nu - 2, nu + 2):
                body(u, u // 2, u % 2, (u < nu, u <= nu, True), nu - 1 - u)

        block = ctx.enter_context(nc.Block())

        @block.sync
        def _(sp):
            for dst, src in loads:
                sp.dma_start(dst[:], src).then_inc(w_loaded, 16)

            def load_x(b, c):
                sp.dma_start(xl[c][:], a["x"][b, c * CH:(c + 1) * CH, :].rearrange("(t p) d -> p t d", p=P))\
                  .then_inc(x_loaded[c], 16)

            load_x(0, 0)
            load_x(0, 1)

            def body(u, b, c, on, nxt):
                if on[1]:
                    c1, b1 = 1 - c, b - (1 - c)
                    sp.wait_ge(ffn.x_done, u)
                    sp.dma_start(scr["x2"][b1, c1 * CH:(c1 + 1) * CH, :].rearrange("(t p) d -> p t d", p=P), xb[c1][:])\
                      .then_inc(x2_stored[c1], 16)
                if on[2]:
                    b2, tok = b - 1, c * CH
                    for hi, lo, lo_done, name, stored in ((qh, ql, ql_done, "q", q_stored),
                                                          (kh, kl, kl_done, "k", k_stored)):
                        sp.wait_ge(lo_done, (u - 2) * NF + NF)
                        for part, src in ((1, lo), (0, hi)):
                            sp.dma_start(scr[name][part, b2, :, tok:tok + CH].rearrange("(f p) t -> p f t", p=P),
                                         src[:]).then_inc(stored, 16)
                    for part, src, done in ((0, fh, fh_done), (1, fl, fl_done)):
                        sp.wait_ge(done, u - 1)
                        for s in range(2):
                            sp.dma_start(scr["far"][part, s, b2, :, tok:tok + CH], src[s * HEADS:(s + 1) * HEADS, :])\
                              .then_inc(f_stored, 16)
                    sp.wait_ge(vv_done, (u - 2) * 2 + 2)
                    for t in range(NT):
                        sp.dma_start(scr["v"][b2, :, tok + t * P:tok + (t + 1) * P, :].rearrange("r p v -> p r v"),
                                     vp[:, t].rearrange("p (r h) v -> p r (h v)", r=NPR)).then_inc(v_stored, 16)
                if nxt >= 2:
                    sp.wait_ge(bias_added, u + 1)
                    sp.wait_ge(ln1.norm_done, u * NT + NT)
                    load_x(b + 1, c)

            rounds(sp, body)
            for sem in x2_stored:
                sp.wait_ge(sem, 16 * nb)
            for sem, n in ((q_stored, 2), (k_stored, 2), (f_stored, 4), (v_stored, NT)):
                sp.wait_ge(sem, 16 * n * nu)

        @block.gpsimd
        def _(pool):
            pool.memset(minus_half[:], -0.5).then_inc(consts_set, 1)
            pool.memset(eps[:], EPS).then_inc(consts_set, 1)
            pool.memset(vp[:], 0.0).then_inc(consts_set, 1)
            pool.wait_ge(consts_set, 3)
            pool.memset(vp[:, :, :, HD:HD + 1], 1.0).then_inc(consts_set, 1)
            pool.wait_ge(w_loaded, w_all)
            pool.tensor_scalar(w["Wk"][:], w["Wk"][:], 0.25, None, ALU.mult).then_inc(scaled, 1)
            pool.tensor_scalar(v["bk"][:], v["bk"][:], 0.25, None, ALU.mult).then_inc(scaled, 1)
            pool.tensor_scalar(v["b_gx"][:], v["b_gx"][:], 0.5, None, ALU.mult).then_inc(scaled, 1)
            pool.tensor_scalar(v["b_ga"][:], v["b_ga"][:], 0.5, None, ALU.mult).then_inc(scaled, 1)

            def body(u, b, c, on, nxt):
                if isinstance(u, int) and u == 0:
                    ln1.pool_rstd(pool, 0, 0, eps, minus_half)
                if on[0]:
                    pool.wait_ge(x_loaded[c], b * 16 + 16)
                    if on[2]:
                        pool.wait_ge(x2_stored[c], b * 16)
                        pool.wait_ge(ln3.norm_done, (u - 1) * NT)
                    pool.tensor_tensor(xb[c][:], xl[c][:], b_out[:].unsqueeze(1).to_broadcast([P, NT, D]), ALU.add)\
                        .then_inc(bias_added, 1)
                if nxt >= 1:
                    ln1.pool_rstd(pool, u + 1, 1 - c, eps, minus_half)
                if on[1]:
                    ffn.pool_square(pool, u - 1)
                    ln3.pool_rstd(pool, u - 1, 1 - c, eps, minus_half)
                if on[0]:
                    ffn.ln.pool_rstd(pool, u, c, eps, minus_half)

            rounds(pool, body)

        @block.scalar
        def _(act):
            act.wait_ge(w_loaded, w_all)
            act.wait_ge(sp_step, 1)
            act.activation(sp_b[:], sp_a[:], ACT.Exp, scale=-1.0).then_inc(sp_step, 1)
            act.wait_ge(sp_step, 2)
            act.activation(sp_c[:], sp_b[:], ACT.Ln, bias=1.0).then_inc(sp_step, 1)
            act.wait_ge(scaled, 4)
            act.wait_ge(decay_set, 1)

            def body(u, b, c, on, nxt):
                if on[0]:
                    for o in range(NF):
                        act.wait_ge(xin_ready, u * NF + o + 1)
                        if o == 0 and on[1]:
                            act.wait_ge(xg_done, u)
                        act.activation(xin[:, o, :], bank[2 + o][:], ACT.Identity, bias=v["b_in"][:, o:o + 1])\
                           .then_inc(xin_done, 1)
                    if on[1]:
                        act.wait_ge(h_done, u * NF)
                    for o in range(NF):
                        act.wait_ge(gx_ready, u * NF + o + 1)
                        act.activation(tgx[:, o, :], bank[o][:], ACT.Tanh, bias=v["b_gx"][:, o:o + 1], scale=0.5)\
                           .then_inc(gx_done, 1)
                if on[1]:
                    ffn.act_input(act, u - 1, 1 - c)
                if on[0]:
                    for o in range(NF):
                        act.wait_ge(ga_ready, u * NF + o + 1)
                        act.activation(tga[:, o, :], bank[2 + o][:], ACT.Tanh, bias=v["b_ga"][:, o:o + 1], scale=0.5)\
                           .then_inc(ga_done, 1)
                    act.wait_ge(ga_done, u * NF + NF)
                    for o in range(NF):
                        act.activation(aa[:, o, :], tga[:, o, :], ACT.Exp, bias=decay[:, o:o + 1],
                                       scale=decay[:, o:o + 1]).then_inc(a_done, 1)
                if on[2]:
                    ln3.act_copy(act, u - 2, c, bank[0:2], lt)
                if on[1]:
                    ffn.act_kr(act, u - 1)
                if on[0]:
                    act.wait_ge(z_done, u + 1)
                    act.activation(zz[:], zz[:], ACT.Sqrt).then_inc(sq_done, 1)
                if on[2]:
                    for hi, ready, done, bb, stored, bk in ((qh, q_ready, qh_done, v["bq"], q_stored, bank[0:2]),
                                                            (kh, k_ready, kh_done, v["bk"], k_stored, bank[4:6])):
                        for o in range(NF):
                            act.wait_ge(ready, (u - 2) * NF + o + 1)
                            if o == 0:
                                wait_pos(act, stored, (u - 2) * 32)
                            act.activation(hi[:, o, :], bk[o][:], ACT.Identity, bias=bb[:, o:o + 1]).then_inc(done, 1)
                    act.wait_ge(f_ready, u - 1)
                    wait_pos(act, f_stored, (u - 2) * 64)
                    act.activation(fh[:], bank[6][0:32, :], ACT.Identity, bias=bfar[:]).then_inc(fh_done, 1)
                if nxt >= 1:
                    ln1.act_copy(act, u + 1, 1 - c, bank[2:4], lnt)

            ln1.act_copy(act, 0, 0, bank[2:4], lnt)
            rounds(act, body)

        @block.vector
        def _(dve):
            dve.wait_ge(w_loaded, w_all)
            dve.scalar_tensor_tensor(sp_a[:], v["a_param"][:], -1.0, v["a_param"][:], ALU.mult, ALU.max)\
               .then_inc(sp_step, 1)
            dve.wait_ge(sp_step, 3)
            dve.scalar_tensor_tensor(decay[:], v["a_param"][:], 0.0, sp_c[:], ALU.max, ALU.add).then_inc(sp_step, 1)
            dve.wait_ge(sp_step, 4)
            dve.tensor_scalar(decay[:], decay[:], -4.0, None, ALU.mult).then_inc(decay_set, 1)
            dve.tensor_copy(far_h[:], far32[:]).then_inc(far_split, 1)
            dve.wait_ge(far_split, 1)
            dve.tensor_tensor(far_l[:], far32[:], far_h[:], ALU.subtract).then_inc(far_split, 1)
            ffn.dve_init(dve)

            def split(u, hi, lo, hi_done, lo_done, bb, stored, bk):
                for o in range(NF):
                    dve.wait_ge(hi_done, u * NF + o + 1)
                    if o == 0:
                        wait_pos(dve, stored, u * 32)
                    dve.scalar_tensor_tensor(lo[:, o, :], bk[o][:], bb[:, o:o + 1], hi[:, o, :], ALU.add,
                                             ALU.subtract).then_inc(lo_done, 1)

            def body(u, b, c, on, nxt):
                if on[0]:
                    dve.wait_ge(gx_done, u * NF + NF)
                    dve.wait_ge(xin_done, u * NF + NF)
                    dve.scalar_tensor_tensor(tgx[:], tgx[:], 1.0, xin[:], ALU.add, ALU.mult).then_inc(xg_done, 1)
                if on[1]:
                    ffn.dve_mix(dve, u - 1, b - (1 - c), 1 - c)
                if on[0]:
                    dve.wait_ge(a_done, u * NF + NF)
                    dve.scalar_tensor_tensor(zz[:], aa[:], -1.0, aa[:], ALU.mult, ALU.mult).then_inc(a2_done, 1)
                    dve.wait_ge(a2_done, u + 1)
                    dve.tensor_scalar(zz[:], zz[:], 1.0, 0.0, ALU.add, ALU.max).then_inc(z_done, 1)
                if nxt >= 1:
                    dve.wait_ge(x_loaded[1 - c], (b + c) * 16 + 16)
                    ln1.dve_stats(dve, u + 1, 1 - c, xl[1 - c])
                if on[2]:
                    split(u - 2, qh, ql, qh_done, ql_done, v["bq"], q_stored, bank[0:2])
                if on[1]:
                    ffn.dve_out(dve, u - 1, xb[1 - c])
                    ln3.dve_stats(dve, u - 1, 1 - c, xb[1 - c])
                if on[0]:
                    dve.wait_ge(sq_done, u + 1)
                    dve.wait_ge(xg_done, u + 1)
                    dve.scalar_tensor_tensor(tgx[:], zz[:], 0.5, tgx[:], ALU.mult, ALU.mult).then_inc(u_done, 1)
                    dve.wait_ge(u_done, u + 1)
                    if on[1]:
                        dve.wait_ge(h_done, u * NF)
                    for f in range(NF):
                        start = 0.0 if c == 0 else hh[0][:, f, CH - 1:CH]
                        dve.tensor_tensor_scan(hh[c][:, f, :], aa[:, f, :], tgx[:, f, :], start, ALU.mult, ALU.add)\
                           .then_inc(h_done, 1)
                if nxt >= 1:
                    ln1.dve_apply(dve, u + 1, 1 - c, xl[1 - c])
                if on[2]:
                    split(u - 2, kh, kl, kh_done, kl_done, v["bk"], k_stored, bank[4:6])
                if on[1]:
                    ln3.dve_apply(dve, u - 1, 1 - c, xb[1 - c])
                if on[2]:
                    dve.wait_ge(fh_done, u - 1)
                    wait_pos(dve, f_stored, (u - 2) * 64)
                    dve.scalar_tensor_tensor(fl[:], bank[6][0:32, :], bfar[:], fh[:], ALU.add, ALU.subtract)\
                       .then_inc(fl_done, 1)
                    wait_pos(dve, v_stored, (u - 2) * NT * 16)
                    for h in range(2):
                        dve.wait_ge(vv_ready, (u - 2) * 2 + h + 1)
                        for t in range(2):
                            ins = dve.tensor_tensor(vp[:, 2 * h + t, :, 0:HD],
                                              bank[(7, 4)[h]][:, t * D:(t + 1) * D].rearrange("p (h d) -> p h d", d=HD),
                                              bv[:].rearrange("p (h d) -> p h d", d=HD), ALU.add)
                        ins.then_inc(vv_done, 1)
                if on[0]:
                    for h in range(2):
                        dve.wait_ge(y_ready, u * 2 + h + 1)
                        dve.wait_ge(bias_added, u + 1)
                        dve.tensor_tensor(xb[c][:, 2 * h:2 * h + 2, :],
                                          bank[h][:].rearrange("p (t d) -> p t d", t=2),
                                          xb[c][:, 2 * h:2 * h + 2, :], ALU.add).then_inc(x1_done, 1)
                    dve.wait_ge(x1_done, u * 2 + 2)
                    ffn.ln.dve_stats(dve, u, c, xb[c])
                    ffn.ln.dve_apply(dve, u, c, xb[c])

            dve.wait_ge(consts_set, 4)
            dve.wait_ge(x_loaded[0], 16)
            ln1.dve_stats(dve, 0, 0, xl[0])
            ln1.dve_apply(dve, 0, 0, xl[0])
            rounds(dve, body)

        @block.tensor
        def _(pe):
            pe.wait_ge(w_loaded, w_all)
            pe.wait_ge(scaled, 4)
            pe.wait_ge(far_split, 2)

            def gate(src, wt, banks, ready, u, free):
                for o in range(NF):
                    free(o)
                    for f in range(NF):
                        mm = pe.matmul(banks[o][:], wt[:, f, o * P:(o + 1) * P], src[:, f, :],
                                       start=(f == 0), stop=(f == NF - 1))
                    mm.then_inc(ready, 1)

            def body(u, b, c, on, nxt):
                if on[0]:
                    pe.wait_ge(ln1.tr_copied, u * NF + NF)
                    gate(lnt, w["W_in"], bank[2:4], xin_ready, u, lambda o: None)
                    pe.wait_ge(xin_done, u * NF + NF)
                    gate(xin, w["W_gx"], bank[0:2], gx_ready, u,
                         lambda o: pe.wait_ge(x1_done, (u - 1) * 2 + o + 1) if on[1] else None)
                if on[1]:
                    def free_tr(f):
                        if not isinstance(u, int) or u > 2:
                            pe.wait_ge(*((vv_done, (u - 3) * 2 + 2), (kl_done, (u - 3) * NF + NF))[f])
                    ffn.ln.pe_transpose(pe, u - 1, 1 - c, bank[4:6], ident, free_tr)
                if on[0]:
                    gate(xin, w["W_ga"], bank[2:4], ga_ready, u, lambda o: None)
                if on[2]:
                    u2 = u - 2

                    def free_t3(f):
                        if on[0]:
                            pe.wait_ge(gx_done, u * NF + f + 1)
                        elif on[1]:
                            pe.wait_ge(x1_done, (u - 1) * 2 + f + 1)
                        else:
                            pe.wait_ge(ql_done, u2 * NF)
                    ln3.pe_transpose(pe, u2, c, bank[0:2], ident, free_t3)
                if on[1]:
                    def free_r(h):
                        if not isinstance(u, int) or u > 2:
                            pe.wait_ge(*((fl_done, u - 2), (vv_done, (u - 3) * 2 + 1))[h])
                        elif u == 2:
                            pe.wait_ge(ffn.rv_done, h + 1)
                    ffn.pe_kr(pe, u - 1, lambda o: pe.wait_ge(ffn.ln.tr_copied, (u - 1) * NF + o + 1), free_r)
                if on[2]:
                    pe.wait_ge(ln3.tr_copied, u2 * NF + NF)
                    gate(lt, w["Wq"], bank[0:2], q_ready, u2, lambda o: None)
                if on[1]:
                    ffn.pe_v(pe, u - 1, lambda h: pe.wait_ge(ffn.r_done, (u - 1) * 2 + h + 1))
                if on[2]:
                    gate(lt, w["Wk"], bank[4:6], k_ready, u2,
                         lambda o: pe.wait_ge(ffn.k_done, (u - 1) * NF + o + 1) if on[1] else
                         pe.wait_ge(*((vv_done, u2 * 2), (kl_done, u2 * NF))[o]))
                    pe.wait_ge(ql_done, u2 * NF + NF)
                    pe.wait_ge(*((ffn.rv_done, (u - 1) * 2 + 1) if on[1] else (fl_done, u2)))
                    for f in range(NF):
                        for qq in (qh, ql):
                            for ff in (far_h, far_l):
                                mm = pe.matmul(bank[6][0:32, :], ff[:, f, :], qq[:, f, :],
                                               start=(f == 0 and qq is qh and ff is far_h),
                                               stop=(f == NF - 1 and qq is ql and ff is far_l))
                    mm.then_inc(f_ready, 1)
                    for h in range(2):
                        bk = bank[(7, 4)[h]]
                        if h == 1:
                            pe.wait_ge(kl_done, u2 * NF + 1)
                        else:
                            pe.wait_ge(*((ffn.rv_done, (u - 1) * 2 + 2) if on[1] else (vv_done, u2 * 2 - 1)))
                        for t in (2 * h, 2 * h + 1):
                            for f in range(NF):
                                mm = pe.matmul(bk[:, (t % 2) * D:(t % 2 + 1) * D], lt[:, f, t * P:(t + 1) * P],
                                               w["Wv"][:, f, :], start=(f == 0), stop=(f == NF - 1))
                        mm.then_inc(vv_ready, 1)
                if nxt >= 1:
                    ln1.pe_transpose(pe, u + 1, 1 - c, bank[2:4], ident,
                                     lambda f: pe.wait_ge(ga_done, u * NF + f + 1))
                if on[0]:
                    pe.wait_ge(h_done, u * NF + NF)
                    if not on[2]:
                        pe.wait_ge(gx_done, u * NF + NF)
                    for h in range(2):
                        for t in (2 * h, 2 * h + 1):
                            for f in range(NF):
                                mm = pe.matmul(bank[h][:, (t % 2) * D:(t % 2 + 1) * D],
                                               hh[c][:, f, t * P:(t + 1) * P], w["W_out"][:, f, :],
                                               start=(f == 0), stop=(f == NF - 1))
                        mm.then_inc(y_ready, 1)

            ln1.pe_transpose(pe, 0, 0, bank[2:4], ident, lambda f: None)
            rounds(pe, body)


def wait_pos(eng, sem, value):
    if not isinstance(value, int) or value > 0:
        eng.wait_ge(sem, value)


BAND, LEFT, RIGHT = range(3)


def variants(i, j0, j1):
    runs = ((LEFT, j0, min(j1, i - 1)), (BAND, max(j0, i - 1), min(j1, i + 2)), (RIGHT, max(j0, i + 2), j1))
    return [(v, a, b) for v, a, b in runs if a < b]


def attend(nc, a, scr, nb):
    npairs = nb * NPR
    LOOPS = (npairs - 2) // 3
    with ExitStack() as ctx:
        m = Pool(nc, ctx)
        st_bank = [m.ps(f"at_st{i}", [P, CH]) for i in range(3)]
        mx_bank = [m.ps(f"at_mx{i}", [P, CH]) for i in range(2)]
        tab_bank = [m.ps(f"at_tab_bank{i}", [P, TW]) for i in range(2)]
        o_bank = m.ps("at_o", [P, CH])

        qs = [m.sb(f"at_q{i}", [P, HP, S], F16) for i in range(3)]
        ks = [m.sb(f"at_k{i}", [P, 3, HP, S], F16) for i in range(3)]
        vs = [m.sb(f"at_v{i}", [P, NTI, HP * VW]) for i in range(3)]
        pos = [m.sb(f"at_pos{i}", [P, NQ, 2, NT, WW], F16) for i in range(3)]
        tab = [m.sb(f"at_tab{i}", [P, 2, NT, TW], F16) for i in range(NQ)]
        tab32 = [m.sb(f"at_tab32_{i}", [P, TW]) for i in range(2)]
        pt = [m.sb(f"at_p{i}", [P, 2, CH]) for i in range(4)]
        os_ = m.sb("at_os", [P, CH])
        rden = m.sb("at_rden", [P, NT, HP])
        att = [m.sb(f"at_att{i}", [P, NT, HP * HD]) for i in range(2)]
        mx = [m.sb(f"at_mx_sb{i}", [P, 2, HP * NT]) for i in range(2)]
        mtop = m.sb("at_mtop", [P, HP * NT])
        mneg = [m.sb(f"at_mneg{i}", [P, HP * NT], F16) for i in range(2)]
        mrow = [m.sb(f"at_mrow{i}", [HP * NT, P], F16) for i in range(2)]
        w32 = m.sb("at_w32", [P, TW])
        w_hi = m.sb("at_w_hi", [P, TW], F16)
        w_lo = m.sb("at_w_lo", [P, TW], F16)
        wt = m.sb("at_wt", [P, TW], F16)
        sel = m.sb("at_sel", [P, 3])
        ident = m.sb("at_ident", [P, P])
        ident_h = m.sb("at_ident_h", [P, P], F16)
        one = m.sb("at_one", [P, 1])
        pick = m.sb("at_pick", [P, HP * (HD + 1)])

        (c_loaded, one_set, c_set, wt_split, wt_loaded, tab_ready, tab_taken, tab_lo, tab_hi_pool, tab_lo_pool, mx_ready, mx_done, mtop_done, mneg_done,
         mrow_ready, mrow_copied, st_ready, exp_done, av_done, o_copied, out_ready, rden_done, att_done) = m.sems(
             "c_loaded one_set c_set wt_split wt_loaded tab_ready tab_taken tab_lo tab_hi_pool tab_lo_pool mx_ready mx_done mtop_done mneg_done "
             "mrow_ready mrow_copied st_ready exp_done av_done o_copied out_ready rden_done att_done")
        q_loaded, k_loaded, v_loaded = [m.sems(" ".join(f"{n}_loaded{i}" for i in range(3))) for n in "qkv"]
        mrow_loaded, att_stored = [m.sems(f"{n}0 {n}1") for n in ("mrow_loaded", "att_stored")]
        tab_written, pos_loaded = [m.sems(" ".join(f"{n}{c}" for c in range(NQ))) for n in ("tab_written", "pos_loaded")]
        def st_of(j, k, jj):
            return (j * 32 + 2 * k + jj) % 3

        def table_of(n, k):
            return (n + 2, k - TLAG) if k >= TLAG else (n + 1, 16 - TLAG + k)

        def turns(eng, body):
            def at(n):
                body(n, n % 3, lambda k: (n + k) // 3,
                     dict(prev=1 <= n <= npairs, now=0 <= n < npairs, nxt=0 <= n + 1 < npairs, far=n + 2 < npairs))

            for n in range(-2, 3):
                at(n)
            if LOOPS > 1:
                with eng.Fori(1, LOOPS) as it:
                    for j in range(3):
                        body(it * 3 + j, j, lambda k, j=j: it + (j + k) // 3,
                             dict(prev=True, now=True, nxt=True, far=True))
            for n in range(max(3 * LOOPS, 3), npairs + 1):
                at(n)

        block = ctx.enter_context(nc.Block())

        @block.sync
        def _(sp):
            for dst, src in ((ident[:], a["ident"]), (pick[:], a["pick"]), (sel[R_ONE:R_MAX + 1, :], a["sel"]),
                             (w32[R_ONE:R_ONE + 2, :], a["br_pad"].unsqueeze(0).to_broadcast([2, TW]))):
                sp.dma_start(dst, src).then_inc(c_loaded, 16)
            for r in range(4):
                sp.dma_start(w32[r * HD:(r + 1) * HD, :], a["wr_pad"]).then_inc(c_loaded, 16)
            sp.wait_ge(wt_split, 2)
            for lo, r0, r1 in ((0, 0, 32), (1, 32, 64), (0, 64, 65), (1, 65, 66)):
                sp.dma_start(wt[r0:r1, :], (w_hi, w_lo)[lo][r0:r1, :]).then_inc(wt_loaded, 16)

            def load_q(n, slot):
                part, row = nb * D * S, HP * S
                for rep in range(2):
                    sp.dma_start(qs[slot][rep * 2 * HD:(rep + 1) * 2 * HD].rearrange("p h s -> p (h s)"),
                                 dram(scr["q"], n * (HD * row), [[part, 2], [row, HD], [1, row]]))\
                      .then_inc(q_loaded[slot], 16)
                sp.dma_start(qs[slot][R_FAR:R_FAR + 4].rearrange("p h s -> p (h s)"),
                             dram(scr["far"], n * row, [[nb * HEADS * S, 4], [1, row]])).then_inc(q_loaded[slot], 16)

            def load_k(n, slot):
                part, row = nb * D * S, HP * S
                for rep in range(2):
                    for v in range(3):
                        sp.dma_start(ks[slot][rep * 2 * HD:(rep + 1) * 2 * HD, v].rearrange("p h s -> p (h s)"),
                                     dram(scr["k"], n * (HD * row) + rep * part, [[0, 2], [row, HD], [1, row]]))\
                          .then_inc(k_loaded[slot], 16)

            def load_v(n, slot):
                sp.dma_start(vs[slot][:], dram(scr["v"], n * (S * HP * VW),
                                               [[HP * VW, P], [P * HP * VW, NTI], [1, HP * VW]]))\
                  .then_inc(v_loaded[slot], 16)

            def write_tables(n, c):
                for done in (tab_lo, tab_lo_pool):
                    sp.wait_ge(done, n * 8 + (NT * c + NT) // 2)
                sp.dma_start(dram(scr["tab"], c * 2 * NT * P * TW, [[TW, P], [P * TW, 2 * NT], [1, TW]]),
                             tab[c][:].rearrange("p x t w -> p (x t) w")).then_inc(tab_written[c], 16)

            def read_windows(n, slot, c):
                sp.wait_ge(tab_written[c], n * 16 + 16)
                sp.dma_start(pos[slot][:, c].rearrange("p x t w -> p (x t) w"),
                             dram(scr["tab"], c * 2 * NT * P * TW + P - 1,
                                  [[TW - 1, P], [P * TW, 2 * NT], [1, WW]])).then_inc(pos_loaded[c], 16)

            def load_mrow(n, slot, h):
                sp.wait_ge(mrow_copied, n * 2 + h + 1)
                for hh in range(HP):
                    sp.dma_start(qs[slot][R_MAX:R_MAX + 1, hh, h * CH:(h + 1) * CH],
                                 mrow[h][hh * NT:(hh + 1) * NT, :]).then_inc(mrow_loaded[h], 16)

            def body(n, j, gen, on):
                if on["nxt"]:
                    write_tables(n + 1, 2)
                if on["far"]:
                    if on["prev"]:
                        sp.wait_ge(st_ready, n * 32)
                    load_q(n + 2, (j + 2) % 3)
                if on["now"]:
                    load_mrow(n, j % 3, 1)
                if on["far"]:
                    load_k(n + 2, (j + 2) % 3)
                    if on["prev"]:
                        sp.wait_ge(av_done, n * 8)
                    load_v(n + 2, (j + 2) % 3)
                if on["nxt"]:
                    read_windows(n + 1, (j + 1) % 3, 2)
                if on["nxt"]:
                    write_tables(n + 1, 3)
                    read_windows(n + 1, (j + 1) % 3, 3)
                if on["far"]:
                    write_tables(n + 2, 0)
                if on["nxt"]:
                    load_mrow(n + 1, (j + 1) % 3, 0)
                if on["far"]:
                    read_windows(n + 2, (j + 2) % 3, 0)
                if on["far"]:
                    write_tables(n + 2, 1)
                    read_windows(n + 2, (j + 2) % 3, 1)

            turns(sp, body)

        @block.gpsimd
        def _(pool):
            def store(n, h):
                pool.wait_ge(att_done, n * 2 + h + 1)
                pool.dma_start(dram(scr["att"], n * (S * HP * HD) + h * (CH * HP * HD),
                                  [[HP * HD, P], [P * HP * HD, NT], [1, HP * HD]]), att[h][:])\
                  .then_inc(att_stored[h], 16)

            pool.memset(one[:], 1.0).then_inc(one_set, 1)
            pool.wait_ge(one_set, 1)

            def body(n, j, gen, on):
                for k in range(16):
                    p, i = table_of(n, k)
                    if i % 2 == 1 and on["far" if k >= TLAG else "nxt"]:
                        part, src = tab[i // NT][:, :, i % NT, :], tab32[(i // 2) % 2]
                        pool.wait_ge(tab_taken, p * 16 + i + 1)
                        pool.tensor_tensor(part[:, 0], src[:], one[:].to_broadcast([P, TW]), ALU.mult)\
                            .then_inc(tab_hi_pool, 1)
                        pool.wait_ge(tab_hi_pool, p * 8 + i // 2 + 1)
                        pool.tensor_tensor(part[:, 1], src[:], part[:, 0], ALU.subtract).then_inc(tab_lo_pool, 1)
                    if k == 3 and on["prev"]:
                        store(n - 1, 1)
                    if k == 11 and on["now"]:
                        store(n, 0)

            turns(pool, body)
            for h in range(2):
                pool.wait_ge(att_stored[h], 16 * npairs)

        @block.scalar
        def _(act):
            def copy_o(n, h):
                act.wait_ge(av_done, n * 8 + 4 * h + 4)
                wait_pos(act, out_ready, n * 2 + h)
                act.activation(os_[:], o_bank[:], ACT.Identity).then_inc(o_copied, 1)

            def exp(n, j, k, jj):
                act.wait_ge(st_ready, n * 32 + 2 * k + jj + 1)
                if jj == 0:
                    wait_pos(act, av_done, n * 8 + k // 2 - 1)
                act.activation(pt[k % 4][:, jj, :], st_bank[st_of(j, k, jj)][:], ACT.Exp).then_inc(exp_done, 1)

            def body(n, j, gen, on):
                for k in range(16):
                    if k == 2 and on["prev"]:
                        copy_o(n - 1, 1)
                    if k == 10 and on["now"]:
                        copy_o(n, 0)
                    if on["now"]:
                        exp(n, j, k, 0)
                    if on["far" if k >= TLAG else "nxt"]:
                        p, i = table_of(n, k)
                        act.wait_ge(tab_ready, p * 16 + i + 1)
                        if i % NT == 0:
                            wait_pos(act, tab_written[i // NT], p * 16)
                        if i % 2 == 0:
                            dst = tab[i // NT][:, 0, i % NT, :]
                        else:
                            dst = tab32[(i // 2) % 2][:]
                            wait_pos(act, tab_lo_pool, p * 8 + i // 2 - 1)
                        act.activation(dst, tab_bank[i % 2][:], ACT.Identity).then_inc(tab_taken, 1)
                    if on["now"]:
                        exp(n, j, k, 1)

            turns(act, body)

        @block.vector
        def _(dve):
            for s in range(3):
                dve.memset(qs[s][R_ONE:R_FAR, :, :], 1.0).then_inc(c_set, 1)
            dve.wait_ge(c_loaded, 8 * 16)
            for s in range(3):
                for v in range(3):
                    dve.tensor_copy(ks[s][R_ONE:R_MAX + 1, v, :, :].rearrange("p h s -> p (h s)"),
                                    sel[R_ONE:R_MAX + 1, v:v + 1].to_broadcast([R_MAX + 1 - R_ONE, HP * S]))\
                       .then_inc(c_set, 1)
            dve.tensor_copy(ident_h[:], ident[:]).then_inc(c_set, 1)
            dve.tensor_copy(w_hi[0:K_TAB, :], w32[0:K_TAB, :]).then_inc(wt_split, 1)
            dve.wait_ge(wt_split, 1)
            dve.tensor_tensor(w_lo[0:K_TAB, :], w32[0:K_TAB, :], w_hi[0:K_TAB, :], ALU.subtract).then_inc(wt_split, 1)

            def negate(n, h):
                dve.wait_ge(mx_done, n * 32 + 16 * h + 16)
                dve.tensor_tensor(mtop[:], mx[h][:, 0, :], mx[h][:, 1, :], ALU.max).then_inc(mtop_done, 1)
                dve.wait_ge(mtop_done, n * 2 + h + 1)
                dve.tensor_scalar(mneg[h][:], mtop[:], -1.0, None, ALU.mult).then_inc(mneg_done, 1)

            def copy_mrow(n, h):
                dve.wait_ge(mrow_ready, n * 2 + h + 1)
                wait_pos(dve, mrow_loaded[h], n * 32)
                dve.tensor_copy(mrow[h][:], mx_bank[0][0:HP * NT, 0:P]).then_inc(mrow_copied, 1)

            def normalise(n, h):
                dve.wait_ge(out_ready, n * 2 + h + 1)
                out = o_bank[:, 0:NT * HP * (HD + 1)].rearrange("p (t h v) -> p t h v", t=NT, h=HP)
                dve.reciprocal(rden[:].unsqueeze(3), out[:, :, :, HD:HD + 1]).then_inc(rden_done, 1)
                dve.wait_ge(rden_done, n * 2 + h + 1)
                wait_pos(dve, att_stored[h], n * 16)
                dve.tensor_tensor(att[h][:].rearrange("p t (h v) -> p t h v", h=HP), out[:, :, :, 0:HD],
                                  rden[:].unsqueeze(3).to_broadcast([P, NT, HP, HD]), ALU.mult).then_inc(att_done, 1)

            def body(n, j, gen, on):
                for k in range(16):
                    if k == 0 and on["now"]:
                        negate(n, 1)
                    if k == 2 and on["now"]:
                        copy_mrow(n, 1)
                    if k == 8 and on["nxt"]:
                        negate(n + 1, 0)
                    if k == 10 and on["nxt"]:
                        copy_mrow(n + 1, 0)
                    if on["nxt"]:
                        for kh in range(2):
                            dve.wait_ge(mx_ready, (n + 1) * 32 + 2 * k + kh + 1)
                            dve.tensor_reduce(mx[k // 8][:, kh, k % 8:k % 8 + 1], mx_bank[kh][:], AX_X, ALU.max)\
                               .then_inc(mx_done, 1)
                    p, i = table_of(n, k)
                    if i % 2 == 0 and on["far" if k >= TLAG else "nxt"]:
                        part = tab[i // NT][:, :, i % NT, :]
                        dve.wait_ge(tab_taken, p * 16 + i + 1)
                        dve.tensor_tensor(part[:, 1], tab_bank[0][:], part[:, 0], ALU.subtract).then_inc(tab_lo, 1)
                    if k == 2 and on["prev"]:
                        normalise(n - 1, 1)
                    if k == 10 and on["now"]:
                        normalise(n, 0)

            turns(dve, body)

        @block.tensor
        def _(pe):
            pe.wait_ge(c_loaded, 8 * 16)
            pe.wait_ge(c_set, 3 + 9 + 1)
            pe.wait_ge(wt_loaded, 4 * 16)

            def scores(n, slot, k, jj):
                h, jt, hh = k // 8, 2 * ((k % 8) // 2) + jj, k % 2
                if k % 8 == 0 and jj == 0:
                    pe.wait_ge(mrow_loaded[h], n * 32 + 32)
                wait_pos(pe, exp_done, n * 32 + 2 * k + jj - 2)
                out = st_bank[st_of(slot, k, jj)]
                tiles = range(h * NT, (h + 1) * NT)
                runs = [(v, [i for i in tiles if test(i - jt)]) for v, test in
                        ((RIGHT, lambda x: x <= -2), (BAND, lambda x: abs(x) <= 1), (LEFT, lambda x: x >= 2))]
                runs = [(v, r) for v, r in runs if r]
                near = [i for v, r in runs if v == BAND for i in r]
                for at, (v, r) in enumerate(runs):
                    mm = pe.matmul(out[:, (r[0] - h * NT) * P:(r[-1] + 1 - h * NT) * P],
                                   ks[slot][0:K_SC, v, hh, jt * P:(jt + 1) * P],
                                   qs[slot][0:K_SC, hh, r[0] * P:(r[-1] + 1) * P],
                                   start=(at == 0), stop=(v != BAND), skip_group_check=True)
                for i in near:
                    w0 = (jt - i + 1) * P
                    for x in range(2):
                        mm = pe.matmul(out[:, (i - h * NT) * P:(i + 1 - h * NT) * P],
                                       pos[slot][:, 2 * h + hh, x, i - h * NT, w0:w0 + P], ident_h[:],
                                       start=False, stop=(x == 1), skip_group_check=True)
                mm.then_inc(st_ready, 1)

            def maxima(n, slot, k, kh, gen):
                h, hh, i = k // 8, (k % 8) // NT, (k // 8) * NT + k % NT
                if k == 0 and kh == 0:
                    pe.wait_ge(k_loaded[slot], (gen + 1) * 6 * 16)
                if k % NT == 0 and kh == 0:
                    pe.wait_ge(pos_loaded[k // NT], (n + 1) * 16)
                wait_pos(pe, mx_done, n * 32 + 2 * k + kh - 1)
                out = mx_bank[kh]
                j0 = kh * NT
                runs = variants(i, j0, j0 + NT)
                for at, (v, ja, jb) in enumerate(runs):
                    mm = pe.matmul(out[:, (ja - j0) * P:(jb - j0) * P], qs[slot][0:K_MAXP, hh, i * P:(i + 1) * P],
                                   ks[slot][0:K_MAXP, v, hh, ja * P:jb * P], start=(at == 0), stop=(v != BAND),
                                   skip_group_check=True)
                for v, ja, jb in runs:
                    if v == BAND:
                        mm = pe.matmul(out[:, (ja - j0) * P:(jb - j0) * P], ident_h[:],
                                       pos[slot][:, k // NT, 0, k % NT, (ja - i + 1) * P:(jb - i + 1) * P],
                                       start=False, stop=True, skip_group_check=True)
                mm.then_inc(mx_ready, 1)

            def table(n, slot, i, gen):
                h, hh, t = i // 8, (i % 8) // NT, (i // 8) * NT + i % NT
                if i == 0:
                    pe.wait_ge(q_loaded[slot], (gen + 1) * 3 * 16)
                if i % 2 == 0:
                    wait_pos(pe, tab_lo, n * 8 + i // 2)
                else:
                    wait_pos(pe, tab_taken, n * 16 + i - 1)
                pe.matmul(tab_bank[i % 2][:], qs[slot][0:K_TAB, hh, t * P:(t + 1) * P], wt[0:K_TAB, :], start=True, stop=True)\
                  .then_inc(tab_ready, 1)

            def turn_maxima(n, h, done):
                pe.wait_ge(mneg_done, n * 2 + h + 1)
                if done is not None:
                    pe.wait_ge(mx_done, done)
                pe.matmul(mx_bank[0][0:HP * NT, 0:P], mneg[h][:], ident_h[:], start=True, stop=True).then_inc(mrow_ready, 1)

            def values(n, slot, g, gen):
                h, jp = g // 4, g % 4
                if g == 0:
                    pe.wait_ge(v_loaded[slot], (gen + 1) * 16)
                if jp == 0:
                    wait_pos(pe, att_done, n * 2 + h)
                pe.wait_ge(exp_done, n * 32 + 4 * g + 4)
                for hh in range(HP):
                    for jj in range(2):
                        r0 = (2 * hh + jj) * VW
                        mm = pe.matmul(o_bank[r0:r0 + VW, :], vs[slot][:, 2 * jp + jj, hh * VW:(hh + 1) * VW],
                                       pt[(2 * g + hh) % 4][:, jj, :], start=(jp == 0), stop=(jp == 3),
                                       skip_group_check=True)
                mm.then_inc(av_done, 1)

            def outputs(n, h):
                pe.wait_ge(o_copied, n * 2 + h + 1)
                w = HP * (HD + 1)
                for t in range(NT):
                    mm = pe.matmul(o_bank[:, t * w:(t + 1) * w], os_[:, t * P:(t + 1) * P], pick[:],
                                   start=True, stop=True)
                mm.then_inc(out_ready, 1)

            def body(n, j, gen, on):
                for k in range(16):
                    if k == 2 and on["now"]:
                        turn_maxima(n, 1, (n + 1) * 32 + 3 if on["nxt"] else None)
                    if k == 10 and on["nxt"]:
                        turn_maxima(n + 1, 0, (n + 1) * 32 + 19)
                    if on["now"]:
                        scores(n, j % 3, k, 0)
                    if on["nxt"]:
                        if k == 2 and on["now"]:
                            pe.wait_ge(mrow_copied, n * 2 + 2)
                        if k == 10:
                            pe.wait_ge(mrow_copied, n * 2 + 3)
                        maxima(n + 1, (j + 1) % 3, k, 0, gen(1))
                    if on["far" if k >= TLAG else "nxt"]:
                        p, i = table_of(n, k)
                        ahead = 2 if k >= TLAG else 1
                        table(p, (j + ahead) % 3, i, gen(ahead))
                    if on["now"]:
                        scores(n, j % 3, k, 1)
                    if on["nxt"]:
                        maxima(n + 1, (j + 1) % 3, k, 1, gen(1))
                    if k == 2 and on["prev"]:
                        outputs(n - 1, 1)
                    if k == 10 and on["now"]:
                        outputs(n, 0)
                    if k == 1 and on["prev"]:
                        values(n - 1, (j - 1) % 3, 7, gen(-1))
                    if k % 2 == 1 and k > 1 and on["now"]:
                        values(n, j % 3, (k - 3) // 2, gen(0))

            turns(pe, body)


def finish(nc, a, scr, nb):
    with ExitStack() as ctx:
        m = Pool(nc, ctx)
        bank = [m.ps(f"fi_bank{i}", [P, CH]) for i in range(6)]
        w_names = ["ffn_wr", "ffn_wk", "ffn_wv"]
        w = {n: m.sb(f"fi_{n}", [P, NF, D]) for n in w_names}
        v = {n: m.sb(f"fi_{n}", [P, NF]) for n in ("mu_r", "mu_k")}
        ident = m.sb("fi_ident", [P, P])
        eps = m.sb("fi_eps", [P, NT])
        minus_half = m.sb("fi_minus_half", [P, NT])
        xl = [m.sb(f"fi_xl{c}", [P, NT, D]) for c in range(2)]
        at = [m.sb(f"fi_at{c}", [P, NT, D]) for c in range(2)]
        xb = [m.sb(f"fi_xb{i}", [P, NT, D]) for i in range(4)]
        ffn = Ffn(m, "f2", bank[0:4], bank[4:6], {"wr": w["ffn_wr"], "wk": w["ffn_wk"], "wv": w["ffn_wv"], **v})
        w_loaded, consts_set, x3_done = m.sems("f2_w_loaded f2_consts_set x3_done")
        x_loaded = m.sems("x2_loaded0 x2_loaded1")
        out_stored = m.sems(" ".join(f"out_stored{i}" for i in range(4)))
        loads = [(w[n], rows(a[n])) for n in w_names] + [(v[n], a[n]) for n in v] + [(ident, a["ident"])]
        w_all = 16 * len(loads)
        nu = nb * NC

        def rounds(eng, body):
            def at(u):
                body(u, u // 2, u % 2, u % 4, lambda d: (u + d) // 4, (u < nu, u > 0), nu - 1 - u)

            for u in range(min(6, nu - 2)):
                at(u)
            if nb > 4:
                with eng.Fori(1, (nb - 2) // 2) as it:
                    for k in range(2, 6):
                        body(it * 4 + k, it * 2 + k // 2, k % 2, k % 4, lambda d, k=k: it + (k + d) // 4,
                             (True, True), 2)
            for u in range(nu - 2, nu + 1):
                at(u)

        block = ctx.enter_context(nc.Block())

        @block.sync
        def _(sp):
            for dst, src in loads:
                sp.dma_start(dst[:], src).then_inc(w_loaded, 16)

            def load_x(b, c):
                tok = slice(c * CH, (c + 1) * CH)
                sp.dma_start(xl[c][:], scr["x2"][b, tok, :].rearrange("(t p) d -> p t d", p=P))\
                  .then_inc(x_loaded[c], 16)
                for t in range(NT):
                    r = c * CH + t * P
                    sp.dma_start(at[c][:, t, :].rearrange("p (r v) -> p r v", r=NPR),
                                 scr["att"][b, :, r:r + P, :].rearrange("r p v -> p r v")).then_inc(x_loaded[c], 16)

            load_x(0, 0)
            load_x(0, 1)

            def body(u, b, c, s, gen, on, nxt):
                if nxt >= 2:
                    sp.wait_ge(x3_done, u + 1)
                    load_x(b + 1, c)
                if on[1]:
                    c1, b1 = 1 - c, b - (1 - c)
                    sp.wait_ge(ffn.x_done, u)
                    sp.dma_start(a["out"][b1, c1 * CH:(c1 + 1) * CH, :].rearrange("(t p) d -> p t d", p=P),
                                 xb[(s - 1) % 4][:]).then_inc(out_stored[(s - 1) % 4], 16)

            rounds(sp, body)
            for sem in out_stored:
                sp.wait_ge(sem, 16 * (nu // 4))

        @block.gpsimd
        def _(pool):
            pool.memset(minus_half[:], -0.5).then_inc(consts_set, 1)
            pool.memset(eps[:], EPS).then_inc(consts_set, 1)
            pool.wait_ge(consts_set, 2)
            ffn.ln.pool_rstd(pool, 0, 0, eps, minus_half)
            ffn.ln.pool_rstd(pool, 1, 1, eps, minus_half)

            def body(u, b, c, s, gen, on, nxt):
                if on[0]:
                    ffn.pool_square(pool, u)
                if nxt >= 2:
                    ffn.ln.pool_rstd(pool, u + 2, c, eps, minus_half)

            rounds(pool, body)

        @block.scalar
        def _(act):
            def body(u, b, c, s, gen, on, nxt):
                if on[0]:
                    ffn.act_input(act, u, c)
                    ffn.act_kr(act, u, (u * 2) if on[1] else None)

            rounds(act, body)

        @block.vector
        def _(dve):
            dve.wait_ge(w_loaded, w_all)
            ffn.dve_init(dve)

            def x3_of(u, b, c, s, gen):
                dve.wait_ge(x_loaded[c], b * 80 + 80)
                wait_pos(dve, out_stored[s], gen * 16)
                dve.tensor_tensor(xb[s][:], xl[c][:], at[c][:], ALU.add).then_inc(x3_done, 1)
                dve.wait_ge(x3_done, u + 1)
                ffn.ln.dve_stats(dve, u, c, xb[s])

            x3_of(0, 0, 0, 0, 0)
            x3_of(1, 0, 1, 1, 0)
            ffn.ln.dve_apply(dve, 0, 0, xb[0])

            def body(u, b, c, s, gen, on, nxt):
                if on[0]:
                    ffn.dve_mix(dve, u, b, c)
                if on[1]:
                    ffn.dve_out(dve, u - 1, xb[(s - 1) % 4])
                if nxt >= 1:
                    ffn.ln.dve_apply(dve, u + 1, 1 - c, xb[(s + 1) % 4])
                if nxt >= 2:
                    x3_of(u + 2, b + 1, c, (s + 2) % 4, gen(2))

            rounds(dve, body)

        @block.tensor
        def _(pe):
            pe.wait_ge(w_loaded, w_all)

            def body(u, b, c, s, gen, on, nxt):
                if on[0]:
                    ffn.ln.pe_transpose(pe, u, c, bank[0:2], ident,
                                        lambda f: pe.wait_ge(ffn.k_done, (u - 1) * NF + f + 1) if on[1] else None)
                if on[1]:
                    ffn.pe_v(pe, u - 1, lambda h: wait_pos(pe, ffn.rv_done, (u - 2) * 2 + h + 1))
                if on[0]:
                    def free_r(h):
                        if on[1]:
                            pe.wait_ge(ffn.r_done, (u - 1) * 2 + h + 1)
                    ffn.pe_kr(pe, u, lambda o: pe.wait_ge(ffn.ln.tr_copied, u * NF + o + 1), free_r)

            rounds(pe, body)


def hybrid_kernel(nc, a, out):
    nb = a["x"].shape[0]
    a = dict(a, out=out)

    def scratch(name, shape, dt=F32):
        return nc.dram_tensor(name, shape, dt).ap()

    scr = {
        "x2": scratch("scr_x2", [nb, S, D]),
        "q": scratch("scr_q", [2, nb, D, S], F16),
        "k": scratch("scr_k", [2, nb, D, S], F16),
        "far": scratch("scr_far", [2, 2, nb, HEADS, S], F16),
        "v": scratch("scr_v", [nb, NPR, S, HP * VW]),
        "tab": scratch("scr_tab", [NQ, 2, NT * P, TW], F16),
        "att": scratch("scr_att", [nb, NPR, S, HP * HD]),
    }
    project(nc, a, scr, nb)
    attend(nc, a, scr, nb)
    finish(nc, a, scr, nb)


def _layout(x, W_in, b_in, W_gx, b_gx, W_ga, b_ga, a_param, W_out, b_out, Wqkv, bqkv, Wr, br, W_r, W_k, W_v, mu_r, mu_k):
    w = Wqkv.reshape(HEADS, 3, HD, D)
    bb = bqkv.reshape(HEADS, 3, HD)
    at = np.clip(np.arange(TW) - (P - 1), 0, R - 1)
    far = np.zeros((D, 32), np.float32)
    for h in range(HEADS):
        rows = (h // HP) * HP * HD + np.arange(HD) * HP + h % HP
        far[rows, h] = Wr[0]
        far[rows, HEADS + h] = Wr[R - 1]
    sel = np.zeros((R_MAX + 1 - R_ONE, 3), np.float32)
    sel[R_MAX - R_ONE, :] = 1.0
    for x2 in (0, 2):
        sel[R_FAR - R_ONE + x2, LEFT] = 1.0
        sel[R_FAR - R_ONE + x2 + 1, RIGHT] = 1.0
    pick = np.zeros((P, HP * (HD + 1)), np.float32)
    for hh in range(HP):
        for jj in range(2):
            for r in range(HD + 1):
                pick[(2 * hh + jj) * VW + r, hh * (HD + 1) + r] = 1.0

    def cols(v):
        return v.reshape(NF, P).T

    def mixed(v):
        return v.reshape((NPR, HP, HD) + v.shape[2:]).swapaxes(1, 2).reshape((D,) + v.shape[2:])

    return {
        "x": x, "W_in": W_in, "b_in": cols(b_in), "W_gx": W_gx, "b_gx": cols(b_gx), "W_ga": W_ga, "b_ga": cols(b_ga),
        "a_param": cols(a_param), "W_out": W_out, "b_out": b_out,
        "Wq": mixed(w[:, 0]).T, "Wk": mixed(w[:, 1]).T, "Wv": w[:, 2].reshape(D, D).T,
        "bq": cols(mixed(bb[:, 0])), "bk": cols(mixed(bb[:, 1])), "bv": bb[:, 2].reshape(D),
        "wr_pad": Wr.T[:, at], "br_pad": br[at], "far": far,
        "bfar": np.repeat(br[[0, R - 1]], HEADS).reshape(2 * HEADS, 1),
        "sel": sel, "pick": pick, "ident": np.eye(P, dtype=np.float32),
        "ffn_wr": W_r.T, "ffn_wk": W_k.T, "ffn_wv": W_v.T, "mu_r": cols(mu_r), "mu_k": cols(mu_k),
    }


_ORDER = ["L0_attn_a_x", "L0_attn_a_W_in", "L0_attn_a_b_in", "L0_attn_a_W_gx", "L0_attn_a_b_gx", "L0_attn_a_W_ga",
          "L0_attn_a_b_ga", "L0_attn_a_a_param", "L0_attn_a_W_out", "L0_attn_a_b_out", "L0_attn_b_Wqkv",
          "L0_attn_b_bqkv", "L0_attn_b_Wr", "L0_attn_b_br", "L0_ffn_W_r", "L0_ffn_W_k", "L0_ffn_W_v",
          "L0_ffn_mu_r", "L0_ffn_mu_k"]


def kernel(**inputs):
    import concourse.bacc as _bacc
    from concourse.bass_utils import run_bass_kernel_spmd as _run

    nc = _bacc.Bacc("TRN2", target_bir_lowering=False, num_devices=1)
    arrays = {f"in_{k}": np.ascontiguousarray(v)
              for k, v in _layout(*[np.asarray(inputs[n]) for n in _ORDER]).items()}
    args = {k[3:]: nc.dram_tensor(k, v.shape, mybir.dt.from_np(v.dtype), kind="ExternalInput").ap()
            for k, v in arrays.items()}
    shape = arrays["in_x"].shape
    out = nc.dram_tensor("out", shape, F32, kind="ExternalOutput").ap()
    hybrid_kernel(nc, args, out)
    r = _run(nc, [arrays], core_ids=[0])
    return r.results[0]["out"]
```

```python
from contextlib import ExitStack

import numpy as np

import concourse.bass as bass
from concourse import mybir

F32 = mybir.dt.float32
F16 = mybir.dt.float16
ALU = mybir.AluOpType
ACT = mybir.ActivationFunctionType
AX_X = mybir.AxisListType.X

P = 128
D = 256
NF = D // P
S = 1024
CH = 512
NC = S // CH
NT = CH // P
HEADS = 16
HD = D // HEADS
WIN = 128
R = 2 * WIN + 1
EPS = 1e-5

HP = 2
NPR = HEADS // HP
VW = 32
NTI = S // P
TW = 3 * P
TR = 4 * P
NQ = 2 * HP
TLAG = 4
WW = 3 * P

R_ONE = 4 * HD
R_FAR = R_ONE + 2
R_MAX = R_FAR + 4
K_TAB, K_MAXP, K_SC = R_FAR, R_MAX, R_MAX + 1


def dram(t, offset, ap):
    return bass.AP(tensor=t.tensor, offset=offset, ap=ap)


class Pool:

    def __init__(self, nc, ctx):
        self.nc, self.ctx = nc, ctx

    def sb(self, name, shape, dt=F32):
        return self.ctx.enter_context(self.nc.sbuf_tensor(name, shape, dt))

    def ps(self, name, shape):
        return self.ctx.enter_context(self.nc.psum_tensor(name, shape, F32))

    def sems(self, names):
        return [self.ctx.enter_context(self.nc.semaphore(n)) for n in names.split()]


PRODUCTS_HI, PRODUCTS_LO = ((0, 0), (0, 1)), ((1, 0),)


def feature_major(pe, banks, w, x, ready, free, wait_hi, wait_lo):
    wait_hi()
    for products in (PRODUCTS_HI, PRODUCTS_LO):
        if products is PRODUCTS_LO:
            wait_lo()
        for o in range(NF):
            if products is PRODUCTS_HI:
                free(o)
            for f in range(NF):
                for px, pw in products:
                    mm = pe.matmul(banks[o][:], w[:, pw, f, o * P:(o + 1) * P], x[:, px, f, :],
                                   start=(px == 0 and pw == 0 and f == 0), stop=(px == 1 and f == NF - 1),
                                   skip_group_check=True)
            if products is PRODUCTS_LO:
                mm.then_inc(ready, 1)


def token_major(pe, banks, w, x, ready, free, wait_hi, wait_lo):
    wait_hi()
    for products in (PRODUCTS_HI, PRODUCTS_LO):
        if products is PRODUCTS_LO:
            wait_lo()
        for h in range(2):
            if products is PRODUCTS_HI:
                free(h)
            for t in (2 * h, 2 * h + 1):
                for f in range(NF):
                    for px, pw in products:
                        mm = pe.matmul(banks[h][:, (t % 2) * D:(t % 2 + 1) * D], x[:, px, f, t * P:(t + 1) * P],
                                       w[:, pw, f, :], start=(px == 0 and pw == 0 and f == 0 and t % 2 == 0),
                                       stop=(px == 1 and f == NF - 1), skip_group_check=True)
            if products is PRODUCTS_LO:
                mm.then_inc(ready, 1)


class Norm:

    def __init__(self, m, tag, low=False):
        self.stats = [m.sb(f"{tag}_stats{c}", [P, NT, 6]) for c in range(2)]
        self.mv = [m.sb(f"{tag}_mv{c}", [P, NT, 2]) for c in range(2)]
        self.ve = [m.sb(f"{tag}_ve{c}", [P, NT]) for c in range(2)]
        self.rstd = [m.sb(f"{tag}_rstd{c}", [P, NT]) for c in range(2)]
        self.gap = m.sb(f"{tag}_gap", [P, 1])
        self.xn = [m.sb(f"{tag}_xn{c}", [P, NT, D]) for c in range(2)]
        self.stats_done, self.rstd_done, self.norm_done, self.tr_ready, self.tr_copied = m.sems(" ".join(
            f"{tag}_{n}" for n in "stats_done rstd_done norm_done tr_ready tr_copied".split()))
        if low:
            self.tr_low, = m.sems(f"{tag}_tr_low")

    def dve_stats(self, dve, u, c, src):
        for t in range(NT):
            dve.bn_stats(self.stats[c][:, t, :], src[:, t, :]).then_inc(self.stats_done, 1)
        dve.wait_ge(self.stats_done, u * 2 * NT + NT)
        dve.memset(self.gap[:], 0.0)
        for t in range(NT):
            dve.bn_aggr(self.mv[c][:, t, :], self.stats[c][:, t, :]).then_inc(self.stats_done, 1)

    def pool_rstd(self, pool, u, c, eps, minus_half):
        pool.wait_ge(self.stats_done, u * 2 * NT + 2 * NT)
        pool.tensor_tensor(self.ve[c][:], self.mv[c][:, :, 1], eps[:], ALU.add).then_inc(self.rstd_done, 1)
        pool.wait_ge(self.rstd_done, u * 2 + 1)
        pool.tensor_tensor(self.rstd[c][:], self.ve[c][:], minus_half[:], ALU.pow).then_inc(self.rstd_done, 1)

    def dve_apply(self, dve, u, c, src):
        dve.wait_ge(self.rstd_done, u * 2 + 2)
        for t in range(NT):
            dve.tensor_scalar(self.xn[c][:, t, :], src[:, t, :], self.mv[c][:, t, 0:1],
                              self.rstd[c][:, t:t + 1], ALU.subtract, ALU.mult).then_inc(self.norm_done, 1)

    def pe_transpose(self, pe, u, c, banks, ident, free):
        pe.wait_ge(self.norm_done, u * NT + NT)
        for f in range(NF):
            free(f)
            for t in range(NT):
                tr = pe.transpose(banks[f][:, t * P:(t + 1) * P], self.xn[c][:, t, f * P:(f + 1) * P], ident[:])
            tr.then_inc(self.tr_ready, 1)

    def act_copy(self, act, u, c, banks, dst):
        for f in range(NF):
            act.wait_ge(self.tr_ready, u * NF + f + 1)
            act.activation(dst[:, f, :], banks[f][:], ACT.Identity).then_inc(self.tr_copied, 1)


    def dve_low(self, dve, u, banks, x):
        for f in range(NF):
            dve.wait_ge(self.tr_copied, u * NF + f + 1)
            dve.tensor_tensor(x[:, 1, f, :], banks[f][:], x[:, 0, f, :], ALU.subtract).then_inc(self.tr_low, 1)


class Ffn:

    def __init__(self, m, tag, tr_banks, banks, v_banks, w):
        self.w, self.tr_banks, self.banks, self.v_banks = w, tr_banks, banks, v_banks
        self.ln = Norm(m, tag)
        self.xt = [m.sb(f"{tag}_xt{c}", [P, NF, CH + 1]) for c in range(2)]
        self.diff = m.sb(f"{tag}_diff", [P, NF, CH])
        self.xr = m.sb(f"{tag}_xr", [P, NF, CH])
        self.xk = m.sb(f"{tag}_xk", [P, NF, CH])
        self.tr = m.sb(f"{tag}_tr", [P, NT, D])
        self.kr = m.sb(f"{tag}_kr", [P, NF, CH])
        self.ka = m.sb(f"{tag}_ka", [P, NF, CH])
        self.rv = m.sb(f"{tag}_rv", [P, NT, D])
        self.xk2, self.xr2, self.ka2 = [m.sb(f"{tag}_{n}2", [P, 2, NF, CH], F16) for n in ("xk", "xr", "ka")]
        self.hi_done, self.lo_done, self.ka_hi, self.ka_lo = m.sems(
            f"{tag}_hi_done {tag}_lo_done {tag}_ka_hi {tag}_ka_lo")
        (self.zeroed, self.before_set, self.diff_done, self.mixed, self.r_ready, self.r_done, self.k_ready,
         self.k_done, self.ka_done, self.v_ready, self.rv_done, self.x_done) = m.sems(" ".join(
             f"{tag}_{n}" for n in ("zeroed before_set diff_done mixed r_ready r_done k_ready k_done ka_done "
                                    "v_ready rv_done x_done").split()))

    def dve_init(self, dve):
        dve.memset(self.xt[0][:, :, 0:1], 0.0).then_inc(self.zeroed, 1)
        dve.wait_ge(self.zeroed, 1)

    def act_input(self, act, u, c):
        self.ln.act_copy(act, u, c, self.tr_banks, self.xt[c][:, :, 1:])
        if c == 1:
            act.wait_ge(self.ln.tr_copied, u * NF)
            act.activation(self.xt[1][:, :, 0:1], self.xt[0][:, :, CH:CH + 1], ACT.Identity)\
               .then_inc(self.before_set, 1)

    def dve_mix(self, dve, u, b, c):
        dve.wait_ge(self.ln.tr_copied, u * NF + NF)
        if c == 1:
            dve.wait_ge(self.before_set, b + 1)
        dve.tensor_tensor(self.diff[:], self.xt[c][:, :, 1:], self.xt[c][:, :, 0:CH], ALU.subtract)\
           .then_inc(self.diff_done, 1)
        dve.wait_ge(self.diff_done, u + 1)
        for dst, mu in ((self.xk, self.w["mu_k"]), (self.xr, self.w["mu_r"])):
            if dst is self.xr:
                wait_pos(dve, self.lo_done, u * 2)
            for f in range(NF):
                dve.scalar_tensor_tensor(dst[:, f, :], self.diff[:, f, :], mu[:, f:f + 1],
                                         self.xt[c][:, f, 0:CH], ALU.mult, ALU.add).then_inc(self.mixed, 1)

    def act_high(self, act, u, n):
        src, dst = ((self.xk, self.xk2), (self.xr, self.xr2), (self.ka, self.ka2))[n]
        if n < 2:
            act.wait_ge(self.mixed, u * 2 * NF + (n + 1) * NF)
        else:
            act.wait_ge(self.ka_done, u * NF + NF)
        act.activation(dst[:, 0], src[:], ACT.Identity).then_inc(self.ka_hi if n == 2 else self.hi_done, 1)

    def pool_low(self, pool, u, n):
        src, dst = ((self.xk, self.xk2), (self.xr, self.xr2), (self.ka, self.ka2))[n]
        if n < 2:
            pool.wait_ge(self.hi_done, u * 2 + n + 1)
        else:
            pool.wait_ge(self.ka_hi, u + 1)
        pool.tensor_tensor(dst[:, 1], src[:], dst[:, 0], ALU.subtract)\
            .then_inc(self.ka_lo if n == 2 else self.lo_done, 1)

    def waits(self, pe, u, n):
        if n == 2:
            return (lambda: pe.wait_ge(self.ka_hi, u + 1)), (lambda: pe.wait_ge(self.ka_lo, u + 1))
        return (lambda: pe.wait_ge(self.hi_done, u * 2 + n + 1)), (lambda: pe.wait_ge(self.lo_done, u * 2 + n + 1))

    def pe_k(self, pe, u, free):
        feature_major(pe, self.banks[0:2], self.w["wk"], self.xk2, self.k_ready, free, *self.waits(pe, u, 0))

    def pe_r(self, pe, u, free):
        token_major(pe, self.banks[2:4], self.w["wr"], self.xr2, self.r_ready, free, *self.waits(pe, u, 1))

    def act_k(self, act, u):
        for o in range(NF):
            act.wait_ge(self.k_ready, u * NF + o + 1)
            act.activation(self.kr[:, o, :], self.banks[o][:], ACT.Relu).then_inc(self.k_done, 1)

    def act_r(self, act, u):
        for h in range(2):
            act.wait_ge(self.r_ready, u * 2 + h + 1)
            act.activation(self.tr[:, 2 * h:2 * h + 2, :], self.banks[2 + h][:].rearrange("p (t d) -> p t d", t=2),
                           ACT.Tanh, scale=0.5).then_inc(self.r_done, 1)

    def pool_square(self, pool, u):
        for o in range(NF):
            pool.wait_ge(self.k_done, u * NF + o + 1)
            pool.tensor_tensor(self.ka[:, o, :], self.kr[:, o, :], self.kr[:, o, :], ALU.mult)\
                .then_inc(self.ka_done, 1)

    def pe_v(self, pe, u, free):
        token_major(pe, self.v_banks, self.w["wv"], self.ka2, self.v_ready, free, *self.waits(pe, u, 2))

    def dve_out(self, dve, u, x):
        for h in range(2):
            dve.wait_ge(self.r_done, u * 2 + h + 1)
            dve.wait_ge(self.v_ready, u * 2 + h + 1)
            dve.scalar_tensor_tensor(self.rv[:, 2 * h:2 * h + 2, :], self.tr[:, 2 * h:2 * h + 2, :], 1.0,
                                     self.v_banks[h][:].rearrange("p (t d) -> p t d", t=2),
                                     ALU.add, ALU.mult).then_inc(self.rv_done, 1)
        dve.wait_ge(self.rv_done, u * 2 + 2)
        dve.scalar_tensor_tensor(x[:], self.rv[:], 0.5, x[:], ALU.mult, ALU.add).then_inc(self.x_done, 1)
        dve.wait_ge(self.x_done, u + 1)


def weights_high(act, w32, w16, copied, before=None):
    for n in w16:
        if before is not None:
            before(n)
        act.activation(w16[n][:, 0], w32[n][:], ACT.Identity).then_inc(copied, 1)


def weights_low(dve, w32, w16, copied, split):
    for i, n in enumerate(w16):
        dve.wait_ge(copied, i + 1)
        dve.tensor_tensor(w16[n][:, 1], w32[n][:], w16[n][:, 0], ALU.subtract).then_inc(split, 1)


def rows(w):
    return w.rearrange("(f p) n -> p f n", p=P)


def project(nc, a, scr, nb):
    with ExitStack() as ctx:
        m = Pool(nc, ctx)
        bank = [m.ps(f"pj_bank{i}", [P, CH]) for i in range(8)]

        w_names = ["W_in", "W_gx", "W_ga", "W_out", "ffn_wr", "ffn_wk", "ffn_wv", "Wq", "Wk", "Wv"]
        w32 = {n: m.sb(f"pj_{n}_32", [P, NF, D]) for n in w_names}
        w = {n: m.sb(f"pj_{n}", [P, 2, NF, D], F16) for n in w_names}
        v_names = ["b_in", "b_gx", "b_ga", "a_param", "mu_r", "mu_k", "bq", "bk"]
        v = {n: m.sb(f"pj_{n}", [P, NF]) for n in v_names}
        b_out = m.sb("pj_b_out", [P, D])
        bv = m.sb("pj_bv", [P, D])
        far32 = m.sb("pj_far32", [P, NF, 32])
        far_h = m.sb("pj_far_h", [P, NF, 32], F16)
        far_l = m.sb("pj_far_l", [P, NF, 32], F16)
        bfar = m.sb("pj_bfar", [32, 1])
        ident = m.sb("pj_ident", [P, P])
        eps = m.sb("pj_eps", [P, NT])
        fetch = m.sb("pj_fetch", [P, 1])
        minus_half = m.sb("pj_minus_half", [P, NT])
        sp_a, sp_b, sp_c, decay = [m.sb(f"pj_sp{i}", [P, NF]) for i in range(4)]

        xl = [m.sb(f"pj_xl{c}", [P, NT, D]) for c in range(2)]
        xb = [m.sb(f"pj_xb{c}", [P, NT, D]) for c in range(2)]
        lnt = m.sb("pj_lnt", [P, 2, NF, CH], F16)
        xin2 = m.sb("pj_xin2", [P, 2, NF, CH], F16)
        h2 = m.sb("pj_h2", [P, 2, NF, CH], F16)
        xin = m.sb("pj_xin", [P, NF, CH])
        tgx = m.sb("pj_tgx", [P, NF, CH])
        tga = m.sb("pj_tga", [P, NF, CH])
        aa = m.sb("pj_aa", [P, NF, CH])
        zz = m.sb("pj_zz", [P, NF, CH])
        hh = [m.sb(f"pj_h{c}", [P, NF, CH]) for c in range(2)]
        lt = m.sb("pj_lt", [P, 2, NF, CH], F16)
        qh, ql, kh, kl = [m.sb(f"pj_{n}", [P, NF, CH], F16) for n in ("qh", "ql", "kh", "kl")]
        fh, fl = [m.sb(f"pj_{n}", [32, CH], F16) for n in ("fh", "fl")]
        vp = m.sb("pj_vp", [P, NT, HEADS, VW])

        ln1, ln3 = Norm(m, "ln1", low=True), Norm(m, "ln3", low=True)
        ffn = Ffn(m, "f1", bank[4:6], bank[4:8], bank[6:8], {"wr": w["ffn_wr"], "wk": w["ffn_wk"], "wv": w["ffn_wv"],
                                       "mu_r": v["mu_r"], "mu_k": v["mu_k"]})
        x_loaded = m.sems("x_loaded0 x_loaded1")
        w_copied, w_split, xin_lo, h_hi, h_lo = m.sems("w_copied w_split xin_lo h_hi h_lo")
        x2_stored = m.sems("x2_stored0 x2_stored1")
        (w_loaded, consts_set, sp_step, decay_set, far_split,
         bias_added, xin_ready, xin_done, gx_ready, gx_done, ga_ready, ga_done, a_done, a2_done, z_done, sq_done,
         xg_done, u_done, h_done, y_ready, x1_done,
         q_ready, qh_done, ql_done, k_ready, kh_done, kl_done, f_ready, fh_done, fl_done, vv_ready, vv_done,
         q_stored, k_stored, f_stored, v_stored) = m.sems(
             "w_loaded consts_set sp_step decay_set far_split "
             "bias_added xin_ready xin_done gx_ready gx_done ga_ready ga_done a_done a2_done z_done sq_done "
             "xg_done u_done h_done y_ready x1_done "
             "q_ready qh_done ql_done k_ready kh_done kl_done f_ready fh_done fl_done vv_ready vv_done "
             "q_stored k_stored f_stored v_stored")

        loads = [(w32[n], rows(a[n])) for n in w_names] + [(v[n], a[n]) for n in v_names]
        loads += [(b_out, a["b_out"].unsqueeze(0).to_broadcast([P, D])), (bv, a["bv"].unsqueeze(0).to_broadcast([P, D])),
                  (far32, a["far"].rearrange("(f p) n -> p f n", p=P)), (bfar, a["bfar"]), (ident, a["ident"])]
        w_all = 16 * len(loads)
        nu = nb * NC

        def rounds(eng, body):
            for u in range(4):
                body(u, u // 2, u % 2, (True, u > 0, u > 1), nu - 1 - u)
            if nb > 3:
                with eng.Fori(2, nb - 1) as b:
                    for c in range(NC):
                        body(b * NC + c, b, c, (True, True, True), 2)
            for u in range(nu - 2, nu + 2):
                body(u, u // 2, u % 2, (u < nu, u <= nu, True), nu - 1 - u)

        block = ctx.enter_context(nc.Block())

        @block.sync
        def _(sp):
            for dst, src in loads:
                sp.dma_start(dst[:], src).then_inc(w_loaded, 16)

            def load_x(b, c):
                sp.dma_start(xl[c][:], a["x"][b, c * CH:(c + 1) * CH, :].rearrange("(t p) d -> p t d", p=P))\
                  .then_inc(x_loaded[c], 16)

            load_x(0, 0)
            load_x(0, 1)

            def body(u, b, c, on, nxt):
                if on[1]:
                    c1, b1 = 1 - c, b - (1 - c)
                    sp.wait_ge(ffn.x_done, u)
                    sp.dma_start(scr["x2"][b1, c1 * CH:(c1 + 1) * CH, :].rearrange("(t p) d -> p t d", p=P), xb[c1][:])\
                      .then_inc(x2_stored[c1], 16)
                if on[2]:
                    b2, tok = b - 1, c * CH
                    for hi, lo, lo_done, name, stored in ((qh, ql, ql_done, "q", q_stored),
                                                          (kh, kl, kl_done, "k", k_stored)):
                        sp.wait_ge(lo_done, (u - 2) * NF + NF)
                        for part, src in ((1, lo), (0, hi)):
                            sp.dma_start(scr[name][part, b2, :, tok:tok + CH].rearrange("(f p) t -> p f t", p=P),
                                         src[:]).then_inc(stored, 16)
                    for part, src, done in ((0, fh, fh_done), (1, fl, fl_done)):
                        sp.wait_ge(done, u - 1)
                        for s in range(2):
                            sp.dma_start(scr["far"][part, s, b2, :, tok:tok + CH], src[s * HEADS:(s + 1) * HEADS, :])\
                              .then_inc(f_stored, 16)
                    sp.wait_ge(vv_done, (u - 2) * 2 + 2)
                    for t in range(NT):
                        sp.dma_start(scr["v"][b2, :, tok + t * P:tok + (t + 1) * P, :].rearrange("r p v -> p r v"),
                                     vp[:, t].rearrange("p (r h) v -> p r (h v)", r=NPR)).then_inc(v_stored, 16)
                if nxt >= 2:
                    sp.wait_ge(bias_added, u + 1)
                    sp.wait_ge(ln1.norm_done, u * NT + NT)
                    load_x(b + 1, c)

            rounds(sp, body)
            for sem in x2_stored:
                sp.wait_ge(sem, 16 * nb)
            for sem, n in ((q_stored, 2), (k_stored, 2), (f_stored, 4), (v_stored, NT)):
                sp.wait_ge(sem, 16 * n * nu)

        @block.gpsimd
        def _(pool):
            pool.memset(minus_half[:], -0.5).then_inc(consts_set, 1)
            pool.memset(eps[:], EPS).then_inc(consts_set, 1)
            pool.memset(vp[:], 0.0).then_inc(consts_set, 1)
            pool.wait_ge(consts_set, 3)
            pool.memset(vp[:, :, :, HD:HD + 1], 1.0).then_inc(consts_set, 1)
            pool.wait_ge(w_loaded, w_all)
            pool.tensor_scalar(w32["Wk"][:], w32["Wk"][:], 0.25, None, ALU.mult).then_inc(consts_set, 1)
            pool.tensor_scalar(v["bk"][:], v["bk"][:], 0.25, None, ALU.mult).then_inc(consts_set, 1)
            pool.tensor_scalar(v["b_gx"][:], v["b_gx"][:], 0.5, None, ALU.mult).then_inc(consts_set, 1)
            pool.tensor_scalar(v["b_ga"][:], v["b_ga"][:], 0.5, None, ALU.mult).then_inc(consts_set, 1)

            def body(u, b, c, on, nxt):
                if isinstance(u, int) and u == 0:
                    ln1.pool_rstd(pool, 0, 0, eps, minus_half)
                if on[0]:
                    pool.wait_ge(x_loaded[c], b * 16 + 16)
                    if on[2]:
                        pool.wait_ge(x2_stored[c], b * 16)
                        pool.wait_ge(ln3.norm_done, (u - 1) * NT)
                    pool.tensor_tensor(xb[c][:], xl[c][:], b_out[:].unsqueeze(1).to_broadcast([P, NT, D]), ALU.add)\
                        .then_inc(bias_added, 1)
                if on[1]:
                    ffn.pool_low(pool, u - 1, 0)
                    ffn.pool_low(pool, u - 1, 1)
                    ffn.pool_square(pool, u - 1)
                if nxt >= 1:
                    ln1.pool_rstd(pool, u + 1, 1 - c, eps, minus_half)
                if on[1]:
                    ffn.pool_low(pool, u - 1, 2)
                if on[0]:
                    pool.wait_ge(h_hi, u + 1)
                    pool.tensor_tensor(h2[:, 1], hh[c][:], h2[:, 0], ALU.subtract).then_inc(h_lo, 1)
                if on[1]:
                    ln3.pool_rstd(pool, u - 1, 1 - c, eps, minus_half)
                if on[0]:
                    ffn.ln.pool_rstd(pool, u, c, eps, minus_half)

            rounds(pool, body)

        @block.scalar
        def _(act):
            act.wait_ge(w_loaded, w_all)
            act.wait_ge(sp_step, 1)
            act.activation(sp_b[:], sp_a[:], ACT.Exp, scale=-1.0).then_inc(sp_step, 1)
            act.wait_ge(sp_step, 2)
            act.activation(sp_c[:], sp_b[:], ACT.Ln, bias=1.0).then_inc(sp_step, 1)
            weights_high(act, w32, w, w_copied, lambda n: act.wait_ge(consts_set, 8) if n == "Wk" else None)
            act.wait_ge(consts_set, 8)
            act.wait_ge(decay_set, 1)

            def body(u, b, c, on, nxt):
                if on[0]:
                    for o in range(NF):
                        act.wait_ge(xin_ready, u * NF + o + 1)
                        if o == 0 and on[1]:
                            act.wait_ge(xg_done, u)
                        act.activation(xin2[:, 0, o, :], bank[2 + o][:], ACT.Identity, bias=v["b_in"][:, o:o + 1])\
                           .then_inc(xin_done, 1)
                    for o in range(NF):
                        act.activation(xin[:, o, :], bank[2 + o][:], ACT.Identity, bias=v["b_in"][:, o:o + 1])\
                           .then_inc(xin_done, 1)
                if on[2]:
                    ln3.act_copy(act, u - 2, c, bank[0:2], lt[:, 0])
                if on[0]:
                    if on[1]:
                        act.wait_ge(h_done, u * NF)
                    for o in range(NF):
                        act.wait_ge(gx_ready, u * NF + o + 1)
                        act.activation(tgx[:, o, :], bank[6 + o][:], ACT.Tanh, bias=v["b_gx"][:, o:o + 1], scale=0.5)\
                           .then_inc(gx_done, 1)
                if on[1]:
                    ffn.act_input(act, u - 1, 1 - c)

                def high(hi, ready, done, bb, stored, bk):
                    for o in range(NF):
                        act.wait_ge(ready, (u - 2) * NF + o + 1)
                        if o == 0:
                            wait_pos(act, stored, (u - 2) * 32)
                        act.activation(hi[:, o, :], bk[o][:], ACT.Identity, bias=bb[:, o:o + 1]).then_inc(done, 1)

                if on[2]:
                    high(qh, q_ready, qh_done, v["bq"], q_stored, bank[0:2])
                if on[1]:
                    ffn.act_high(act, u - 1, 0)
                    ffn.act_high(act, u - 1, 1)
                if on[0]:
                    for o in range(NF):
                        act.wait_ge(ga_ready, u * NF + o + 1)
                        act.activation(tga[:, o, :], bank[2 + o][:], ACT.Tanh, bias=v["b_ga"][:, o:o + 1], scale=0.5)\
                           .then_inc(ga_done, 1)
                    act.wait_ge(ga_done, u * NF + NF)
                    for o in range(NF):
                        act.activation(aa[:, o, :], tga[:, o, :], ACT.Exp, bias=decay[:, o:o + 1],
                                       scale=decay[:, o:o + 1]).then_inc(a_done, 1)
                if on[1]:
                    ffn.act_k(act, u - 1)
                    ffn.act_r(act, u - 1)
                    ffn.act_high(act, u - 1, 2)
                if on[0]:
                    act.wait_ge(z_done, u + 1)
                    act.activation(zz[:], zz[:], ACT.Sqrt).then_inc(sq_done, 1)
                if on[2]:
                    high(kh, k_ready, kh_done, v["bk"], k_stored, bank[4:6])
                if on[0]:
                    act.wait_ge(h_done, u * NF + NF)
                    act.activation(h2[:, 0], hh[c][:], ACT.Identity).then_inc(h_hi, 1)
                    act.activation(fetch[:], eps[:, 0:1], ACT.Tanh)
                if nxt >= 1:
                    ln1.act_copy(act, u + 1, 1 - c, bank[2:4], lnt[:, 0])
                if on[2]:
                    act.wait_ge(f_ready, u - 1)
                    wait_pos(act, f_stored, (u - 2) * 64)
                    act.activation(fh[:], bank[0][0:32, :], ACT.Identity, bias=bfar[:]).then_inc(fh_done, 1)

            ln1.act_copy(act, 0, 0, bank[2:4], lnt[:, 0])
            rounds(act, body)

        @block.vector
        def _(dve):
            dve.wait_ge(w_loaded, w_all)
            dve.scalar_tensor_tensor(sp_a[:], v["a_param"][:], -1.0, v["a_param"][:], ALU.mult, ALU.max)\
               .then_inc(sp_step, 1)
            dve.wait_ge(sp_step, 3)
            dve.scalar_tensor_tensor(decay[:], v["a_param"][:], 0.0, sp_c[:], ALU.max, ALU.add).then_inc(sp_step, 1)
            dve.wait_ge(sp_step, 4)
            dve.tensor_scalar(decay[:], decay[:], -4.0, None, ALU.mult).then_inc(decay_set, 1)
            dve.tensor_copy(far_h[:], far32[:]).then_inc(far_split, 1)
            dve.wait_ge(far_split, 1)
            dve.tensor_tensor(far_l[:], far32[:], far_h[:], ALU.subtract).then_inc(far_split, 1)
            ffn.dve_init(dve)

            weights_low(dve, w32, w, w_copied, w_split)

            def split(u, hi, lo, hi_done, lo_done, bb, stored, bk):
                for o in range(NF):
                    dve.wait_ge(hi_done, u * NF + o + 1)
                    if o == 0:
                        wait_pos(dve, stored, u * 32)
                    dve.scalar_tensor_tensor(lo[:, o, :], bk[o][:], bb[:, o:o + 1], hi[:, o, :], ALU.add,
                                             ALU.subtract).then_inc(lo_done, 1)

            def body(u, b, c, on, nxt):
                if on[0]:
                    dve.wait_ge(xin_done, u * 2 * NF + 2 * NF)
                    dve.tensor_tensor(xin2[:, 1], xin[:], xin2[:, 0], ALU.subtract).then_inc(xin_lo, 1)
                if on[1]:
                    ffn.ln.dve_apply(dve, u - 1, 1 - c, xb[1 - c])
                if on[2]:
                    ln3.dve_low(dve, u - 2, bank[0:2], lt)
                if on[0]:
                    dve.wait_ge(gx_done, u * NF + NF)
                    dve.scalar_tensor_tensor(tgx[:], tgx[:], 1.0, xin[:], ALU.add, ALU.mult).then_inc(xg_done, 1)
                if on[1]:
                    ffn.dve_mix(dve, u - 1, b - (1 - c), 1 - c)
                if on[2]:
                    split(u - 2, qh, ql, qh_done, ql_done, v["bq"], q_stored, bank[0:2])
                if on[0]:
                    dve.wait_ge(a_done, u * NF + NF)
                    dve.scalar_tensor_tensor(zz[:], aa[:], -1.0, aa[:], ALU.mult, ALU.mult).then_inc(a2_done, 1)
                    dve.wait_ge(a2_done, u + 1)
                    dve.tensor_scalar(zz[:], zz[:], 1.0, 0.0, ALU.add, ALU.max).then_inc(z_done, 1)
                if nxt >= 1:
                    dve.wait_ge(x_loaded[1 - c], (b + c) * 16 + 16)
                    ln1.dve_stats(dve, u + 1, 1 - c, xl[1 - c])
                    ln1.dve_apply(dve, u + 1, 1 - c, xl[1 - c])
                if on[0]:
                    dve.wait_ge(sq_done, u + 1)
                    dve.wait_ge(xg_done, u + 1)
                    dve.scalar_tensor_tensor(tgx[:], zz[:], 0.5, tgx[:], ALU.mult, ALU.mult).then_inc(u_done, 1)
                    dve.wait_ge(u_done, u + 1)
                    if on[1]:
                        dve.wait_ge(h_done, u * NF)
                    for f in range(NF):
                        start = 0.0 if c == 0 else hh[0][:, f, CH - 1:CH]
                        dve.tensor_tensor_scan(hh[c][:, f, :], aa[:, f, :], tgx[:, f, :], start, ALU.mult, ALU.add)\
                           .then_inc(h_done, 1)
                if on[2]:
                    split(u - 2, kh, kl, kh_done, kl_done, v["bk"], k_stored, bank[4:6])
                if on[1]:
                    ffn.dve_out(dve, u - 1, xb[1 - c])
                if nxt >= 1:
                    ln1.dve_low(dve, u + 1, bank[2:4], lnt)
                if on[1]:
                    ln3.dve_stats(dve, u - 1, 1 - c, xb[1 - c])
                if on[2]:
                    dve.wait_ge(fh_done, u - 1)
                    wait_pos(dve, f_stored, (u - 2) * 64)
                    dve.scalar_tensor_tensor(fl[:], bank[0][0:32, :], bfar[:], fh[:], ALU.add, ALU.subtract)\
                       .then_inc(fl_done, 1)
                    wait_pos(dve, v_stored, (u - 2) * NT * 16)
                    for h in range(2):
                        dve.wait_ge(vv_ready, (u - 2) * 2 + h + 1)
                        for t in range(2):
                            ins = dve.tensor_tensor(vp[:, 2 * h + t, :, 0:HD],
                                              bank[(1, 4)[h]][:, t * D:(t + 1) * D].rearrange("p (h d) -> p h d", d=HD),
                                              bv[:].rearrange("p (h d) -> p h d", d=HD), ALU.add)
                        ins.then_inc(vv_done, 1)
                if on[1]:
                    ln3.dve_apply(dve, u - 1, 1 - c, xb[1 - c])
                if on[0]:
                    for h in range(2):
                        dve.wait_ge(y_ready, u * 2 + h + 1)
                        dve.wait_ge(bias_added, u + 1)
                        dve.tensor_tensor(xb[c][:, 2 * h:2 * h + 2, :],
                                          bank[6 + h][:].rearrange("p (t d) -> p t d", t=2),
                                          xb[c][:, 2 * h:2 * h + 2, :], ALU.add).then_inc(x1_done, 1)
                    dve.wait_ge(x1_done, u * 2 + 2)
                    ffn.ln.dve_stats(dve, u, c, xb[c])

            dve.wait_ge(consts_set, 4)
            dve.wait_ge(x_loaded[0], 16)
            ln1.dve_stats(dve, 0, 0, xl[0])
            ln1.dve_apply(dve, 0, 0, xl[0])
            ln1.dve_low(dve, 0, bank[2:4], lnt)
            rounds(dve, body)

        @block.tensor
        def _(pe):
            pe.wait_ge(w_loaded, w_all)
            pe.wait_ge(w_split, len(w))
            pe.wait_ge(far_split, 2)

            def nothing(*_):
                pass

            def body(u, b, c, on, nxt):
                u2 = u - 2
                if on[0]:
                    feature_major(pe, bank[2:4], w["W_in"], lnt, xin_ready, nothing,
                                  lambda: pe.wait_ge(ln1.tr_low, u * NF + NF), nothing)
                if on[2]:
                    ln3.pe_transpose(pe, u2, c, bank[0:2], ident,
                                     lambda f: wait_pos(pe, *((fl_done, u2), (vv_done, u2 * 2 - 1))[f]))
                if on[0]:
                    feature_major(pe, bank[6:8], w["W_gx"], xin2, gx_ready,
                                  lambda o: pe.wait_ge(x1_done, (u - 1) * 2 + o + 1) if on[1] else None,
                                  lambda: pe.wait_ge(xin_done, u * 2 * NF + NF), lambda: pe.wait_ge(xin_lo, u + 1))
                if on[1]:
                    ffn.ln.pe_transpose(pe, u - 1, 1 - c, bank[4:6], ident,
                                        lambda f: wait_pos(pe, *((vv_done, (u - 2) * 2), (kl_done, (u - 2) * NF))[f]))
                if on[2]:
                    feature_major(pe, bank[0:2], w["Wq"], lt, q_ready, nothing,
                                  lambda: pe.wait_ge(ln3.tr_low, u2 * NF + NF), nothing)
                if on[0]:
                    feature_major(pe, bank[2:4], w["W_ga"], xin2, ga_ready, nothing,
                                  lambda: pe.wait_ge(xin_done, u * 2 * NF + 2 * NF), nothing)
                if on[1]:
                    ffn.pe_k(pe, u - 1, lambda o: pe.wait_ge(ffn.ln.tr_copied, (u - 1) * NF + o + 1))
                    ffn.pe_r(pe, u - 1,
                              lambda h: pe.wait_ge(gx_done, u * NF + h + 1) if on[0] else
                              pe.wait_ge(x1_done, (u - 1) * 2 + h + 1))
                if on[2]:
                    feature_major(pe, bank[4:6], w["Wk"], lt, k_ready,
                                  lambda o: pe.wait_ge(ffn.k_done, (u - 1) * NF + o + 1) if on[1] else
                                  pe.wait_ge(*((vv_done, u2 * 2), (kl_done, u2 * NF))[o]), nothing, nothing)
                if on[1]:
                    ffn.pe_v(pe, u - 1, lambda h: pe.wait_ge(ffn.r_done, (u - 1) * 2 + h + 1))
                if nxt >= 1:
                    ln1.pe_transpose(pe, u + 1, 1 - c, bank[2:4], ident,
                                     lambda f: pe.wait_ge(ga_done, u * NF + f + 1))
                if on[2]:
                    pe.wait_ge(ql_done, u2 * NF + NF)
                    for f in range(NF):
                        for qq in (qh, ql):
                            for ff in (far_h, far_l):
                                mm = pe.matmul(bank[0][0:32, :], ff[:, f, :], qq[:, f, :],
                                               start=(f == 0 and qq is qh and ff is far_h),
                                               stop=(f == NF - 1 and qq is ql and ff is far_l))
                    mm.then_inc(f_ready, 1)
                    token_major(pe, (bank[1], bank[4]), w["Wv"], lt, vv_ready,
                                lambda h: pe.wait_ge(kl_done, u2 * NF + 1) if h == 1 else None, nothing, nothing)
                if on[0]:
                    token_major(pe, bank[6:8], w["W_out"], h2, y_ready,
                                lambda h: pe.wait_ge(*((ffn.rv_done, (u - 1) * 2 + h + 1) if on[1] else
                                                       (gx_done, u * NF + h + 1))),
                                lambda: pe.wait_ge(h_hi, u + 1), lambda: pe.wait_ge(h_lo, u + 1))

            ln1.pe_transpose(pe, 0, 0, bank[2:4], ident, lambda f: None)
            rounds(pe, body)


def wait_pos(eng, sem, value):
    if not isinstance(value, int) or value > 0:
        eng.wait_ge(sem, value)


LEFT, RIGHT = range(2)


def variants(i, j0, j1):
    runs = ((LEFT, j0, min(j1, i + 2)), (RIGHT, max(j0, i + 2), j1))
    return [(v, a, b) for v, a, b in runs if a < b]


def attend(nc, a, scr, nb):
    npairs = nb * NPR
    LOOPS = (npairs - 2) // 3
    with ExitStack() as ctx:
        m = Pool(nc, ctx)
        st_bank = [m.ps(f"at_st{i}", [P, CH]) for i in range(3)]
        mx_bank = [m.ps(f"at_mx{i}", [P, CH]) for i in range(2)]
        tab_bank = [m.ps(f"at_tab_bank{i}", [P, CH]) for i in range(2)]
        o_bank = m.ps("at_o", [P, CH])

        qs = [m.sb(f"at_q{i}", [P, HP, S], F16) for i in range(3)]
        ks = [m.sb(f"at_k{i}", [P, 2, HP, S], F16) for i in range(3)]
        vs = [m.sb(f"at_v{i}", [P, NTI, HP * VW]) for i in range(3)]
        pos = [m.sb(f"at_pos{i}", [P, NQ, 2, NT, WW], F16) for i in range(3)]
        tab = [m.sb(f"at_tab{i}", [P, 2, NT, TW], F16) for i in range(NQ)]
        tab32 = [m.sb(f"at_tab32_{i}", [P, TW]) for i in range(2)]
        pt = [m.sb(f"at_p{i}", [P, 2, CH]) for i in range(4)]
        os_ = m.sb("at_os", [P, CH])
        rden = m.sb("at_rden", [P, NT, HP])
        att = [m.sb(f"at_att{i}", [P, NT, HP * HD]) for i in range(2)]
        mx = [m.sb(f"at_mx_sb{i}", [P, 2, HP * NT]) for i in range(2)]
        mtop = m.sb("at_mtop", [P, HP * NT])
        mneg = [m.sb(f"at_mneg{i}", [P, HP * NT], F16) for i in range(2)]
        mrow = [m.sb(f"at_mrow{i}", [HP * NT, P], F16) for i in range(2)]
        w32 = m.sb("at_w32", [P, TW])
        w32s = m.sb("at_w32s", [P, TW])
        w_hi = m.sb("at_w_hi", [P, TW], F16)
        w_lo = m.sb("at_w_lo", [P, TW], F16)
        wt = m.sb("at_wt", [P, TW], F16)
        sel = m.sb("at_sel", [P, 2])
        zeros = m.sb("at_zeros", [P, P - 1], F16)
        ident = m.sb("at_ident", [P, P])
        ident_h = m.sb("at_ident_h", [P, P], F16)
        one = m.sb("at_one", [P, 1])
        pick = m.sb("at_pick", [P, HP * (HD + 1)])

        (c_loaded, zeros_written, w_shifted, one_set, c_set, wt_split, wt_loaded,
         tab_ready, tab_taken, tab_lo, tab_hi_pool, tab_lo_pool, mx_ready, mx_done, mtop_done, mneg_done,
         mrow_ready, mrow_copied, st_ready, exp_done, av_done, o_copied, out_ready, rden_done, att_done) = m.sems(
             "c_loaded zeros_written w_shifted one_set c_set wt_split wt_loaded "
             "tab_ready tab_taken tab_lo tab_hi_pool tab_lo_pool mx_ready mx_done mtop_done mneg_done "
             "mrow_ready mrow_copied st_ready exp_done av_done o_copied out_ready rden_done att_done")
        q_loaded, kv_loaded = [m.sems(" ".join(f"{n}_loaded{i}" for i in range(3))) for n in ("q", "kv")]
        mrow_loaded, att_stored = [m.sems(f"{n}0 {n}1") for n in ("mrow_loaded", "att_stored")]
        tab_written, pos_loaded = [m.sems(" ".join(f"{n}{c}" for c in range(NQ))) for n in ("tab_written", "pos_loaded")]

        def st_of(j, k, jj):
            return (j * 32 + 2 * k + jj) % 3

        def table_of(n, k):
            return (n + 2, k - TLAG) if k >= TLAG else (n + 1, 16 - TLAG + k)

        def turns(eng, body):
            def at(n):
                body(n, n % 3, lambda k: (n + k) // 3,
                     dict(prev=1 <= n <= npairs, now=0 <= n < npairs, nxt=0 <= n + 1 < npairs, far=n + 2 < npairs))

            for n in range(-2, 3):
                at(n)
            if LOOPS > 1:
                with eng.Fori(1, LOOPS) as it:
                    for j in range(3):
                        body(it * 3 + j, j, lambda k, j=j: it + (j + k) // 3,
                             dict(prev=True, now=True, nxt=True, far=True))
            for n in range(max(3 * LOOPS, 3), npairs + 1):
                at(n)

        block = ctx.enter_context(nc.Block())

        @block.sync
        def _(sp):
            for dst, src in ((ident[:], a["ident"]), (pick[:], a["pick"]), (sel[R_ONE:R_MAX + 1, :], a["sel"]),
                             (w32[R_ONE:R_ONE + 2, :], a["br_pad"].unsqueeze(0).to_broadcast([2, TW]))):
                sp.dma_start(dst, src).then_inc(c_loaded, 16)
            for r in range(4):
                sp.dma_start(w32[r * HD:(r + 1) * HD, :], a["wr_pad"]).then_inc(c_loaded, 16)
            sp.wait_ge(c_set, 1)
            sp.dma_start(dram(scr["tab"], 0, [[TR, P], [P * TR, 2 * NT * NQ], [1, P - 1]]),
                         zeros[:].unsqueeze(1).to_broadcast([P, 2 * NT * NQ, P - 1])).then_inc(zeros_written, 16)
            sp.wait_ge(wt_split, 2)
            for lo, r0, r1 in ((0, 0, 32), (1, 32, 64), (0, 64, 65), (1, 65, 66)):
                sp.dma_start(wt[r0:r1, :], (w_hi, w_lo)[lo][r0:r1, :]).then_inc(wt_loaded, 16)

            def load_q(n, slot):
                part, row = nb * D * S, HP * S
                for rep in range(2):
                    sp.dma_start(qs[slot][rep * 2 * HD:(rep + 1) * 2 * HD].rearrange("p h s -> p (h s)"),
                                 dram(scr["q"], n * (HD * row), [[part, 2], [row, HD], [1, row]]))\
                      .then_inc(q_loaded[slot], 16)
                sp.dma_start(qs[slot][R_FAR:R_FAR + 4].rearrange("p h s -> p (h s)"),
                             dram(scr["far"], n * row, [[nb * HEADS * S, 4], [1, row]])).then_inc(q_loaded[slot], 16)

            def load_k(n, slot):
                part, row = nb * D * S, HP * S
                for rep in range(2):
                    for v in range(2):
                        sp.dma_start(ks[slot][rep * 2 * HD:(rep + 1) * 2 * HD, v].rearrange("p h s -> p (h s)"),
                                     dram(scr["k"], n * (HD * row) + rep * part, [[0, 2], [row, HD], [1, row]]))\
                          .then_inc(kv_loaded[slot], 16)

            def load_v(n, slot):
                sp.dma_start(vs[slot][:], dram(scr["v"], n * (S * HP * VW),
                                               [[HP * VW, P], [P * HP * VW, NTI], [1, HP * VW]]))\
                  .then_inc(kv_loaded[slot], 16)

            def write_tables(n, c):
                for done in (tab_lo, tab_lo_pool):
                    sp.wait_ge(done, n * 8 + (NT * c + NT) // 2)
                sp.dma_start(dram(scr["tab"], c * 2 * NT * P * TR + P - 1, [[TR, P], [P * TR, 2 * NT], [1, TW]]),
                             tab[c][:].rearrange("p x t w -> p (x t) w")).then_inc(tab_written[c], 16)

            def read_windows(n, slot, c):
                if isinstance(n, int) and n == 0:
                    sp.wait_ge(zeros_written, 16)
                sp.wait_ge(tab_written[c], n * 16 + 16)
                sp.dma_start(pos[slot][:, c].rearrange("p x t w -> p (x t) w"),
                             dram(scr["tab"], c * 2 * NT * P * TR + P - 1,
                                  [[TR - 1, P], [P * TR, 2 * NT], [1, WW]])).then_inc(pos_loaded[c], 16)

            def load_mrow(n, slot, h):
                sp.wait_ge(mrow_copied, n * 2 + h + 1)
                for hh in range(HP):
                    sp.dma_start(qs[slot][R_MAX:R_MAX + 1, hh, h * CH:(h + 1) * CH],
                                 mrow[h][hh * NT:(hh + 1) * NT, :]).then_inc(mrow_loaded[h], 16)

            def body(n, j, gen, on):
                if on["nxt"]:
                    write_tables(n + 1, 2)
                if on["far"]:
                    if on["prev"]:
                        sp.wait_ge(st_ready, n * 32)
                    load_q(n + 2, (j + 2) % 3)
                if on["now"]:
                    load_mrow(n, j % 3, 1)
                if on["far"]:
                    load_k(n + 2, (j + 2) % 3)
                    if on["prev"]:
                        sp.wait_ge(av_done, n * 8)
                    load_v(n + 2, (j + 2) % 3)
                if on["nxt"]:
                    read_windows(n + 1, (j + 1) % 3, 2)
                if on["nxt"]:
                    write_tables(n + 1, 3)
                    read_windows(n + 1, (j + 1) % 3, 3)
                if on["far"]:
                    write_tables(n + 2, 0)
                if on["nxt"]:
                    load_mrow(n + 1, (j + 1) % 3, 0)
                if on["far"]:
                    read_windows(n + 2, (j + 2) % 3, 0)
                if on["far"]:
                    write_tables(n + 2, 1)
                    read_windows(n + 2, (j + 2) % 3, 1)

            turns(sp, body)

        @block.gpsimd
        def _(pool):
            def store(n, h):
                pool.wait_ge(att_done, n * 2 + h + 1)
                pool.dma_start(dram(scr["att"], n * (S * HP * HD) + h * (CH * HP * HD),
                                  [[HP * HD, P], [P * HP * HD, NT], [1, HP * HD]]), att[h][:])\
                  .then_inc(att_stored[h], 16)

            pool.memset(one[:], 1.0).then_inc(one_set, 1)
            pool.wait_ge(one_set, 1)

            def body(n, j, gen, on):
                for k in range(16):
                    p, i = table_of(n, k)
                    if i % 2 == 1 and on["far" if k >= TLAG else "nxt"]:
                        part, src = tab[i // NT][:, :, i % NT, :], tab32[(i // 2) % 2]
                        pool.wait_ge(tab_taken, p * 16 + i + 1)
                        pool.tensor_tensor(part[:, 0], src[:], one[:].to_broadcast([P, TW]), ALU.mult)\
                            .then_inc(tab_hi_pool, 1)
                        pool.wait_ge(tab_hi_pool, p * 8 + i // 2 + 1)
                        pool.tensor_tensor(part[:, 1], src[:], part[:, 0], ALU.subtract).then_inc(tab_lo_pool, 1)
                    if k == 3 and on["prev"]:
                        store(n - 1, 1)
                    if k == 11 and on["now"]:
                        store(n, 0)

            turns(pool, body)
            for h in range(2):
                pool.wait_ge(att_stored[h], 16 * npairs)

        @block.scalar
        def _(act):
            def copy_o(n, h):
                act.wait_ge(av_done, n * 8 + 4 * h + 4)
                wait_pos(act, out_ready, n * 2 + h)
                act.activation(os_[:], o_bank[:], ACT.Identity).then_inc(o_copied, 1)

            def exp(n, j, k, jj):
                act.wait_ge(st_ready, n * 32 + 2 * k + jj + 1)
                if jj == 0:
                    wait_pos(act, av_done, n * 8 + k // 2 - 1)
                act.activation(pt[k % 4][:, jj, :], st_bank[st_of(j, k, jj)][:], ACT.Exp).then_inc(exp_done, 1)

            def body(n, j, gen, on):
                for k in range(16):
                    if k == 2 and on["prev"]:
                        copy_o(n - 1, 1)
                    if k == 10 and on["now"]:
                        copy_o(n, 0)
                    if on["now"]:
                        exp(n, j, k, 0)
                    if on["far" if k >= TLAG else "nxt"]:
                        p, i = table_of(n, k)
                        act.wait_ge(tab_ready, p * 16 + i + 1)
                        if i % NT == 0:
                            wait_pos(act, tab_written[i // NT], p * 16)
                        if i % 2 == 0:
                            dst = tab[i // NT][:, 0, i % NT, :]
                        else:
                            dst = tab32[(i // 2) % 2][:]
                            wait_pos(act, tab_lo_pool, p * 8 + i // 2 - 1)
                        act.activation(dst, tab_bank[i % 2][:, 0:TW], ACT.Identity).then_inc(tab_taken, 1)
                    if on["now"]:
                        exp(n, j, k, 1)

            turns(act, body)

        @block.vector
        def _(dve):
            dve.memset(zeros[:], 0.0).then_inc(c_set, 1)
            for s in range(3):
                dve.memset(qs[s][R_ONE:R_FAR, :, :], 1.0).then_inc(c_set, 1)
            dve.wait_ge(c_loaded, 8 * 16)
            dve.tensor_scalar(w32s[0:K_TAB, :], w32[0:K_TAB, :], w32[0:K_TAB, 0:1], None, ALU.subtract)\
               .then_inc(w_shifted, 1)
            dve.wait_ge(w_shifted, 1)
            dve.tensor_copy(w_hi[0:K_TAB, :], w32s[0:K_TAB, :]).then_inc(wt_split, 1)
            dve.wait_ge(wt_split, 1)
            dve.tensor_tensor(w_lo[0:K_TAB, :], w32s[0:K_TAB, :], w_hi[0:K_TAB, :], ALU.subtract).then_inc(wt_split, 1)
            dve.tensor_copy(ident_h[:], ident[:]).then_inc(c_set, 1)
            for s in range(3):
                for v in range(2):
                    dve.tensor_copy(ks[s][R_ONE:R_MAX + 1, v, :, :].rearrange("p h s -> p (h s)"),
                                    sel[R_ONE:R_MAX + 1, v:v + 1].to_broadcast([R_MAX + 1 - R_ONE, HP * S]))\
                       .then_inc(c_set, 1)

            def negate(n, h):
                dve.wait_ge(mx_done, n * 32 + 16 * h + 16)
                dve.tensor_tensor(mtop[:], mx[h][:, 0, :], mx[h][:, 1, :], ALU.max).then_inc(mtop_done, 1)
                dve.wait_ge(mtop_done, n * 2 + h + 1)
                dve.tensor_scalar(mneg[h][:], mtop[:], -1.0, None, ALU.mult).then_inc(mneg_done, 1)

            def copy_mrow(n, h):
                dve.wait_ge(mrow_ready, n * 2 + h + 1)
                wait_pos(dve, mrow_loaded[h], n * 32)
                dve.tensor_copy(mrow[h][:], mx_bank[0][0:HP * NT, 0:P]).then_inc(mrow_copied, 1)

            def normalise(n, h):
                dve.wait_ge(out_ready, n * 2 + h + 1)
                out = o_bank[:, 0:NT * HP * (HD + 1)].rearrange("p (t h v) -> p t h v", t=NT, h=HP)
                dve.reciprocal(rden[:].unsqueeze(3), out[:, :, :, HD:HD + 1]).then_inc(rden_done, 1)
                dve.wait_ge(rden_done, n * 2 + h + 1)
                wait_pos(dve, att_stored[h], n * 16)
                dve.tensor_tensor(att[h][:].rearrange("p t (h v) -> p t h v", h=HP), out[:, :, :, 0:HD],
                                  rden[:].unsqueeze(3).to_broadcast([P, NT, HP, HD]), ALU.mult).then_inc(att_done, 1)

            def body(n, j, gen, on):
                for k in range(16):
                    if k == 0 and on["now"]:
                        negate(n, 1)
                    if k == 2 and on["now"]:
                        copy_mrow(n, 1)
                    if k == 8 and on["nxt"]:
                        negate(n + 1, 0)
                    if k == 10 and on["nxt"]:
                        copy_mrow(n + 1, 0)
                    if on["nxt"]:
                        for kh in range(2):
                            dve.wait_ge(mx_ready, (n + 1) * 32 + 2 * k + kh + 1)
                            dve.tensor_reduce(mx[k // 8][:, kh, k % 8:k % 8 + 1], mx_bank[kh][:], AX_X, ALU.max)\
                               .then_inc(mx_done, 1)
                    p, i = table_of(n, k)
                    if i % 2 == 0 and on["far" if k >= TLAG else "nxt"]:
                        part = tab[i // NT][:, :, i % NT, :]
                        dve.wait_ge(tab_taken, p * 16 + i + 1)
                        dve.tensor_tensor(part[:, 1], tab_bank[0][:, 0:TW], part[:, 0], ALU.subtract).then_inc(tab_lo, 1)
                    if k == 2 and on["prev"]:
                        normalise(n - 1, 1)
                    if k == 10 and on["now"]:
                        normalise(n, 0)

            turns(dve, body)

        @block.tensor
        def _(pe):
            pe.wait_ge(c_loaded, 8 * 16)
            pe.wait_ge(c_set, 5)
            pe.wait_ge(wt_loaded, 4 * 16)

            def scores(n, slot, k, jj):
                h, jt, hh = k // 8, 2 * ((k % 8) // 2) + jj, k % 2
                if k % 8 == 0 and jj == 0:
                    pe.wait_ge(mrow_loaded[h], n * 32 + 32)
                wait_pos(pe, exp_done, n * 32 + 2 * k + jj - 2)
                out = st_bank[st_of(slot, k, jj)]
                tiles = range(h * NT, (h + 1) * NT)
                runs = [(v, [i for i in tiles if test(i - jt)]) for v, test in
                        ((RIGHT, lambda x: x <= -2), (LEFT, lambda x: x >= -1))]
                runs = [(v, r) for v, r in runs if r]
                near = [i for i in tiles if abs(i - jt) <= 1]
                for at, (v, r) in enumerate(runs):
                    mm = pe.matmul(out[:, (r[0] - h * NT) * P:(r[-1] + 1 - h * NT) * P],
                                   ks[slot][0:K_SC, v, hh, jt * P:(jt + 1) * P],
                                   qs[slot][0:K_SC, hh, r[0] * P:(r[-1] + 1) * P],
                                   start=(at == 0), stop=True, skip_group_check=True)
                for i in near:
                    w0 = (jt - i + 1) * P
                    for x in range(2):
                        mm = pe.matmul(out[:, (i - h * NT) * P:(i + 1 - h * NT) * P],
                                       pos[slot][:, 2 * h + hh, x, i - h * NT, w0:w0 + P], ident_h[:],
                                       start=False, stop=(x == 1), skip_group_check=True)
                mm.then_inc(st_ready, 1)

            def maxima(n, slot, k, kh, gen):
                h, hh, i = k // 8, (k % 8) // NT, (k // 8) * NT + k % NT
                if k == 0 and kh == 0:
                    if isinstance(n, int) and n == 0:
                        pe.wait_ge(c_set, 5 + 6)
                    pe.wait_ge(kv_loaded[slot], (gen + 1) * 5 * 16)
                if k % NT == 0 and kh == 0:
                    pe.wait_ge(pos_loaded[k // NT], (n + 1) * 16)
                wait_pos(pe, mx_done, n * 32 + 2 * k + kh - 1)
                out = mx_bank[kh]
                j0 = kh * NT
                runs = variants(i, j0, j0 + NT)
                for at, (v, ja, jb) in enumerate(runs):
                    mm = pe.matmul(out[:, (ja - j0) * P:(jb - j0) * P], qs[slot][0:K_MAXP, hh, i * P:(i + 1) * P],
                                   ks[slot][0:K_MAXP, v, hh, ja * P:jb * P], start=(at == 0), stop=True,
                                   skip_group_check=True)
                ja, jb = max(j0, i - 1), min(j0 + NT, i + 2)
                if ja < jb:
                    mm = pe.matmul(out[:, (ja - j0) * P:(jb - j0) * P], ident_h[:],
                                   pos[slot][:, k // NT, 0, k % NT, (ja - i + 1) * P:(jb - i + 1) * P],
                                   start=False, stop=True, skip_group_check=True)
                mm.then_inc(mx_ready, 1)

            def table(n, slot, i, gen):
                h, hh, t = i // 8, (i % 8) // NT, (i // 8) * NT + i % NT
                if i == 0:
                    pe.wait_ge(q_loaded[slot], (gen + 1) * 3 * 16)
                if i % 2 == 0:
                    wait_pos(pe, tab_lo, n * 8 + i // 2)
                else:
                    wait_pos(pe, tab_taken, n * 16 + i - 1)
                pe.matmul(tab_bank[i % 2][:, 0:TW], qs[slot][0:K_TAB, hh, t * P:(t + 1) * P], wt[0:K_TAB, :],
                          start=True, stop=True).then_inc(tab_ready, 1)

            def turn_maxima(n, h, done):
                pe.wait_ge(mneg_done, n * 2 + h + 1)
                if done is not None:
                    pe.wait_ge(mx_done, done)
                pe.matmul(mx_bank[0][0:HP * NT, 0:P], mneg[h][:], ident_h[:], start=True, stop=True).then_inc(mrow_ready, 1)

            def values(n, slot, g, gen):
                h, jp = g // 4, g % 4
                if jp == 0:
                    wait_pos(pe, att_done, n * 2 + h)
                pe.wait_ge(exp_done, n * 32 + 4 * g + 4)
                for hh in range(HP):
                    for jj in range(2):
                        r0 = (2 * hh + jj) * VW
                        mm = pe.matmul(o_bank[r0:r0 + VW, :], vs[slot][:, 2 * jp + jj, hh * VW:(hh + 1) * VW],
                                       pt[(2 * g + hh) % 4][:, jj, :], start=(jp == 0), stop=(jp == 3),
                                       skip_group_check=True)
                mm.then_inc(av_done, 1)

            def outputs(n, h):
                pe.wait_ge(o_copied, n * 2 + h + 1)
                w = HP * (HD + 1)
                for t in range(NT):
                    mm = pe.matmul(o_bank[:, t * w:(t + 1) * w], os_[:, t * P:(t + 1) * P], pick[:],
                                   start=True, stop=True)
                mm.then_inc(out_ready, 1)

            def body(n, j, gen, on):
                for k in range(16):
                    if k == 2 and on["now"]:
                        turn_maxima(n, 1, (n + 1) * 32 + 3 if on["nxt"] else None)
                    if k == 10 and on["nxt"]:
                        turn_maxima(n + 1, 0, (n + 1) * 32 + 19)
                    if on["now"]:
                        scores(n, j % 3, k, 0)
                    if on["nxt"]:
                        if k == 2 and on["now"]:
                            pe.wait_ge(mrow_copied, n * 2 + 2)
                        if k == 10:
                            pe.wait_ge(mrow_copied, n * 2 + 3)
                        maxima(n + 1, (j + 1) % 3, k, 0, gen(1))
                    if on["far" if k >= TLAG else "nxt"]:
                        p, i = table_of(n, k)
                        ahead = 2 if k >= TLAG else 1
                        table(p, (j + ahead) % 3, i, gen(ahead))
                    if on["now"]:
                        scores(n, j % 3, k, 1)
                    if on["nxt"]:
                        maxima(n + 1, (j + 1) % 3, k, 1, gen(1))
                    if k == 2 and on["prev"]:
                        outputs(n - 1, 1)
                    if k == 10 and on["now"]:
                        outputs(n, 0)
                    if k == 1 and on["prev"]:
                        values(n - 1, (j - 1) % 3, 7, gen(-1))
                    if k % 2 == 1 and k > 1 and on["now"]:
                        values(n, j % 3, (k - 3) // 2, gen(0))

            turns(pe, body)


def finish(nc, a, scr, nb):
    with ExitStack() as ctx:
        m = Pool(nc, ctx)
        bank = [m.ps(f"fi_bank{i}", [P, CH]) for i in range(8)]
        w_names = ["ffn_wr", "ffn_wk", "ffn_wv"]
        w32 = {n: m.sb(f"fi_{n}_32", [P, NF, D]) for n in w_names}
        w = {n: m.sb(f"fi_{n}", [P, 2, NF, D], F16) for n in w_names}
        v = {n: m.sb(f"fi_{n}", [P, NF]) for n in ("mu_r", "mu_k")}
        ident = m.sb("fi_ident", [P, P])
        eps = m.sb("fi_eps", [P, NT])
        minus_half = m.sb("fi_minus_half", [P, NT])
        xl = [m.sb(f"fi_xl{c}", [P, NT, D]) for c in range(2)]
        at = [m.sb(f"fi_at{c}", [P, NT, D]) for c in range(2)]
        xb = [m.sb(f"fi_xb{i}", [P, NT, D]) for i in range(4)]
        ffn = Ffn(m, "f2", bank[6:8], bank[0:4], bank[4:6], {"wr": w["ffn_wr"], "wk": w["ffn_wk"], "wv": w["ffn_wv"], **v})
        w_loaded, consts_set, x3_done = m.sems("f2_w_loaded f2_consts_set x3_done")
        w_copied, w_split = m.sems("f2_w_copied f2_w_split")
        x_loaded = m.sems("x2_loaded0 x2_loaded1")
        out_stored = m.sems(" ".join(f"out_stored{i}" for i in range(4)))
        loads = [(w32[n], rows(a[n])) for n in w_names] + [(v[n], a[n]) for n in v] + [(ident, a["ident"])]
        w_all = 16 * len(loads)
        nu = nb * NC

        def rounds(eng, body):
            def at(u):
                body(u, u // 2, u % 2, u % 4, lambda d: (u + d) // 4, nu - 1 - u)

            for u in range(min(4, nu - 4)):
                at(u)
            if nb > 4:
                with eng.Fori(1, nb // 2 - 1) as it:
                    for k in range(4):
                        body(it * 4 + k, it * 2 + k // 2, k % 2, k, lambda d, k=k: it + (k + d) // 4, 4)
            for u in range(nu - 4, nu):
                at(u)

        block = ctx.enter_context(nc.Block())

        @block.sync
        def _(sp):
            for dst, src in loads:
                sp.dma_start(dst[:], src).then_inc(w_loaded, 16)

            def load_x(b, c):
                tok = slice(c * CH, (c + 1) * CH)
                sp.dma_start(xl[c][:], scr["x2"][b, tok, :].rearrange("(t p) d -> p t d", p=P))\
                  .then_inc(x_loaded[c], 16)
                for t in range(NT):
                    r = c * CH + t * P
                    sp.dma_start(at[c][:, t, :].rearrange("p (r v) -> p r v", r=NPR),
                                 scr["att"][b, :, r:r + P, :].rearrange("r p v -> p r v")).then_inc(x_loaded[c], 16)

            load_x(0, 0)
            load_x(0, 1)
            for u in range(2, 4):
                sp.wait_ge(x3_done, u - 1)
                load_x(1, u - 2)

            def body(u, b, c, s, gen, nxt):
                if nxt >= 4:
                    sp.wait_ge(x3_done, u + 3)
                    load_x(b + 2, c)
                sp.wait_ge(ffn.x_done, u + 1)
                sp.dma_start(a["out"][b, c * CH:(c + 1) * CH, :].rearrange("(t p) d -> p t d", p=P), xb[s][:])\
                  .then_inc(out_stored[s], 16)

            rounds(sp, body)
            for sem in out_stored:
                sp.wait_ge(sem, 16 * (nu // 4))

        @block.gpsimd
        def _(pool):
            pool.memset(minus_half[:], -0.5).then_inc(consts_set, 1)
            pool.memset(eps[:], EPS).then_inc(consts_set, 1)
            pool.wait_ge(consts_set, 2)
            ffn.ln.pool_rstd(pool, 0, 0, eps, minus_half)
            ffn.ln.pool_rstd(pool, 1, 1, eps, minus_half)

            ffn.pool_low(pool, 0, 0)
            ffn.pool_low(pool, 0, 1)

            def body(u, b, c, s, gen, nxt):
                ffn.pool_square(pool, u)
                if nxt >= 2:
                    ffn.ln.pool_rstd(pool, u + 2, c, eps, minus_half)
                ffn.pool_low(pool, u, 2)
                if nxt >= 1:
                    ffn.pool_low(pool, u + 1, 0)
                    ffn.pool_low(pool, u + 1, 1)

            rounds(pool, body)

        @block.scalar
        def _(act):
            act.wait_ge(w_loaded, w_all)
            weights_high(act, w32, w, w_copied)

            ffn.act_input(act, 0, 0)
            ffn.act_high(act, 0, 0)
            ffn.act_high(act, 0, 1)

            def body(u, b, c, s, gen, nxt):
                ffn.act_k(act, u)
                if nxt >= 1:
                    ffn.act_input(act, u + 1, 1 - c)
                ffn.act_high(act, u, 2)
                wait_pos(act, ffn.rv_done, u * 2)
                ffn.act_r(act, u)
                if nxt >= 1:
                    ffn.act_high(act, u + 1, 0)
                    ffn.act_high(act, u + 1, 1)

            rounds(act, body)

        @block.vector
        def _(dve):
            dve.wait_ge(w_loaded, w_all)
            ffn.dve_init(dve)
            weights_low(dve, w32, w, w_copied, w_split)

            def x3_of(u, b, c, s, gen):
                dve.wait_ge(x_loaded[c], b * 80 + 80)
                wait_pos(dve, out_stored[s], gen * 16)
                dve.tensor_tensor(xb[s][:], xl[c][:], at[c][:], ALU.add).then_inc(x3_done, 1)
                dve.wait_ge(x3_done, u + 1)
                ffn.ln.dve_stats(dve, u, c, xb[s])

            x3_of(0, 0, 0, 0, 0)
            x3_of(1, 0, 1, 1, 0)
            ffn.ln.dve_apply(dve, 0, 0, xb[0])

            ffn.dve_mix(dve, 0, 0, 0)
            ffn.ln.dve_apply(dve, 1, 1, xb[1])

            def body(u, b, c, s, gen, nxt):
                if nxt >= 2:
                    x3_of(u + 2, b + 1, c, (s + 2) % 4, gen(2))
                if nxt >= 1:
                    ffn.dve_mix(dve, u + 1, b + c, 1 - c)
                if nxt >= 2:
                    ffn.ln.dve_apply(dve, u + 2, c, xb[(s + 2) % 4])
                ffn.dve_out(dve, u, xb[s])

            rounds(dve, body)

        @block.tensor
        def _(pe):
            pe.wait_ge(w_loaded, w_all)
            pe.wait_ge(w_split, len(w))

            ffn.ln.pe_transpose(pe, 0, 0, bank[6:8], ident, lambda f: None)

            def body(u, b, c, s, gen, nxt):
                def before(done):
                    return lambda i: wait_pos(pe, done, u * 2 - 1 + i) if not isinstance(u, int) or u > 0 else None

                ffn.pe_k(pe, u, before(ffn.k_done))
                if nxt >= 1:
                    ffn.ln.pe_transpose(pe, u + 1, 1 - c, bank[6:8], ident,
                                        lambda f: pe.wait_ge(ffn.ln.tr_copied, u * NF + f + 1))
                ffn.pe_r(pe, u, before(ffn.r_done))
                ffn.pe_v(pe, u, before(ffn.rv_done))

            rounds(pe, body)


def hybrid_kernel(nc, a, out):
    nb = a["x"].shape[0]
    a = dict(a, out=out)

    def scratch(name, shape, dt=F32):
        return nc.dram_tensor(name, shape, dt).ap()

    scr = {
        "x2": scratch("scr_x2", [nb, S, D]),
        "q": scratch("scr_q", [2, nb, D, S], F16),
        "k": scratch("scr_k", [2, nb, D, S], F16),
        "far": scratch("scr_far", [2, 2, nb, HEADS, S], F16),
        "v": scratch("scr_v", [nb, NPR, S, HP * VW]),
        "tab": scratch("scr_tab", [NQ, 2, NT * P, TR], F16),
        "att": scratch("scr_att", [nb, NPR, S, HP * HD]),
    }
    project(nc, a, scr, nb)
    attend(nc, a, scr, nb)
    finish(nc, a, scr, nb)


def _layout(x, W_in, b_in, W_gx, b_gx, W_ga, b_ga, a_param, W_out, b_out, Wqkv, bqkv, Wr, br, W_r, W_k, W_v, mu_r, mu_k):
    w = Wqkv.reshape(HEADS, 3, HD, D)
    bb = bqkv.reshape(HEADS, 3, HD)
    at = np.clip(np.arange(TW), 0, R - 1)
    far = np.zeros((D, 32), np.float32)
    for h in range(HEADS):
        rows = (h // HP) * HP * HD + np.arange(HD) * HP + h % HP
        far[rows, h] = Wr[0]
        far[rows, HEADS + h] = Wr[R - 1]
    sel = np.zeros((R_MAX + 1 - R_ONE, 2), np.float32)
    sel[R_MAX - R_ONE, :] = 1.0
    for x2 in (0, 2):
        sel[R_FAR - R_ONE + x2, LEFT] = 1.0
        sel[R_FAR - R_ONE + x2 + 1, RIGHT] = 1.0
    pick = np.zeros((P, HP * (HD + 1)), np.float32)
    for hh in range(HP):
        for jj in range(2):
            for r in range(HD + 1):
                pick[(2 * hh + jj) * VW + r, hh * (HD + 1) + r] = 1.0

    def cols(v):
        return v.reshape(NF, P).T

    def mixed(v):
        return v.reshape((NPR, HP, HD) + v.shape[2:]).swapaxes(1, 2).reshape((D,) + v.shape[2:])

    return {
        "x": x, "W_in": W_in, "b_in": cols(b_in), "W_gx": W_gx, "b_gx": cols(b_gx), "W_ga": W_ga, "b_ga": cols(b_ga),
        "a_param": cols(a_param), "W_out": W_out, "b_out": b_out,
        "Wq": mixed(w[:, 0]).T, "Wk": mixed(w[:, 1]).T, "Wv": w[:, 2].reshape(D, D).T,
        "bq": cols(mixed(bb[:, 0])), "bk": cols(mixed(bb[:, 1])), "bv": bb[:, 2].reshape(D),
        "wr_pad": Wr.T[:, at], "br_pad": br[at], "far": far,
        "bfar": np.repeat(br[[0, R - 1]], HEADS).reshape(2 * HEADS, 1),
        "sel": sel, "pick": pick, "ident": np.eye(P, dtype=np.float32),
        "ffn_wr": W_r.T, "ffn_wk": W_k.T, "ffn_wv": W_v.T, "mu_r": cols(mu_r), "mu_k": cols(mu_k),
    }


_ORDER = ["L0_attn_a_x", "L0_attn_a_W_in", "L0_attn_a_b_in", "L0_attn_a_W_gx", "L0_attn_a_b_gx", "L0_attn_a_W_ga",
          "L0_attn_a_b_ga", "L0_attn_a_a_param", "L0_attn_a_W_out", "L0_attn_a_b_out", "L0_attn_b_Wqkv",
          "L0_attn_b_bqkv", "L0_attn_b_Wr", "L0_attn_b_br", "L0_ffn_W_r", "L0_ffn_W_k", "L0_ffn_W_v",
          "L0_ffn_mu_r", "L0_ffn_mu_k"]


def kernel(**inputs):
    import concourse.bacc as _bacc
    from concourse.bass_utils import run_bass_kernel_spmd as _run

    nc = _bacc.Bacc("TRN2", target_bir_lowering=False, num_devices=1)
    arrays = {f"in_{k}": np.ascontiguousarray(v)
              for k, v in _layout(*[np.asarray(inputs[n]) for n in _ORDER]).items()}
    args = {k[3:]: nc.dram_tensor(k, v.shape, mybir.dt.from_np(v.dtype), kind="ExternalInput").ap()
            for k, v in arrays.items()}
    shape = arrays["in_x"].shape
    out = nc.dram_tensor("out", shape, F32, kind="ExternalOutput").ap()
    hybrid_kernel(nc, args, out)
    r = _run(nc, [arrays], core_ids=[0])
    return r.results[0]["out"]
```
